# Optimizing a Trainium2 kernel written in Bass

```python
import numpy as np
import jax
import jax.numpy as jnp

def _softmax(x, axis=-1):
    return jax.nn.softmax(x, axis=axis)

def _gelu(x):
    return jax.nn.gelu(x, approximate=True)

def _silu(x):
    return jax.nn.silu(x)

def _sigmoid(x):
    return jax.nn.sigmoid(x)

def _layernorm(x, axis=-1, eps=1e-05):
    m = jnp.mean(x, axis=axis, keepdims=True)
    v = jnp.var(x, axis=axis, keepdims=True)
    return (x - m) / jnp.sqrt(v + eps)

def _scatter_add(tgt, idx, src, axis=0):
    return tgt.at[idx].add(src)

def _segment_sum(src, seg, n):
    return jax.ops.segment_sum(src, seg, n)
kernel_name = 'mk_decoder_postln_d1_seqx_r8_283348'

def setup_inputs(seed: int=0):
    np.random.seed(seed)
    _w = jnp.asarray

    def _rec_inputs():
        import jax
        import jax.numpy as jnp
        _rk = jax.random.key(seed)
        x = 7.22e-05 + 1 * jax.random.normal(jax.random.fold_in(_rk, 1), (4, 256, 128), jnp.float32)
        _lenS = 256 - jax.random.randint(jax.random.fold_in(_rk, 7), (4,), 0, max(1, 256 // 4) + 1, jnp.int32)
        _lenS2 = 256 - jax.random.randint(jax.random.fold_in(_rk, 8), (4,), 0, max(1, 256 // 4) + 1, jnp.int32)
        _ctx_768P = jax.random.normal(jax.random.fold_in(_rk, 11), (4, 16, 96), jnp.float32)
        _ctx_768c = jax.random.dirichlet(jax.random.fold_in(_rk, 511), 0.3 * jnp.ones((16,), jnp.float32), (4, 256))
        _ctx_768t = jnp.einsum('bsk,bkd->bsd', _ctx_768c, _ctx_768P)
        _ctx_768t = _ctx_768t * jax.lax.rsqrt(jnp.mean(jnp.square(_ctx_768t)) + 1e-12) * 0.953939
        ctx_768 = -0.000191848 + 0.999787 * (_ctx_768t + 0.3 * jax.random.normal(jax.random.fold_in(_rk, 611), (4, 256, 96), jnp.float32))
        return (x, ctx_768)
    x, ctx_768 = _rec_inputs()

    def _L0_attn_setup():
        import jax, jax.numpy as jnp
        import numpy as np
        D = 128
        key = jax.random.key(seed)
        ks = jax.random.split(key, 9)
        s = 1.0 / np.sqrt(D)
        x = jax.random.normal(ks[0], (512, 8, D), dtype=jnp.float32)
        Wq = jax.random.uniform(ks[1], (D, D), jnp.float32, -s, s)
        bq = jax.random.uniform(ks[2], (D,), jnp.float32, -s, s)
        Wk = jax.random.uniform(ks[3], (D, D), jnp.float32, -s, s)
        bk = jax.random.uniform(ks[4], (D,), jnp.float32, -s, s)
        Wv = jax.random.uniform(ks[5], (D, D), jnp.float32, -s, s)
        bv = jax.random.uniform(ks[6], (D,), jnp.float32, -s, s)
        Wo = jax.random.uniform(ks[7], (D, D), jnp.float32, -s, s)
        bo = jax.random.uniform(ks[8], (D,), jnp.float32, -s, s)
        return {'x': x, 'Wq': Wq, 'bq': bq, 'Wk': Wk, 'bk': bk, 'Wv': Wv, 'bv': bv, 'Wo': Wo, 'bo': bo}
    _L0_attn_all = _L0_attn_setup()
    _L0_attn_in = {k: v for k, v in _L0_attn_all.items() if k in ('Wq', 'bq', 'Wk', 'bk', 'Wv', 'bv', 'Wo', 'bo')}
    del _L0_attn_all

    def _L0_xattn_setup():
        import jax, jax.numpy as jnp
        import numpy as np
        B, LQ, LK = (4, 256, 256)
        D1, D2, H = (128, 96, 128)
        key = jax.random.key(seed)
        ks = jax.random.split(key, 9)
        s1, s2, sh = (1.0 / np.sqrt(D1), 1.0 / np.sqrt(D2), 1.0 / np.sqrt(H))
        return {'query': jax.random.normal(ks[0], (B, LQ, D1), jnp.float32), 'key': jax.random.normal(ks[1], (B, LK, D2), jnp.float32), 'value': jax.random.normal(ks[2], (B, LK, D2), jnp.float32), 'Wq': jax.random.normal(ks[3], (D1, H), jnp.float32) * s1, 'bq': jax.random.normal(ks[4], (H,), jnp.float32) * s1, 'Wk': jax.random.normal(ks[5], (D2, H), jnp.float32) * s2, 'bk': jax.random.normal(ks[6], (H,), jnp.float32) * s2, 'Wv': jax.random.normal(ks[7], (D2, H), jnp.float32) * s2, 'bv': jax.random.normal(ks[8], (H,), jnp.float32) * s2}
    _L0_xattn_all = _L0_xattn_setup()
    _L0_xattn_in = {k: v for k, v in _L0_xattn_all.items() if k in ('Wq', 'bq', 'Wk', 'bk', 'Wv', 'bv')}
    del _L0_xattn_all

    def _L0_ffn_setup():
        import jax, jax.numpy as jnp
        import numpy as np
        DIM = 128
        DEPTH = 6
        HEADS = 16
        DIM_HEAD = 64
        WINDOW = 32
        INNER = HEADS * DIM_HEAD
        DIM_INNER = int(DIM * 4 * 2 / 3)
        QK_SCALE = 8.0

        def shift_tokens(t):
            a, s = jnp.split(t, 2, -1)
            s = jnp.pad(s, ((0, 0), (1, 0), (0, 0)))[:, :-1]
            return jnp.concatenate([a, s], -1)

        def l2norm(t):
            return t / jnp.maximum(jnp.linalg.norm(t, axis=-1, keepdims=True), 1e-12)

        def rotate_half(x):
            x1, x2 = jnp.split(x, 2, -1)
            return jnp.concatenate([-x2, x1], -1)

        def rotary_tables(n):
            half = jnp.arange(0, DIM_HEAD, 2, dtype=jnp.float32)
            inv_freq = 1.0 / 10000.0 ** (half / DIM_HEAD)
            t = jnp.arange(n, dtype=jnp.float32)
            freqs = t[:, None] * inv_freq[None, :]
            freqs = jnp.concatenate([freqs, freqs], -1)
            base_scale = (half + 0.4 * DIM_HEAD) / (1.4 * DIM_HEAD)
            power = (t - n // 2) / (WINDOW // 2)
            scale = base_scale[None, :] ** power[:, None]
            scale = jnp.concatenate([scale, scale], -1)
            return (freqs, scale)

        def local_attention(q, k, v):
            b, h, n, d = q.shape
            w = WINDOW
            nw = n // w
            bq = q.reshape(b, h, nw, w, d)
            bk = k.reshape(b, h, nw, w, d)
            bv = v.reshape(b, h, nw, w, d)

            def look(t):
                p = jnp.pad(t, ((0, 0), (0, 0), (1, 0), (0, 0), (0, 0)))
                return jnp.concatenate([p[:, :, :nw], p[:, :, 1:]], axis=3)
            bk2, bv2 = (look(bk), look(bv))
            seq = jnp.arange(n).reshape(nw, w)
            seq_p = jnp.pad(seq, ((1, 0), (0, 0)), constant_values=-1)
            jt = jnp.concatenate([seq_p[:nw], seq_p[1:]], axis=1)
            it = seq[:, :, None]
            jb = jt[:, None, :]
            mask = (it < jb) | (it > jb + w) | (jb == -1)
            sim = jnp.einsum('bhwie,bhwje->bhwij', bq, bk2) * QK_SCALE
            sim = jnp.where(mask, -jnp.finfo(sim.dtype).max, sim)
            attn = jax.nn.softmax(sim, -1)
            out = jnp.einsum('bhwij,bhwje->bhwie', attn, bv2)
            return out.reshape(b, h, n, d)

        def attn_layer(x, Wqkv, qs, ksc, Wo):
            b, n, _ = x.shape
            qkv = x @ Wqkv
            q, k, v = jnp.split(qkv, 3, -1)
            sh = lambda t: t.reshape(b, n, HEADS, DIM_HEAD).transpose(0, 2, 1, 3)
            q, k, v = (sh(q), sh(k), sh(v))
            q = l2norm(q) * qs
            k = l2norm(k) * ksc
            freqs, scale = rotary_tables(n)
            cos, sin = (jnp.cos(freqs), jnp.sin(freqs))
            q = q * cos * scale + rotate_half(q) * sin * scale
            inv = 1.0 / scale
            k = k * cos * inv + rotate_half(k) * sin * inv
            out = local_attention(q, k, v)
            out = out.transpose(0, 2, 1, 3).reshape(b, n, INNER)
            return out @ Wo

        def ffn_layer(x, g, bln, W1, b1, W2, b2):
            mu = x.mean(-1, keepdims=True)
            var = ((x - mu) ** 2).mean(-1, keepdims=True)
            xn = (x - mu) / jnp.sqrt(var + 1e-05) * g + bln
            hg = xn @ W1 + b1
            a, gate = jnp.split(hg, 2, -1)
            return a * jax.nn.gelu(gate, approximate=False) @ W2 + b2
        key = jax.random.key(seed)
        ks = jax.random.split(key, 8)
        B, N = (2, 256)
        init = lambda k, shape: jax.random.normal(k, shape, jnp.float32) * 0.02
        return {'x': jax.random.normal(ks[0], (B, N, DIM), jnp.float32), 'Wqkv': init(ks[1], (DEPTH, DIM, 3 * INNER)), 'q_scale': jnp.ones((DEPTH, DIM_HEAD), jnp.float32), 'k_scale': jnp.ones((DEPTH, DIM_HEAD), jnp.float32), 'Wo': init(ks[2], (DEPTH, INNER, DIM)), 'ln_g': jnp.ones((DEPTH, DIM), jnp.float32), 'ln_b': jnp.zeros((DEPTH, DIM), jnp.float32), 'W1': init(ks[3], (DEPTH, DIM, 2 * DIM_INNER)), 'b1': jnp.zeros((DEPTH, 2 * DIM_INNER), jnp.float32), 'W2': init(ks[4], (DEPTH, DIM_INNER, DIM)), 'b2': jnp.zeros((DEPTH, DIM), jnp.float32)}
    _L0_ffn_all = _L0_ffn_setup()
    _L0_ffn_in = {k: v for k, v in _L0_ffn_all.items() if k in ('Wqkv', 'q_scale', 'k_scale', 'Wo', 'ln_g', 'ln_b', 'W1', 'b1', 'W2', 'b2')}
    del _L0_ffn_all
    return {'x': x, 'ctx_768': ctx_768, 'L0_attn_Wq': _L0_attn_in['Wq'], 'L0_attn_bq': _L0_attn_in['bq'], 'L0_attn_Wk': _L0_attn_in['Wk'], 'L0_attn_bk': _L0_attn_in['bk'], 'L0_attn_Wv': _L0_attn_in['Wv'], 'L0_attn_bv': _L0_attn_in['bv'], 'L0_attn_Wo': _L0_attn_in['Wo'], 'L0_attn_bo': _L0_attn_in['bo'], 'L0_xattn_Wq': _L0_xattn_in['Wq'], 'L0_xattn_bq': _L0_xattn_in['bq'], 'L0_xattn_Wk': _L0_xattn_in['Wk'], 'L0_xattn_bk': _L0_xattn_in['bk'], 'L0_xattn_Wv': _L0_xattn_in['Wv'], 'L0_xattn_bv': _L0_xattn_in['bv'], 'L0_ffn_Wqkv': _L0_ffn_in['Wqkv'], 'L0_ffn_q_scale': _L0_ffn_in['q_scale'], 'L0_ffn_k_scale': _L0_ffn_in['k_scale'], 'L0_ffn_Wo': _L0_ffn_in['Wo'], 'L0_ffn_ln_g': _L0_ffn_in['ln_g'], 'L0_ffn_ln_b': _L0_ffn_in['ln_b'], 'L0_ffn_W1': _L0_ffn_in['W1'], 'L0_ffn_b1': _L0_ffn_in['b1'], 'L0_ffn_W2': _L0_ffn_in['W2'], 'L0_ffn_b2': _L0_ffn_in['b2']}

def reference(x, ctx_768, L0_attn_Wq, L0_attn_bq, L0_attn_Wk, L0_attn_bk, L0_attn_Wv, L0_attn_bv, L0_attn_Wo, L0_attn_bo, L0_xattn_Wq, L0_xattn_bq, L0_xattn_Wk, L0_xattn_bk, L0_xattn_Wv, L0_xattn_bv, L0_ffn_Wqkv, L0_ffn_q_scale, L0_ffn_k_scale, L0_ffn_Wo, L0_ffn_ln_g, L0_ffn_ln_b, L0_ffn_W1, L0_ffn_b1, L0_ffn_W2, L0_ffn_b2):
    import jax
    import jax.numpy as jnp

    def _L0_attn_ref(x, Wq, bq, Wk, bk, Wv, bv, Wo, bo):
        import jax, jax.numpy as jnp
        import numpy as np
        D = 128
        Q = jax.nn.elu(x @ Wq.T + bq) + 1.0
        K = jax.nn.elu(x @ Wk.T + bk) + 1.0
        V = x @ Wv.T + bv
        KV = jnp.einsum('sbd,sbe->bde', K, V)
        out = jnp.einsum('sbd,bde->sbe', Q, KV)
        return out @ Wo.T + bo

    def _L0_xattn_ref(query, key, value, Wq, bq, Wk, bk, Wv, bv):
        import jax, jax.numpy as jnp
        import numpy as np
        B, LQ, LK = (4, 256, 256)
        D1, D2, H = (128, 96, 128)
        q = jnp.einsum('bqd,dh->bqh', query, Wq) + bq
        k = jnp.einsum('bkd,dh->bkh', key, Wk) + bk
        v = jnp.einsum('bkd,dh->bkh', value, Wv) + bv
        scores = jnp.einsum('bqh,bkh->bqk', q, k)
        weights = jax.nn.softmax(scores, axis=-1)
        return jnp.einsum('bqk,bkh->bqh', weights, v)

    def _L0_ffn_ref(x, Wqkv, q_scale, k_scale, Wo, ln_g, ln_b, W1, b1, W2, b2):
        import jax, jax.numpy as jnp
        import numpy as np
        DIM = 128
        DEPTH = 6
        HEADS = 16
        DIM_HEAD = 64
        WINDOW = 32
        INNER = HEADS * DIM_HEAD
        DIM_INNER = int(DIM * 4 * 2 / 3)
        QK_SCALE = 8.0

        def shift_tokens(t):
            a, s = jnp.split(t, 2, -1)
            s = jnp.pad(s, ((0, 0), (1, 0), (0, 0)))[:, :-1]
            return jnp.concatenate([a, s], -1)

        def l2norm(t):
            return t / jnp.maximum(jnp.linalg.norm(t, axis=-1, keepdims=True), 1e-12)

        def rotate_half(x):
            x1, x2 = jnp.split(x, 2, -1)
            return jnp.concatenate([-x2, x1], -1)

        def rotary_tables(n):
            half = jnp.arange(0, DIM_HEAD, 2, dtype=jnp.float32)
            inv_freq = 1.0 / 10000.0 ** (half / DIM_HEAD)
            t = jnp.arange(n, dtype=jnp.float32)
            freqs = t[:, None] * inv_freq[None, :]
            freqs = jnp.concatenate([freqs, freqs], -1)
            base_scale = (half + 0.4 * DIM_HEAD) / (1.4 * DIM_HEAD)
            power = (t - n // 2) / (WINDOW // 2)
            scale = base_scale[None, :] ** power[:, None]
            scale = jnp.concatenate([scale, scale], -1)
            return (freqs, scale)

        def local_attention(q, k, v):
            b, h, n, d = q.shape
            w = WINDOW
            nw = n // w
            bq = q.reshape(b, h, nw, w, d)
            bk = k.reshape(b, h, nw, w, d)
            bv = v.reshape(b, h, nw, w, d)

            def look(t):
                p = jnp.pad(t, ((0, 0), (0, 0), (1, 0), (0, 0), (0, 0)))
                return jnp.concatenate([p[:, :, :nw], p[:, :, 1:]], axis=3)
            bk2, bv2 = (look(bk), look(bv))
            seq = jnp.arange(n).reshape(nw, w)
            seq_p = jnp.pad(seq, ((1, 0), (0, 0)), constant_values=-1)
            jt = jnp.concatenate([seq_p[:nw], seq_p[1:]], axis=1)
            it = seq[:, :, None]
            jb = jt[:, None, :]
            mask = (it < jb) | (it > jb + w) | (jb == -1)
            sim = jnp.einsum('bhwie,bhwje->bhwij', bq, bk2) * QK_SCALE
            sim = jnp.where(mask, -jnp.finfo(sim.dtype).max, sim)
            attn = jax.nn.softmax(sim, -1)
            out = jnp.einsum('bhwij,bhwje->bhwie', attn, bv2)
            return out.reshape(b, h, n, d)

        def attn_layer(x, Wqkv, qs, ksc, Wo):
            b, n, _ = x.shape
            qkv = x @ Wqkv
            q, k, v = jnp.split(qkv, 3, -1)
            sh = lambda t: t.reshape(b, n, HEADS, DIM_HEAD).transpose(0, 2, 1, 3)
            q, k, v = (sh(q), sh(k), sh(v))
            q = l2norm(q) * qs
            k = l2norm(k) * ksc
            freqs, scale = rotary_tables(n)
            cos, sin = (jnp.cos(freqs), jnp.sin(freqs))
            q = q * cos * scale + rotate_half(q) * sin * scale
            inv = 1.0 / scale
            k = k * cos * inv + rotate_half(k) * sin * inv
            out = local_attention(q, k, v)
            out = out.transpose(0, 2, 1, 3).reshape(b, n, INNER)
            return out @ Wo

        def ffn_layer(x, g, bln, W1, b1, W2, b2):
            mu = x.mean(-1, keepdims=True)
            var = ((x - mu) ** 2).mean(-1, keepdims=True)
            xn = (x - mu) / jnp.sqrt(var + 1e-05) * g + bln
            hg = xn @ W1 + b1
            a, gate = jnp.split(hg, 2, -1)
            return a * jax.nn.gelu(gate, approximate=False) @ W2 + b2
        for i in range(DEPTH):
            x = attn_layer(shift_tokens(x), Wqkv[i], q_scale[i], k_scale[i], Wo[i]) + x
            x = ffn_layer(shift_tokens(x), ln_g[i], ln_b[i], W1[i], b1[i], W2[i], b2[i]) + x
        return x
    x = _layernorm(x + _L0_attn_ref(x, L0_attn_Wq, L0_attn_bq, L0_attn_Wk, L0_attn_bk, L0_attn_Wv, L0_attn_bv, L0_attn_Wo, L0_attn_bo), axis=-1)
    x = _layernorm(x + _L0_xattn_ref(x, ctx_768, ctx_768, L0_xattn_Wq, L0_xattn_bq, L0_xattn_Wk, L0_xattn_bk, L0_xattn_Wv, L0_xattn_bv), axis=-1)
    x = _layernorm(x + _L0_ffn_ref(x, L0_ffn_Wqkv, L0_ffn_q_scale, L0_ffn_k_scale, L0_ffn_Wo, L0_ffn_ln_g, L0_ffn_ln_b, L0_ffn_W1, L0_ffn_b1, L0_ffn_W2, L0_ffn_b2), axis=-1)
    return x

_drawn_inputs = setup_inputs


def setup_inputs(seed=0):
    import zlib

    import numpy as np

    out = dict(_drawn_inputs(seed))
    spreads = {'L0_ffn_q_scale': (1.0, 0.6),
     'L0_ffn_k_scale': (1.0, 0.6),
     'L0_ffn_ln_g': (1.0, 0.6),
     'L0_ffn_ln_b': (0.0, 0.8),
     'L0_ffn_b1': (0.0, 0.8),
     'L0_ffn_b2': (0.0, 0.1)}
    factors = {'L0_attn_bq': 23.038,
     'L0_attn_bk': 28.354,
     'L0_attn_bo': 51.598,
     'L0_xattn_bk': 200.0,
     'L0_ffn_W1': 3.651,
     'L0_ffn_W2': 3.623}
    for name, (base, spread) in spreads.items():
        noise = np.random.default_rng([zlib.crc32(name.encode()), seed]).standard_normal(out[name].shape)
        drawn = base * np.exp(spread * noise) if base else spread * noise
        out[name] = jnp.asarray(drawn.astype(out[name].dtype))
    for name, factor in factors.items():
        out[name] = (out[name] * factor).astype(out[name].dtype)
    return out
```

```python
import numpy as np
import concourse.bass as bass
from concourse import mybir
from contextlib import ExitStack

F32 = mybir.dt.float32
BF16 = mybir.dt.bfloat16
ALU = mybir.AluOpType
ACT = mybir.ActivationFunctionType
AX = mybir.AxisListType

P = 128
B, N, D = 4, 256, 128
T = B * N
DC = 96
DEPTH, HEADS, DH, WIN = 6, 16, 64, 32
INNER = HEADS * DH
QKV = 3 * INNER
FF = int(D * 4 * 2 / 3)
FCH = [128, 128, FF - 256]
NT = N // P
CH = 512
HC = CH // DH
SPAN = P + WIN
STW = SPAN + P
GROUPS = [(0, 6), (6, 11), (11, 16)]
VW = DH + 1
NCOL = 9
EPS = 1e-5
BIG = -1.0e30


def build(nc, a, out):
    ctx = ExitStack()
    with ctx:
        ctx.enter_context(nc.allow_low_precision(reason="shift of the softmax is rounded to bf16, and used alike in numerator and sum"))

        def sb(name, shape, dt=F32):
            return ctx.enter_context(nc.sbuf_tensor(name, shape, dt))

        def sem(name):
            return ctx.enter_context(nc.semaphore(name))

        wqkv = sb("wqkv", [P, QKV])
        wo = sb("wo", [P, 8, D])
        w1 = sb("w1", [P, 2 * FF])
        w2 = sb("w2", [P, 3, D])
        cols = sb("cols", [P, NCOL])
        qk_scale = sb("qk_scale", [P, 4 * DH])
        ident = sb("ident", [P, P])
        identb = sb("identb", [P, P], BF16)
        mean_w = sb("mean_w", [P, P])
        rot_base = sb("rot_base", [P, NT, 4 * DH])
        rot = sb("rot", [P, NT, 4 * DH])
        mask_q = sb("mask_q", [P, 2, CH], BF16)
        mask_k = sb("mask_k", [P, STW], BF16)
        pick = sb("pick", [P, HEADS, P], BF16)
        neg_half = sb("neg_half", [P, N])
        x_t = sb("x_t", [P, B, N])
        x_in = sb("x_in", [P, T])
        xs_a = sb("xs_a", [P, B, N])
        xs_f = sb("xs_f", [P, N])
        raw = sb("raw", [P, NT, 2 * INNER])
        sq = sb("sq", [P, 2, CH])
        rope = sb("rope", [P, NT, 2 * INNER])
        rope_b = sb("rope_b", [P, NT, 2 * INNER])
        ssq = sb("ssq", [P, NT, 2 * HEADS])
        ssq_c = sb("ssq_c", [P, NT, 2 * HEADS])
        rnorm = sb("rnorm", [P, NT, 2 * HEADS])
        v = sb("v", [P, 2, NT, HEADS * VW])
        qk_t = sb("qk_t", [P, 2, 8, N])
        qk_b = sb("qk_b", [P, 2, 8, N], BF16)
        negm = sb("negm", [P, NT, HEADS], BF16)
        negm_t = sb("negm_t", [P, STW], BF16)
        probs = sb("probs", [P, 4, STW])
        rsum = sb("rsum", [P, NT, HEADS])
        o = sb("o", [P, NT, INNER])
        o_t = sb("o_t", [P, 8, N])
        xc = sb("xc", [P, N])
        xsq = sb("xsq", [P, N])
        var = sb("var", [P, N])
        rstd = sb("rstd", [P, N])
        xn = sb("xn", [P, N])
        xg = sb("xg", [P, N])
        gate = sb("gate", [P, 3, N])
        hid = sb("hid", [P, 3, N])

        ps = [ctx.enter_context(nc.psum_tensor(f"ps{i}", [P, 512], F32)) for i in range(8)]
        PF = ps[0:2]
        PA = ps[2:4]
        PO = ps[4:6]
        PB = ps[6:8]
        negt_ps = PA[0][:, :].bitcast(BF16)

        s_const = sem("constants_loaded")
        s_wqkv, s_wo, s_w1, s_w2, s_cols, s_qks = (sem(f"{n}_loaded") for n in ("wqkv", "wo", "w1", "w2", "cols", "qk_scale"))
        s_zero = sem("zeros_set")
        s_xsa = sem("xs_a_ready")
        pf_full = [sem(f"front_bank{i}_full") for i in range(2)]
        pa_full = [sem(f"score_bank{i}_full") for i in range(2)]
        pb_full = [sem(f"back_bank{i}_full") for i in range(2)]
        s_rot = sem("rotation_tables_ready")
        s_raw = sem("raw_ready")
        s_sq = sem("squares_ready")
        s_ssq = sem("ssq_ready")
        s_clamp = sem("ssq_clamped")
        s_rn = sem("rnorm_ready")
        s_rmul = sem("rope_products_ready")
        s_radd = sem("rope_sum_ready")
        s_rope = sem("rope_ready")
        s_v = sem("v_ready")
        s_qkt = sem("qk_t_ready")
        s_negm = sem("negm_ready")
        s_negt = sem("negm_t_ready")
        s_probs = sem("probs_ready")
        s_av = sem("values_weighted")
        s_rsum = sem("rsum_ready")
        s_o = sem("o_ready")
        s_ot = sem("o_t_ready")
        s_x1 = sem("x_after_attention_ready")
        s_xc = sem("xc_ready")
        s_xsq = sem("xsq_ready")
        s_var = sem("var_ready")
        s_rstd = sem("rstd_ready")
        s_xn = sem("xn_ready")
        s_xg = sem("xg_ready")
        s_gate = sem("gate_ready")
        s_hid = sem("hid_ready")
        s_xt = sem("x_after_attention_kept")
        s_x2 = sem("x_kept")
        s_out = sem("out_written")
        e_load = sem("entry_inputs_loaded")
        e_pe, e_act, e_dve, e_pool = (sem(f"entry_{n}") for n in ("products", "activations", "vectors", "powers"))
        f_pe, f_act, f_dve, f_pool = (sem(f"final_{n}") for n in ("products", "activations", "vectors", "powers"))

        def at(per_step, s, k):
            if type(s) is tuple:
                layer, b = s
                return layer * (B * per_step) + (b * per_step + k + 1)
            return s * per_step + k + 1

        def plus(s, n):
            if type(s) is tuple:
                layer, b = s
                return (layer + (b + n) // B, (b + n) % B) if (b + n) // B else (layer, b + n)
            return s + n

        def batch(s):
            return s[1] if type(s) is tuple else s % B

        def first(s):
            return type(s) is not tuple and s == 0

        F_USES, A_USES, B_USES = 10, (11, 10), (7, 4)
        OT = [(0, 0), (1, 0), (0, 1), (1, 1)]
        WO_, MEAN, VAR, G01, C2, A01, W2_ = (0, 2), (1, 2), (0, 3), (0, 4), (1, 3), (0, 5), (0, 6)

        def layer_of(s):
            return s[0] if type(s) is tuple else s // B

        raw4 = raw[:, :, :].rearrange("p t (g n) -> p (t g) n", n=T)
        rope4 = rope[:, :, :].rearrange("p t (g n) -> p (t g) n", n=T)
        ropeb4 = rope_b[:, :, :].rearrange("p t (g n) -> p (t g) n", n=T)
        x_all = x_t[:, :, :].rearrange("p b n -> p (b n)")
        xs_all = xs_a[:, :, :]
        q_e, k_e, neg_q, neg_k = (raw4[:, i, :] for i in range(4))
        v_e, masked, att, y = (rope4[:, i, :] for i in range(4))
        yc, ysq, yvar, yrstd = (ropeb4[:, i, :] for i in range(4))
        qkf = qk_t[:, :, :, :].rearrange("p a c n -> p (a c n)")
        soft = qkf[:, 0:2 * T].rearrange("p (i k) -> p i k", k=N)
        soft_t = qkf[:, 2 * T:4 * T].rearrange("p (b n) -> p b n", n=2 * N)
        w_e = [o[:, 0, i * P:(i + 1) * P] for i in range(8)]
        WQ, WK, WV, WOT, XQ, XK, XV, SAME = range(8)
        vb1, vb2 = o[:, 1, 0:P], o[:, 1, P:2 * P]
        ctx_t = o_t[:, :, :].rearrange("p c n -> p (c n)")[:, 0:T]
        x_nb = o_t[:, :, :].rearrange("p c n -> p (c n)")[:, T:2 * T]
        ecols = sb("ecols", [P, 5])
        emax = sb("emax", [P, 8])
        esum = sb("esum", [P, 8])
        erec = sb("erec", [P, 8])
        half = lambda ap, g: ap[:, g * CH:(g + 1) * CH]
        E_PE = ["q0", "q1", "k0", "k1", "v0", "v1", "s0", "s1", "att0", "att1", "wo0", "wo1", "mean0", "mean1",
                "var0", "var1", "xk0", "xk1", "xv0", "xv1", "xq0", "xq1", "sc0", "sc1", "sc2", "sc3", "tr0", "tr1", "tr2",
                "tr3", "xo0", "xo1", "xo2", "xo3", "mean2", "mean3", "var2", "var3"]
        E_ACT = ["exp0", "exp1", "exp2", "exp3", "att0", "att1", "sq0", "sq1", "soft0", "soft1", "soft2", "soft3",
                 "tr0", "tr1", "tr2", "tr3", "sq2", "sq3"]
        E_DVE = ["neg0", "neg1", "neg2", "neg3", "pos0", "pos1", "pos2", "pos3", "v0", "v1", "q0", "q1", "k0", "k1",
                 "masked0", "masked1", "y0", "y1", "yc0", "yc1", "var0", "var1", "x0", "x1",
                 "xk0", "xk1", "xv0", "xv1", "xq0", "xq1", "max0", "max1", "max2", "max3", "rec", "soft", "y2", "y3",
                 "yc2", "yc3", "var2", "var3", "done"]
        E_POOL = ["rstd0", "rstd1", "rstd2", "rstd3"]
        F_PE = ["mean0", "mean1", "var0", "var1"]
        F_ACT = ["sq0", "sq1"]
        F_DVE = ["sum0", "sum1", "yc0", "yc1", "var0", "var1", "y0", "y1"]
        F_POOL = ["rstd0", "rstd1"]
        N_ENTRY_LOADS = 25

        def entry_loads(eng):
            for dst, src in ([(x_nb, a["x_nb"]), (ecols[:, :], a["ecols"])]
                             + [(w_e[i][0:h, :], a[n]) for i, (n, h) in enumerate(
                                 (("wq", P), ("wk", P), ("wv", P), ("wot", P), ("xwq", P), ("xwk", DC), ("xwv", DC), ("same", P)))]
                             + [(vb1, a["bv"].broadcast_to([P, P])), (vb2, a["xbv"].broadcast_to([P, P])),
                                (ctx_t[0:DC, :], a["ctx_t"]), (mean_w[:, :], a["mean_w"]), (ident[:, :], a["ident"])]):
                eng.dma_start(dst, src).then_inc(e_load, 16)
            for dst, src in ((identb[:, :], a["identb"]), (mask_q[:, :, :], a["mask_q"]), (mask_k[:, :], a["mask_k"]),
                             (pick[:, :, :], a["pick"]), (rot_base[:, :, :], a["rot_base"])):
                eng.dma_start(dst, src).then_inc(s_const, 16)
        E_LOADS, C_LOADS = 15 * 16, 5 * 16

        def entry_tensor(pe):
            mm = nc.tensor.matmul
            done = lambda ins: ins.then_inc(e_pe, 1)
            act_did = lambda name: pe.wait_ge(e_act, E_ACT.index(name) + 1)
            dve_did = lambda name: pe.wait_ge(e_dve, E_DVE.index(name) + 1)
            pe.wait_ge(e_load, E_LOADS)
            for i, w in enumerate((WQ, WK)):
                for g in range(2):
                    done(mm(ps[2 * i + g][:, :], w_e[w], half(x_nb, g), start=True, stop=True))
            for g in range(2):
                for k in range(4):
                    kk = 4 * g + k
                    last = mm(ps[4 + g][:, k * P:(k + 1) * P], x_nb[:, kk * P:(kk + 1) * P], w_e[WV], start=True, stop=True,
                              skip_group_check=True)
                done(last)
            dve_did("k1")
            for g in range(2):
                for k in range(4):
                    c = slice((4 * g + k) * P, (4 * g + k + 1) * P)
                    last = mm(ps[g][:, k * P:(k + 1) * P], k_e[:, c], q_e[:, c], start=True, stop=True, skip_group_check=True)
                done(last)
            for g in range(2):
                dve_did(f"masked{g}")
                for k in range(4):
                    c = slice((4 * g + k) * P, (4 * g + k + 1) * P)
                    last = mm(ps[2 + g][:, k * P:(k + 1) * P], v_e[:, c], masked[:, c], start=True, stop=True, skip_group_check=True)
                done(last)
            act_did("att1")
            for g in range(2):
                done(mm(ps[4 + g][:, :], w_e[WOT], half(att, g), start=True, stop=True))

            def norm_sums(src, ready, sq_ready, b0, b1):
                for g in range(2):
                    ready(g)
                    done(mm(ps[b0 + g][:, :], mean_w[:, :], half(src, g), start=True, stop=True))
                for g in range(2):
                    sq_ready(g)
                    done(mm(ps[b1 + g][:, :], mean_w[:, :], half(ysq, g), start=True, stop=True))

            norm_sums(y, lambda g: dve_did(f"y{g}"), lambda g: act_did(f"sq{g}"), 6, 0)
            for g in range(2):
                done(mm(ps[4 + g][:, :], w_e[XK][0:DC, :], half(ctx_t, g)[0:DC, :], start=True, stop=True))
            for g in range(2):
                for k in range(4):
                    kk = 4 * g + k
                    last = mm(ps[6 + g][:, k * P:(k + 1) * P], ctx_t[0:DC, kk * P:(kk + 1) * P], w_e[XV][0:DC, :],
                              start=True, stop=True, skip_group_check=True)
                done(last)
            for g in range(2):
                dve_did("x1")
                done(mm(ps[2 + g][:, :], w_e[XQ], half(x_all, g), start=True, stop=True))
            for b in range(B):
                dve_did("xq1")
                for j in range(2):
                    i = 2 * b + j
                    last = mm(ps[b][:, j * N:(j + 1) * N], q_e[:, i * P:(i + 1) * P], k_e[:, b * N:(b + 1) * N],
                              start=True, stop=True, skip_group_check=True)
                done(last)
            dve_did("soft")
            for b in range(B):
                for kt in range(2):
                    for j in range(2):
                        last = nc.tensor.transpose(ps[4 + b][:, kt * N + j * P:kt * N + (j + 1) * P],
                                                   soft[:, 2 * b + j, kt * P:(kt + 1) * P], ident[:, :])
                done(last)
            for b in range(B):
                act_did(f"tr{b}")
                for kt in range(2):
                    i = 2 * b + kt
                    last = mm(ps[b][:, 0:N], v_e[:, i * P:(i + 1) * P], soft_t[:, b, kt * N:(kt + 1) * N],
                              start=(kt == 0), stop=(kt == 1))
                done(last)
            norm_sums(y, lambda g: dve_did(f"y{2 + g}"), lambda g: act_did(f"sq{2 + g}"), 4, 6)

        def entry_scalar(act):
            fn = nc.scalar.activation
            done = lambda ins: ins.then_inc(e_act, 1)
            pe_did = lambda name: act.wait_ge(e_pe, E_PE.index(name) + 1)
            dve_did = lambda name: act.wait_ge(e_dve, E_DVE.index(name) + 1)
            for i in range(4):
                dve_did(f"neg{i}")
                src = half((neg_q, neg_k)[i // 2], i % 2)
                done(fn(src, src, ACT.Exp))
            for g in range(2):
                pe_did(f"att{g}")
                done(nc.scalar.copy(half(att, g), ps[2 + g][:, :]))
            for g in range(2):
                dve_did(f"yc{g}")
                done(fn(half(ysq, g), half(yc, g), ACT.Square))
            for b in range(B):
                dve_did(f"max{b}")
                for j in range(2):
                    i = 2 * b + j
                    last = fn(soft[:, i, :], ps[b][:, j * N:(j + 1) * N], ACT.Exp, bias=emax[:, i:i + 1],
                              accum_out=esum[:, i:i + 1])
                done(last)
            for b in range(B):
                pe_did(f"tr{b}")
                done(nc.scalar.copy(soft_t[:, b, :], ps[4 + b][:, :]))
            for g in range(2):
                dve_did(f"yc{2 + g}")
                done(fn(half(ysq, g), half(yc, g), ACT.Square))

        def entry_vector(dve):
            tt, tsc = nc.vector.tensor_tensor, nc.vector.tensor_scalar
            done = lambda ins: ins.then_inc(e_dve, 1)
            pe_did = lambda name: dve.wait_ge(e_pe, E_PE.index(name) + 1)
            act_did = lambda name: dve.wait_ge(e_act, E_ACT.index(name) + 1)
            pool_did = lambda name: dve.wait_ge(e_pool, E_POOL.index(name) + 1)
            dve_did = lambda name: dve.wait_ge(e_dve, E_DVE.index(name) + 1)
            nc.vector.memset(xs_a[64:P, :, 0:1], 0.0)
            nc.vector.memset(xs_f[64:P, 0:1], 0.0)
            nc.vector.memset(negm_t[:, :], 0.0).then_inc(s_zero, 1)
            dve.wait_ge(e_load, E_LOADS)
            pos = (yc, ysq)
            for i in range(4):
                pe_did(("q0", "q1", "k0", "k1")[i])
                done(tsc(half((neg_q, neg_k)[i // 2], i % 2), ps[i][:, :], ecols[:, i // 2:i // 2 + 1], 0.0, ALU.add, ALU.min))
            for i in range(4):
                done(tsc(half(pos[i // 2], i % 2), ps[i][:, :], ecols[:, i // 2:i // 2 + 1], 0.0, ALU.add, ALU.max))
            for g in range(2):
                pe_did(f"v{g}")
                done(tt(half(v_e, g).rearrange("p (k e) -> p k e", e=P), ps[4 + g][:, :].rearrange("p (k e) -> p k e", e=P),
                        vb1.unsqueeze(1).broadcast_to([P, 4, P]), ALU.add))
            for i in range(4):
                act_did(f"exp{i}")
                if i == 0:
                    dve_did("pos3")
                done(tt(half((q_e, k_e)[i // 2], i % 2), half(pos[i // 2], i % 2), half((neg_q, neg_k)[i // 2], i % 2), ALU.add))
            for g in range(2):
                pe_did(f"s{g}")
                done(tt(half(masked, g).rearrange("p (k e) -> p k e", e=P), ps[g][:, :].rearrange("p (k e) -> p k e", e=P),
                        w_e[SAME].unsqueeze(1).broadcast_to([P, 4, P]), ALU.mult))
            for g in range(2):
                pe_did(f"wo{g}")
                done(nc.vector.scalar_tensor_tensor(out=half(y, g), in0=ps[4 + g][:, :], scalar=ecols[:, 2:3],
                                                    in1=half(x_nb, g), op0=ALU.add, op1=ALU.add))

            def norm(k, b0, b1):
                for g in range(2):
                    pe_did(f"mean{k + g}")
                    if g == 0:
                        dve_did(f"y{k + 1}")
                    done(tt(half(yc, g), half(y, g), ps[b0 + g][:, :], ALU.subtract))
                for g in range(2):
                    pe_did(f"var{k + g}")
                    done(tsc(half(yvar, g), ps[b1 + g][:, :], EPS, None, ALU.add))

            norm(0, 6, 0)
            for g in range(2):
                pool_did(f"rstd{g}")
                done(tt(x_t[:, :, g * P:(g + 1) * P], half(yc, g).rearrange("p (n b) -> p b n", b=B),
                        half(yrstd, g).rearrange("p (n b) -> p b n", b=B), ALU.mult))
            for g in range(2):
                pe_did(f"xk{g}")
                done(tsc(half(k_e, g), ps[4 + g][:, :], ecols[:, 4:5], None, ALU.add))
            for g in range(2):
                pe_did(f"xv{g}")
                done(tt(half(v_e, g).rearrange("p (k e) -> p k e", e=P), ps[6 + g][:, :].rearrange("p (k e) -> p k e", e=P),
                        vb2.unsqueeze(1).broadcast_to([P, 4, P]), ALU.add))
            for g in range(2):
                pe_did(f"xq{g}")
                done(tsc(half(q_e, g), ps[2 + g][:, :], ecols[:, 3:4], None, ALU.add))
            for b in range(B):
                pe_did(f"sc{b}")
                done(nc.vector.tensor_reduce(emax[:, 2 * b:2 * b + 2], ps[b][:, :].rearrange("p (j k) -> p j k", j=2),
                                             AX.X, ALU.max, negate=True))
            act_did("soft3")
            done(nc.vector.reciprocal(erec[:, :], esum[:, :]))
            dve_did("rec")
            done(tt(soft, soft, erec[:, :].unsqueeze(2).broadcast_to([P, 8, N]), ALU.mult))
            for g in range(2):
                for j in range(2):
                    b = 2 * g + j
                    pe_did(f"xo{b}")
                    last = tt(y[:, b * N:(b + 1) * N], ps[b][:, 0:N], x_t[:, b, :], ALU.add)
                done(last)
            norm(2, 4, 6)
            for g in range(2):
                pool_did(f"rstd{2 + g}")
                bs = slice(2 * g, 2 * g + 2)
                c3 = half(yc, g).rearrange("p (b n) -> p b n", n=N)
                r3 = half(yrstd, g).rearrange("p (b n) -> p b n", n=N)
                tt(half(x_in, g), half(yc, g), half(yrstd, g), ALU.mult)
                last = tt(x_t[:, bs, :], c3, r3, ALU.mult)
                if g == 1:
                    last.then_inc(s_x2, 1)
                tt(xs_a[0:64, bs, :], c3[0:64], r3[0:64], ALU.mult)
                tt(xs_a[64:P, bs, 1:N], c3[64:P, :, 0:N - 1], r3[64:P, :, 0:N - 1], ALU.mult).then_inc(s_xsa, 2)

        def entry_gpsimd(pool):
            dve_did = lambda name: pool.wait_ge(e_dve, E_DVE.index(name) + 1)
            nc.gpsimd.memset(neg_half[:, :], -0.5).then_inc(s_zero, 1)
            nc.gpsimd.memset(v[:, :, :, :].rearrange("p a t (h e) -> p (a t h) e", e=VW)[:, :, DH:VW], 1.0).then_inc(s_zero, 1)
            pool.wait_ge(s_zero, 3)
            for k in (0, 2):
                for g in range(2):
                    dve_did(f"var{k + g}")
                    for j in range(2):
                        c = slice((2 * g + j) * N, (2 * g + j + 1) * N)
                        last = nc.gpsimd.tensor_tensor(yrstd[:, c], yvar[:, c], neg_half[:, :], ALU.pow)
                    last.then_inc(e_pool, 1)

        def final_tensor(pe):
            dve_did = lambda name: pe.wait_ge(f_dve, F_DVE.index(name) + 1)
            for g in range(2):
                dve_did(f"sum{g}")
                nc.tensor.matmul(ps[g][:, :], mean_w[:, :], half(y, g), start=True, stop=True).then_inc(f_pe, 1)
            for g in range(2):
                pe.wait_ge(f_act, g + 1)
                nc.tensor.matmul(ps[2 + g][:, :], mean_w[:, :], half(ysq, g), start=True, stop=True).then_inc(f_pe, 1)

        def final_scalar(act):
            for g in range(2):
                act.wait_ge(f_dve, F_DVE.index(f"yc{g}") + 1)
                nc.scalar.activation(half(ysq, g), half(yc, g), ACT.Square).then_inc(f_act, 1)

        def final_vector(dve):
            dve_did = lambda name: dve.wait_ge(f_dve, F_DVE.index(name) + 1)
            dve.wait_ge(s_x2, 1 + DEPTH * B)
            for g in range(2):
                nc.vector.tensor_tensor(half(y, g), half(x_all, g), half(x_in, g), ALU.add).then_inc(f_dve, 1)
            for g in range(2):
                dve.wait_ge(f_pe, g + 1)
                dve_did(f"sum{g}")
                nc.vector.tensor_tensor(half(yc, g), half(y, g), ps[g][:, :], ALU.subtract).then_inc(f_dve, 1)
            for g in range(2):
                dve.wait_ge(f_pe, 3 + g)
                nc.vector.tensor_scalar(half(yvar, g), ps[2 + g][:, :], EPS, None, ALU.add).then_inc(f_dve, 1)
            for g in range(2):
                dve.wait_ge(f_pool, g + 1)
                nc.vector.tensor_tensor(half(y, g), half(yc, g), half(yrstd, g), ALU.mult).then_inc(f_dve, 1)

        def final_gpsimd(pool):
            for g in range(2):
                pool.wait_ge(f_dve, F_DVE.index(f"var{g}") + 1)
                for j in range(2):
                    c = slice((2 * g + j) * N, (2 * g + j + 1) * N)
                    last = nc.gpsimd.tensor_tensor(yrstd[:, c], yvar[:, c], neg_half[:, :], ALU.pow)
                last.then_inc(f_pool, 1)

        def final_store(eng):
            for g in range(2):
                eng.wait_ge(f_dve, F_DVE.index(f"y{g}") + 1)
                eng.dma_start(out[:, g * CH:(g + 1) * CH], half(y, g)).then_inc(s_out, 16)
            eng.wait_ge(s_out, 32)

        block = ctx.enter_context(nc.Block())

        def iteration(s, turn, back_a, scores, back_b, shift, head, back_slot, proj_slot, tail,
                      do_back=True, do_attend=True, do_proj=True):
            if do_attend:
                turn(plus(s, 1))
            if do_back:
                back_a(s)
            if do_attend:
                scores(plus(s, 1))
            if do_back:
                back_b(s)
            if do_attend:
                shift(plus(s, 1))
            for slot in range(HEADS):
                if do_attend:
                    head(plus(s, 1), slot)
                if do_back:
                    back_slot(s, slot)
                if do_proj:
                    proj_slot(plus(s, 2), slot)
            if do_attend:
                tail(plus(s, 1))
            if do_proj:
                proj_slot(plus(s, 2), HEADS)

        def run(fori, turn, back_a, scores, back_b, shift, head, back_slot, proj_slot, tail):
            stages = (turn, back_a, scores, back_b, shift, head, back_slot, proj_slot, tail)
            for slot in range(HEADS + 1):
                proj_slot(0, slot)
            iteration(-1, *stages, do_back=False)
            with fori(0, DEPTH - 1) as layer:
                for b in range(B):
                    iteration((layer, b), *stages)
            for i in range((DEPTH - 1) * B, DEPTH * B):
                iteration(i, *stages, do_attend=i + 1 < DEPTH * B, do_proj=i + 2 < DEPTH * B)

        @block.sync
        def _(sp):
            def load(layer, what):
                if what == "wqkv":
                    sp.dma_start(wqkv[:, :], a["wqkv"][layer, :, :]).then_inc(s_wqkv, 16)
                elif what == "qks":
                    sp.dma_start(qk_scale[:, :], a["qk_scale"][layer, :, :].broadcast_to([P, 4 * DH])).then_inc(s_qks, 16)
                elif what == "wo":
                    sp.dma_start(wo[:, :, :], a["wo"][layer, :, :, :].rearrange("c p n -> p c n")).then_inc(s_wo, 16)
                elif what == "w1":
                    sp.dma_start(w1[:, :], a["w1"][layer, :, :]).then_inc(s_w1, 16)
                elif what == "w2":
                    sp.dma_start(w2[:, :, :], a["w2"][layer, :, :, :].rearrange("c p n -> p c n")).then_inc(s_w2, 16)
                elif what == "cols":
                    sp.dma_start(cols[:, :], a["cols"][layer, :, :]).then_inc(s_cols, 16)

            entry_loads(sp)
            for what in ("wqkv", "qks", "wo", "w1", "w2", "cols"):
                load(0, what)
            with sp.Fori(0, DEPTH - 1) as layer:
                last = (layer, B - 1)
                sp.wait_ge(pf_full[1], at(F_USES, last, 5))
                load(layer + 1, "wqkv")
                sp.wait_ge(s_rot, layer + 1)
                load(layer + 1, "qks")
                sp.wait_ge(pb_full[0], at(B_USES[0], last, WO_[1]))
                load(layer + 1, "wo")
                sp.wait_ge(pb_full[0], at(B_USES[0], last, A01[1]))
                load(layer + 1, "w1")
                sp.wait_ge(pb_full[0], at(B_USES[0], last, W2_[1]))
                load(layer + 1, "w2")
                sp.wait_ge(s_x2, at(1, last, 0) + 1)
                load(layer + 1, "cols")
            final_store(sp)

        @block.tensor
        def _(pe):
            mm = nc.tensor.matmul

            def front_bank_read(s, bank, use):
                if use == 0:
                    if not first(s):
                        pe.wait_ge(s_qkt, at(8, s, 6 + bank) - 8)
                elif use <= 6:
                    t, c = divmod(bank + 2 * (use - 1), 6)
                    if c < 4:
                        pe.wait_ge(s_sq, at(8, s, t * 4 + c))
                    else:
                        pe.wait_ge(s_v, at(4, s, t * 2 + c - 4))
                else:
                    pe.wait_ge(s_qkt, at(8, s, 2 * (use - 7) + bank))

            def proj_slot(s, slot):
                if slot >= 12:
                    return
                b = batch(s)
                t, c = slot // 6, slot % 6
                if slot == 0:
                    pe.wait_ge(s_xsa, B if first(s) else at(1, s, 0))
                    if b == 0:
                        pe.wait_ge(s_wqkv, layer_of(s) * 16 + 16)
                bank, use = slot % 2, slot // 2
                front_bank_read(s, bank, use)
                mm(PF[bank][:, :], xs_a[:, b, t * P:(t + 1) * P], wqkv[:, c * CH:(c + 1) * CH],
                   start=True, stop=True).then_inc(pf_full[bank], 1)

            def turn(s):
                for t in range(NT):
                    for c in range(4):
                        n = t * 4 + c
                        bank, use = n % 2, 6 + n // 2
                        pe.wait_ge(s_rope, at(8, s, n))
                        front_bank_read(s, bank, use)
                        for j in range(4):
                            last = nc.tensor.transpose(PF[bank][:, j * P:(j + 1) * P],
                                                       rope[:, t, c * CH + j * P:c * CH + (j + 1) * P], ident[:, :])
                        last.then_inc(pf_full[bank], 1)

            def scores(s):
                pe.wait_ge(s_qkt, at(8, s, 7))
                for t in range(NT):
                    for par in range(2):
                        if t == 1:
                            pe.wait_ge(s_negm, at(4, s, par))
                        elif not first(s):
                            pe.wait_ge(s_probs, at(HEADS, s, 14 + par) - HEADS)
                        mm(PA[par][:, :], identb[:, :], mask_q[:, t, :], start=True, stop=False, skip_group_check=True)
                        r = 64 * par
                        for hh in range(8):
                            for u in range(4):
                                w = 4 * t + u
                                lo = max(w - 1, 0) * WIN
                                n = (w + 1) * WIN - lo
                                last = mm(PA[par][32 * u:32 * u + 32, hh * 64 + 64 - n:hh * 64 + 64],
                                          qk_b[r:r + 64, 0, hh, w * WIN:(w + 1) * WIN],
                                          qk_b[r:r + 64, 1, hh, lo:lo + n], start=False, stop=(hh == 7 and u == 3),
                                          skip_group_check=True)
                        last.then_inc(pa_full[par], 1)

            def shift(s):
                pe.wait_ge(s_negm, at(4, s, 3))
                for t in range(NT):
                    last = nc.tensor.transpose(negt_ps[0:HEADS, t * P:(t + 1) * P], negm[:, t, :], identb[:, :])
                last.then_inc(pa_full[0], 1)

            def head(s, h):
                par, hh = h % 2, h // 2
                r = 64 * par
                bank = PA[par]
                if h < 2:
                    pe.wait_ge(s_negt, at(1, s, 0))
                else:
                    pe.wait_ge(s_probs, at(HEADS, s, h - 2))
                mm(bank[:, 0:STW], identb[:, :], mask_k[:, :], start=True, stop=False, skip_group_check=True)
                mm(bank[:, 0:STW], pick[:, h, :], negm_t[:, :], start=False, stop=False, skip_group_check=True)
                mm(bank[:, 0:SPAN], qk_t[r:r + 64, 1, hh, 0:P], qk_t[r:r + 64, 0, hh, 0:SPAN],
                   start=False, stop=False, skip_group_check=True)
                mm(bank[:, SPAN:STW], qk_t[r:r + 64, 1, hh, P:N], qk_t[r:r + 64, 0, hh, P:N],
                   start=False, stop=True, skip_group_check=True).then_inc(pa_full[par], 1)
                if h > 0:
                    weigh(s, h - 1)

            def weigh(s, h):
                g = [i for i, (lo, hi) in enumerate(GROUPS) if lo <= h < hi][0]
                j = h - GROUPS[g][0]
                if h == GROUPS[g][0] and not (first(s) and g == 0):
                    pe.wait_ge(s_o, at(3, s, g) - 1)
                if h == 0:
                    pe.wait_ge(s_v, at(4, s, 3))
                pe.wait_ge(s_probs, at(HEADS, s, h))
                vb = v[:, batch(s) % 2, :, :]
                pr = probs[:, h % 4, :]
                mm(PO[0][:, j * VW:(j + 1) * VW], pr[:, 0:P], vb[:, 0, h * VW:(h + 1) * VW], start=True, stop=True,
                   skip_group_check=True)
                mm(PO[1][:, j * VW:(j + 1) * VW], pr[:, SPAN:STW], vb[:, 1, h * VW:(h + 1) * VW], start=True, stop=False,
                   skip_group_check=True)
                mm(PO[1][0:WIN, j * VW:(j + 1) * VW], pr[:, P:SPAN], vb[:, 0, h * VW:(h + 1) * VW], start=False, stop=True,
                   skip_group_check=True).then_inc(s_av, 1)

            def tail(s):
                weigh(s, HEADS - 1)

            def loaded(s, which):
                if batch(s) == 0:
                    pe.wait_ge(which, layer_of(s) * 16 + 16)

            def back_a(s):
                pe.wait_ge(s_o, at(3, s, 2))
                for n in range(4):
                    t, half = n // 2, n % 2
                    bank = OT[n][0]
                    if n >= 2:
                        pe.wait_ge(s_ot, at(4, s, n - 2))
                    else:
                        pe.wait_ge(s_x2, at(1, s, 0))
                    for j in range(4):
                        c = half * 4 + j
                        last = nc.tensor.transpose(PB[bank][:, j * P:(j + 1) * P], o[:, t, c * P:(c + 1) * P], ident[:, :])
                    last.then_inc(pb_full[bank], 1)

            def back_b(s):
                pe.wait_ge(s_ot, at(4, s, 3))
                loaded(s, s_wo)
                for c in range(8):
                    last = mm(PB[0][:, 0:N], wo[:, c, :], o_t[:, c, :], start=(c == 0), stop=(c == 7))
                last.then_inc(pb_full[0], 1)

            def expand(bank, col, c, gate_part):
                m, w0 = FCH[c], gate_part * FF + c * P
                return mm(PB[bank][0:m, col:col + N], w1[:, w0:w0 + m], xg[:, :], start=True, stop=True, skip_group_check=True)

            def back_slot(s, slot):
                if slot == 1:
                    pe.wait_ge(s_x1, at(1, s, 0))
                    mm(PB[1][:, 0:N], mean_w[:, :], xs_f[:, :], start=True, stop=True).then_inc(pb_full[1], 1)
                elif slot == 3:
                    pe.wait_ge(s_xsq, at(1, s, 0))
                    pe.wait_ge(s_xt, at(1, s, 0))
                    mm(PB[0][:, 0:N], mean_w[:, :], xsq[:, :], start=True, stop=True).then_inc(pb_full[0], 1)
                elif slot == 7:
                    pe.wait_ge(s_xg, at(1, s, 0))
                    loaded(s, s_w1)
                    expand(0, 0, 0, 1)
                    expand(0, N, 1, 1).then_inc(pb_full[0], 1)
                elif slot == 8:
                    expand(1, 0, 2, 1)
                    expand(1, N, 2, 0).then_inc(pb_full[1], 1)
                elif slot == 10:
                    pe.wait_ge(s_gate, at(3, s, 1))
                    expand(0, 0, 0, 0)
                    expand(0, N, 1, 0).then_inc(pb_full[0], 1)
                elif slot == 13:
                    pe.wait_ge(s_hid, at(3, s, 2))
                    loaded(s, s_w2)
                    for c in range(3):
                        last = mm(PB[0][:, 0:N], w2[0:FCH[c], c, :], hid[0:FCH[c], c, :], start=(c == 0), stop=(c == 2))
                    last.then_inc(pb_full[0], 1)

            entry_tensor(pe)
            run(pe.Fori, turn, back_a, scores, back_b, shift, head, back_slot, proj_slot, tail)
            final_tensor(pe)

        @block.scalar
        def _(act):
            fn = nc.scalar.activation

            def proj_slot(s, slot):
                if slot >= 12:
                    return
                t, c = slot // 6, slot % 6
                bank, use = slot % 2, slot // 2
                act.wait_ge(pf_full[bank], at(F_USES, s, use))
                if c < 4:
                    n = t * 4 + c
                    if not first(s):
                        act.wait_ge(s_rmul, at(8, s, n) - 8)
                    nc.scalar.copy(raw[:, t, c * CH:(c + 1) * CH], PF[bank][:, :]).then_inc(s_raw, 1)
                    if not (first(s) and n < 2):
                        act.wait_ge(s_ssq, at(8, s, n) - 2)
                    fn(sq[:, n % 2, :], PF[bank][:, :], ACT.Square).then_inc(s_sq, 1)
                else:
                    h0 = (c - 4) * HC
                    dst = v[:, batch(s) % 2, t, h0 * VW:(h0 + HC) * VW].rearrange("p (h e) -> p h e", e=VW)[:, :, 0:DH]
                    nc.scalar.copy(dst, PF[bank][:, :].rearrange("p (h e) -> p h e", e=DH)).then_inc(s_v, 1)

            def turn(s):
                for t in range(NT):
                    for c in range(4):
                        n = t * 4 + c
                        bank, use = n % 2, 6 + n // 2
                        act.wait_ge(pf_full[bank], at(F_USES, s, use))
                        src = PF[bank][:, :].rearrange("p (j t) -> p j t", j=4)
                        j0 = (c % 2) * 4
                        nc.scalar.copy(qk_b[:, c // 2, j0:j0 + 4, t * P:(t + 1) * P], src)
                        nc.scalar.copy(qk_t[:, c // 2, j0:j0 + 4, t * P:(t + 1) * P], src).then_inc(s_qkt, 1)

            def back_a(s):
                for n in range(4):
                    t, half = n // 2, n % 2
                    bank, use = OT[n]
                    act.wait_ge(pb_full[bank], at(B_USES[bank], s, use))
                    nc.scalar.copy(o_t[:, half * 4:half * 4 + 4, t * P:(t + 1) * P],
                                   PB[bank][:, :].rearrange("p (j t) -> p j t", j=4)).then_inc(s_ot, 1)

            def head(s, h):
                par, hh = h % 2, h // 2
                use = (3 if par == 0 else 2) + hh
                act.wait_ge(pa_full[par], at(A_USES[par], s, use))
                if not (first(s) and h < 4):
                    act.wait_ge(s_av, at(HEADS, s, h) - 4)
                fn(probs[:, h % 4, :], PA[par][:, 0:STW], ACT.Exp).then_inc(s_probs, 1)

            def back_slot(s, slot):
                if slot == 2:
                    act.wait_ge(s_xc, at(1, s, 0))
                    fn(xsq[:, :], xc[:, :], ACT.Square).then_inc(s_xsq, 1)
                elif slot == 9:
                    if batch(s) == 0:
                        act.wait_ge(s_cols, layer_of(s) * 16 + 16)
                    for c, (where, col) in enumerate(((G01, 0), (G01, N), (C2, 0))):
                        bank, use = where
                        m = FCH[c]
                        if c != 1:
                            act.wait_ge(pb_full[bank], at(B_USES[bank], s, use))
                        fn(gate[0:m, c, :], PB[bank][0:m, col:col + N], ACT.Gelu, bias=cols[0:m, 6 + c:7 + c]).then_inc(s_gate, 1)

            nothing = lambda *_: None
            entry_scalar(act)
            run(act.Fori, turn, back_a, nothing, nothing, nothing, head, back_slot, proj_slot, nothing)
            final_scalar(act)

        @block.vector
        def _(dve):
            tt, tsc = nc.vector.tensor_tensor, nc.vector.tensor_scalar

            def combine(s, t, c):
                n = t * 4 + c
                ch = rope[:, t, c * CH:(c + 1) * CH]
                dve.wait_ge(s_rmul, at(8, s, n))
                tt(ch, ch, rope_b[:, t, c * CH:(c + 1) * CH], ALU.add).then_inc(s_radd, 1)
                if c == 0:
                    dve.wait_ge(s_rn, at(2, s, t))
                dve.wait_ge(s_radd, at(8, s, n))
                ch3 = ch.rearrange("p (h e) -> p h e", e=DH)
                tt(ch3, ch3, rnorm[:, t, c * HC:(c + 1) * HC].unsqueeze(2).broadcast_to([P, HC, DH]),
                   ALU.mult).then_inc(s_rope, 1)

            def proj_slot(s, slot):
                if slot == 0 and batch(s) == 0:
                    dve.wait_ge(s_qks, layer_of(s) * 16 + 16)
                    if not first(s):
                        dve.wait_ge(s_rmul, at(8, s, 0) - 1)
                    tt(rot[:, :, :], rot_base[:, :, :], qk_scale[:, :].unsqueeze(1).broadcast_to([P, NT, 4 * DH]),
                       ALU.mult).then_inc(s_rot, 1)
                if slot < 12 and slot % 6 < 4:
                    t, c = slot // 6, slot % 6
                    n = t * 4 + c
                    dve.wait_ge(s_sq, at(8, s, n))
                    nc.vector.tensor_reduce(ssq[:, t, c * HC:(c + 1) * HC], sq[:, n % 2, :].rearrange("p (h e) -> p h e", e=DH),
                                            AX.X, ALU.add).then_inc(s_ssq, 1)
                    if c == 3:
                        dve.wait_ge(s_ssq, at(8, s, n))
                        if not first(s):
                            dve.wait_ge(s_rn, at(2, s, t) - 2)
                        tsc(ssq_c[:, t, :], ssq[:, t, :], 1e-24, None, ALU.max).then_inc(s_clamp, 1)
                if 7 <= slot < 11:
                    combine(s, 0, slot - 7)
                if slot >= 13:
                    combine(s, 1, slot - 13)

            def scores(s):
                for t in range(NT):
                    for par in range(2):
                        dve.wait_ge(pa_full[par], at(A_USES[par], s, t))
                        nc.vector.tensor_reduce(negm[:, t, :].rearrange("p (h two) -> p two h", two=2)[:, par, :],
                                                PA[par][:, :].rearrange("p (h k) -> p h k", h=8), AX.X, ALU.max,
                                                negate=True).then_inc(s_negm, 1)

            def shift(s):
                dve.wait_ge(pa_full[0], at(A_USES[0], s, 2))
                nc.vector.tensor_copy(negm_t[0:HEADS, 0:SPAN], negt_ps[0:HEADS, 0:SPAN])
                nc.vector.tensor_copy(negm_t[0:HEADS, SPAN:STW], negt_ps[0:HEADS, P:N]).then_inc(s_negt, 1)

            def evacuate(s, g):
                lo, hi = GROUPS[g]
                n = hi - lo
                dve.wait_ge(s_av, at(HEADS, s, hi - 1))
                for t in range(NT):
                    src = PO[t][:, 0:n * VW].rearrange("p (h e) -> p h e", e=VW)
                    nc.vector.reciprocal(rsum[:, t, lo:hi], src[:, :, DH]).then_inc(s_rsum, 1)
                dve.wait_ge(s_rsum, at(6, s, 2 * g + 1))
                for t in range(NT):
                    src = PO[t][:, 0:n * VW].rearrange("p (h e) -> p h e", e=VW)
                    last = tt(o[:, t, lo * DH:hi * DH].rearrange("p (h e) -> p h e", e=DH), src[:, :, 0:DH],
                              rsum[:, t, lo:hi].unsqueeze(2).broadcast_to([P, n, DH]), ALU.mult)
                last.then_inc(s_o, 1)

            def head(s, h):
                for g, (lo, hi) in enumerate(GROUPS[:2]):
                    if h == hi + 1:
                        evacuate(s, g)

            def tail(s):
                evacuate(s, 2)

            def shifted(dst, bank, b, op):
                op(dst[0:64, :], bank[0:64, 0:N], x_t[0:64, b, :])
                return op(dst[64:P, 1:N], bank[64:P, 0:N - 1], x_t[64:P, b, 0:N - 1])

            def back_b(s):
                b = batch(s)
                dve.wait_ge(pb_full[0], at(B_USES[0], s, WO_[1]))
                shifted(xs_f, PB[0], b, lambda d, p, x: tt(d, p, x, ALU.add)).then_inc(s_x1, 1)
                dve.wait_ge(s_x1, at(1, s, 0))
                tt(x_t[:, b, :], PB[0][:, 0:N], x_t[:, b, :], ALU.add).then_inc(s_xt, 1)

            def back_slot(s, slot):
                b = batch(s)
                if slot == 1:
                    dve.wait_ge(pb_full[1], at(B_USES[1], s, MEAN[1]))
                    tt(xc[:, :], xs_f[:, :], PB[1][:, 0:N], ALU.subtract).then_inc(s_xc, 1)
                elif slot == 3:
                    dve.wait_ge(pb_full[0], at(B_USES[0], s, VAR[1]))
                    tsc(var[:, :], PB[0][:, 0:N], EPS, None, ALU.add).then_inc(s_var, 1)
                elif slot == 5:
                    dve.wait_ge(s_rstd, at(1, s, 0))
                    tt(xn[:, :], xc[:, :], rstd[:, :], ALU.mult).then_inc(s_xn, 1)
                    dve.wait_ge(s_xn, at(1, s, 0))
                    if b == 0:
                        dve.wait_ge(s_cols, layer_of(s) * 16 + 16)
                    tsc(xg[:, :], xn[:, :], cols[:, 0:1], cols[:, 1:2], ALU.mult, ALU.add).then_inc(s_xg, 1)
                elif slot in (10, 11):
                    for c, where, col, event in (((2, C2, N, 0),) if slot == 10 else ((0, A01, 0, 1), (1, A01, N, 2))):
                        bank, use = where
                        m = FCH[c]
                        dve.wait_ge(s_gate, at(3, s, c))
                        if col != N or c == 2:
                            dve.wait_ge(pb_full[bank], at(B_USES[bank], s, use))
                        nc.vector.scalar_tensor_tensor(out=hid[0:m, c, :], in0=PB[bank][0:m, col:col + N],
                                                       scalar=cols[0:m, 3 + c:4 + c], in1=gate[0:m, c, :],
                                                       op0=ALU.add, op1=ALU.mult).then_inc(s_hid, 1)
                elif slot == 13:
                    dve.wait_ge(pb_full[0], at(B_USES[0], s, W2_[1]))
                    add = lambda d, p, x, bias: nc.vector.scalar_tensor_tensor(out=d, in0=p, scalar=bias, in1=x,
                                                                              op0=ALU.add, op1=ALU.add)
                    add(xs_a[0:64, b, :], PB[0][0:64, 0:N], x_t[0:64, b, :], cols[0:64, 2:3])
                    add(xs_a[64:P, b, 1:N], PB[0][64:P, 0:N - 1], x_t[64:P, b, 0:N - 1], cols[64:P, 2:3]).then_inc(s_xsa, 1)
                    dve.wait_ge(s_xsa, at(1, plus(s, B), 0))
                    add(x_t[:, b, :], PB[0][:, 0:N], x_t[:, b, :], cols[:, 2:3]).then_inc(s_x2, 1)

            nothing = lambda *_: None
            entry_vector(dve)
            run(dve.Fori, nothing, nothing, scores, back_b, shift, head, back_slot, proj_slot, tail)
            final_vector(dve)

        @block.gpsimd
        def _(pool):
            tt = nc.gpsimd.tensor_tensor

            def products(s, t, c):
                n = t * 4 + c
                kind = c // 2
                if n == 0 and batch(s) == 0:
                    pool.wait_ge(s_rot, layer_of(s) + 1)
                pool.wait_ge(s_raw, at(8, s, n))
                if not first(s):
                    pool.wait_ge(pf_full[n % 2], at(F_USES, s, 6 + n // 2) - F_USES)
                ch = slice(c * CH, (c + 1) * CH)
                x3 = raw[:, t, ch].rearrange("p (h e) -> p h e", e=DH)
                a3 = rope[:, t, ch].rearrange("p (h e) -> p h e", e=DH)
                b3 = rope_b[:, t, ch].rearrange("p (h e) -> p h e", e=DH)
                ta = rot[:, t, kind * 2 * DH:kind * 2 * DH + DH].unsqueeze(1)
                tb = rot[:, t, kind * 2 * DH + DH:(kind + 1) * 2 * DH].unsqueeze(1)
                hf = DH // 2
                tt(a3, x3, ta.broadcast_to([P, HC, DH]), ALU.mult)
                tt(b3[:, :, 0:hf], x3[:, :, hf:DH], tb[:, :, 0:hf].broadcast_to([P, HC, hf]), ALU.mult)
                tt(b3[:, :, hf:DH], x3[:, :, 0:hf], tb[:, :, hf:DH].broadcast_to([P, HC, hf]), ALU.mult).then_inc(s_rmul, 1)

            def proj_slot(s, slot):
                if slot in (5, 11):
                    t = slot // 6
                    pool.wait_ge(s_clamp, at(2, s, t))
                    if not first(s):
                        pool.wait_ge(s_rope, at(8, s, t * 4 + 3) - 8)
                    tt(rnorm[:, t, :], ssq_c[:, t, :], neg_half[:, 0:2 * HEADS], ALU.pow).then_inc(s_rn, 1)
                if 1 <= slot < 5:
                    products(s, 0, slot - 1)
                if 7 <= slot < 11:
                    products(s, 1, slot - 7)

            def back_slot(s, slot):
                if slot == 4:
                    pool.wait_ge(s_var, at(1, s, 0))
                    tt(rstd[:, :], var[:, :], neg_half[:, :], ALU.pow).then_inc(s_rstd, 1)

            nothing = lambda *_: None
            entry_gpsimd(pool)
            run(pool.Fori, nothing, nothing, nothing, nothing, nothing, nothing, back_slot, proj_slot,
                nothing)
            final_gpsimd(pool)


def tables():
    half = np.arange(0, DH, 2, dtype=np.float32)
    inv_freq = np.float32(1.0) / np.float32(10000.0) ** (half / np.float32(DH))
    t = np.arange(N, dtype=np.float32)
    freqs = (t[:, None] * inv_freq[None, :]).astype(np.float32)
    base = ((half + np.float32(0.4 * DH)) / np.float32(1.4 * DH)).astype(np.float32)
    power = ((t - N // 2) / (WIN // 2)).astype(np.float32)
    scale = (base[None, :].astype(np.float64) ** power[:, None].astype(np.float64))
    cos, sin = np.cos(freqs.astype(np.float64)), np.sin(freqs.astype(np.float64))
    two = lambda lo, hi: np.concatenate([lo, hi], -1)
    rows = np.stack([two(cos * scale, cos * scale) * 8.0, two(-sin * scale, sin * scale) * 8.0,
                     two(cos / scale, cos / scale), two(-sin / scale, sin / scale)], 1)
    rot_base = rows.reshape(NT, P, 4 * DH).transpose(1, 0, 2).astype(np.float32)
    bf = mybir.dt.np(BF16)
    i, rel = np.arange(WIN)[:, None], np.arange(2 * WIN)[None, :] - WIN
    win = np.where((i < rel) | (i > rel + WIN), BIG, 0.0)
    later = np.tile(win, (4, 1))
    start = later.copy()
    start[0:WIN, 0:WIN] = BIG
    mask_q = np.stack([np.tile(start, (1, 8)), np.tile(later, (1, 8))], 1).astype(bf)
    j, q = np.arange(P)[:, None], np.arange(SPAN)[None, :]
    near = (q // WIN == j // WIN) | (q // WIN == j // WIN + 1)
    allowed = near & (j <= q) & (q <= j + WIN)
    full = np.where(allowed, 0.0, BIG)
    mask_k = np.concatenate([full, full[:, 0:P]], 1).astype(bf)
    pick = np.zeros((P, HEADS, P), bf)
    for h in range(HEADS):
        pick[h, h, :] = 1
    pos = np.arange(P) // B
    return {
        "rot_base": rot_base, "mask_q": mask_q, "mask_k": mask_k, "pick": pick,
        "ident": np.eye(P, dtype=np.float32), "identb": np.eye(P).astype(bf),
        "mean_w": np.full((P, P), 1.0 / P, np.float32),
        "same": (pos[:, None] == pos[None, :]).astype(np.float32),
    }


def kernel(**inputs):
    import concourse.bacc as bacc
    from concourse.bass_utils import run_bass_kernel_spmd

    f = {n: np.asarray(x) for n, x in inputs.items()}
    row = lambda x: np.ascontiguousarray(x.reshape(1, -1))
    A, X, L = "L0_attn_", "L0_xattn_", "L0_ffn_"
    hf = DH // 2
    swap = lambda x: np.concatenate([x[:, hf:], x[:, :hf]], 1)
    qs, ks = f[L + "q_scale"], f[L + "k_scale"]
    wqkv = f[L + "Wqkv"]
    w2 = np.zeros((DEPTH, 3, P, D), np.float32)
    w2.reshape(DEPTH, 3 * P, D)[:, :FF] = f[L + "W2"]
    b1 = np.zeros((DEPTH, 2, 3 * P), np.float32)
    b1[:, :, :FF] = f[L + "b1"].reshape(DEPTH, 2, FF)
    cols = np.concatenate([f[L + "ln_g"][:, None], f[L + "ln_b"][:, None], f[L + "b2"][:, None], b1.reshape(DEPTH, 6, P)], 1)
    arrays = {
        "x_nb": f["x"].transpose(2, 1, 0).reshape(D, T), "ctx_t": f["ctx_768"].reshape(T, DC).T,
        "wq": f[A + "Wq"].T, "wk": f[A + "Wk"].T, "wv": f[A + "Wv"].T, "wot": f[A + "Wo"].T,
        "xwq": f[X + "Wq"], "xwk": f[X + "Wk"], "xwv": f[X + "Wv"],
        "bv": row(f[A + "bv"]), "xbv": row(f[X + "bv"]),
        "ecols": np.stack([f[A + "bq"], f[A + "bk"], f[A + "bo"], f[X + "bq"], f[X + "bk"]], 1),
        "wqkv": wqkv, "wo": f[L + "Wo"].reshape(DEPTH, 8, P, D), "w1": f[L + "W1"], "w2": w2,
        "cols": cols.transpose(0, 2, 1),
        "qk_scale": np.stack([qs, swap(qs), ks, swap(ks)], 1).reshape(DEPTH, 1, 4 * DH),
        **tables(),
    }
    nc = bacc.Bacc("TRN2", target_bir_lowering=False, num_devices=1)
    data, aps = {}, {}
    for name, x in arrays.items():
        x = np.ascontiguousarray(x)
        data[f"in_{name}"] = x
        aps[name] = nc.dram_tensor(f"in_{name}", x.shape, mybir.dt.from_np(x.dtype), kind="ExternalInput").ap()
    out = nc.dram_tensor("out_t", (D, T), F32, kind="ExternalOutput").ap()
    build(nc, aps, out)
    r = run_bass_kernel_spmd(nc, [data], core_ids=[0])
    return np.ascontiguousarray(r.results[0]["out_t"].T).reshape(B, N, D)
```

```python
import numpy as np
import concourse.bass as bass
from concourse import mybir
from contextlib import ExitStack

F32 = mybir.dt.float32
BF16 = mybir.dt.bfloat16
ALU = mybir.AluOpType
ACT = mybir.ActivationFunctionType
AX = mybir.AxisListType

P = 128
B, N, D = 4, 256, 128
T = B * N
DC = 96
DEPTH, HEADS, DH, WIN = 6, 16, 64, 32
INNER = HEADS * DH
QKV = 3 * INNER
FF = int(D * 4 * 2 / 3)
FCH = [128, 128, FF - 256]
NT = N // P
CH = 512
HC = CH // DH
SPAN = P + WIN
STW = SPAN + P
GROUPS = [(0, 3), (3, 6), (6, 9), (9, 12), (12, 14), (14, 16)]
NG = len(GROUPS)
VW = DH + 1
NCOL = 9
EPS = 1e-5
RSQRT_STEPS = 12
POOL_STEPS = 12
RSQRT_MAGIC = float(0x5F3759DF)
BIG = -1.0e30


def build(nc, a, out):
    ctx = ExitStack()
    with ctx:
        ctx.enter_context(nc.allow_low_precision(reason="shift of the softmax is rounded to bf16, and used alike in numerator and sum"))

        def sb(name, shape, dt=F32):
            return ctx.enter_context(nc.sbuf_tensor(name, shape, dt))

        def sem(name):
            return ctx.enter_context(nc.semaphore(name))

        wqkv = sb("wqkv", [P, QKV])
        wo = sb("wo", [P, 8, D])
        w1 = sb("w1", [P, 2 * FF])
        w2 = sb("w2", [P, 3, D])
        cols = sb("cols", [P, NCOL])
        qk_scale = sb("qk_scale", [P, 4 * DH])
        ident = sb("ident", [P, P])
        identb = sb("identb", [P, P], BF16)
        mean_w = sb("mean_w", [P, P])
        rot_base = sb("rot_base", [P, NT, 4 * DH])
        rot = sb("rot", [P, NT, 4 * DH])
        mask_q = sb("mask_q", [P, 2, CH], BF16)
        pick = sb("pick", [P, HEADS, P], BF16)
        x_t = sb("x_t", [P, B, N])
        x_in = sb("x_in", [P, T])
        xs_a = sb("xs_a", [P, B, N])
        xs_f = sb("xs_f", [P, N])
        raw = sb("raw", [P, NT, 2 * INNER])
        sq = sb("sq", [P, 2, CH])
        rope = sb("rope", [P, NT, 2 * INNER])
        rope_b = sb("rope_b", [P, NT, 2 * INNER])
        ssq = sb("ssq", [P, NT, 2 * HEADS])
        rn_guess = sb("rn_guess", [P, NT, 2 * HEADS])
        three_halves = sb("three_halves", [P, 2 * HEADS])
        rn_tmp = sb("rn_tmp", [P, 2 * HEADS])
        minus_half_ssq = sb("minus_half_ssq", [P, NT, 2 * HEADS])
        ssq_c = sb("ssq_c", [P, NT, 2 * HEADS])
        rnorm = sb("rnorm", [P, NT, 2 * HEADS])
        v = sb("v", [P, 2, NT, HEADS * VW])
        qk_t2 = sb("qk_t", [P, 2, 2, 8, N])
        qk_b2 = sb("qk_b", [P, 2, 2, 8, N], BF16)
        negm = sb("negm", [P, NT, HEADS], BF16)
        shift_k = sb("shift_k", [P, STW], BF16)
        probs = sb("probs", [P, 4, STW])
        rsum = sb("rsum", [P, NT, HEADS])
        o = sb("o", [P, NT, INNER])
        o_t = sb("o_t", [P, 8, N])
        xc = sb("xc", [P, N])
        xsq = sb("xsq", [P, N])
        var = sb("var", [P, N])
        rstd = sb("rstd", [P, N])
        rstd_tmp = sb("rstd_tmp", [P, N])
        xn = sb("xn", [P, N])
        xg = sb("xg", [P, N])
        gate = sb("gate", [P, 3, N])
        hid = sb("hid", [P, 3, N])

        ps = [ctx.enter_context(nc.psum_tensor(f"ps{i}", [P, 512], F32)) for i in range(8)]
        PF = ps[0:2]
        PA = ps[2:4]
        PO = ps[4:6]
        PB = ps[6:8]
        negt_ps = PA[0][:, :].bitcast(BF16)

        s_const = sem("constants_loaded")
        s_wqkv, s_wo, s_w1, s_w2, s_cols, s_qks = (sem(f"{n}_loaded") for n in ("wqkv", "wo", "w1", "w2", "cols", "qk_scale"))
        s_zero = sem("zeros_set")
        s_xsa = sem("xs_a_ready")
        pf_full = [sem(f"front_bank{i}_full") for i in range(2)]
        pa_full = [sem(f"score_bank{i}_full") for i in range(2)]
        pb_full = [sem(f"back_bank{i}_full") for i in range(2)]
        s_rot = sem("rotation_tables_ready")
        s_raw = sem("raw_ready")
        s_sq = sem("squares_ready")
        s_ssq = sem("ssq_ready")
        s_clamp = sem("ssq_clamped")
        s_guess = sem("rnorm_guess_steps")
        s_rn = sem("rnorm_steps")
        s_rmul = sem("rope_products_ready")
        s_radd = sem("rope_sum_ready")
        s_rope = [sem("rope_ready_by_pool"), sem("rope_ready_by_vector")]
        s_v = sem("v_ready")
        s_qkt = [sem("qk_t_ready_by_scalar"), sem("qk_t_ready_by_vector")]
        s_negm = sem("negm_ready")
        s_negt = sem("negm_t_ready")
        s_probs = sem("probs_ready")
        s_av = sem("values_weighted")
        s_rsum = sem("rsum_ready")
        s_o = sem("o_ready")
        s_ot = sem("o_t_ready")
        s_x1 = sem("x_after_attention_ready")
        s_xc = sem("xc_ready")
        s_xsq = sem("xsq_ready")
        s_var = sem("var_ready")
        s_seed = sem("rstd_seed_steps")
        s_rstd = sem("rstd_steps")
        s_xn = sem("xn_ready")
        s_xg = sem("xg_ready")
        s_gate = sem("gate_ready")
        s_hid = sem("hid_ready")
        s_xt = sem("x_after_attention_kept")
        s_x2 = sem("x_kept")
        s_out = sem("out_written")
        e_load = sem("entry_inputs_loaded")
        e_pe, e_act, e_dve, e_rstd = (sem(f"entry_{n}") for n in ("products", "activations", "vectors", "rstd_steps"))
        f_pe, f_act, f_dve, f_rstd = (sem(f"final_{n}") for n in ("products", "activations", "vectors", "rstd_steps"))

        def at(per_step, s, k):
            if type(s) is tuple:
                layer, b = s
                return layer * (B * per_step) + (b * per_step + k + 1)
            return s * per_step + k + 1

        def plus(s, n):
            if type(s) is tuple:
                layer, b = s
                return (layer + (b + n) // B, (b + n) % B) if (b + n) // B else (layer, b + n)
            return s + n

        def batch(s):
            return s[1] if type(s) is tuple else s % B

        def first(s):
            return type(s) is not tuple and s == 0

        F_USES, A_USES, B_USES = 10, (11, 10), (7, 4)
        OT = [(0, 0), (1, 0), (0, 1), (1, 1)]
        WO_, MEAN, VAR, G01, C2, A01, W2_ = (0, 2), (1, 2), (0, 3), (0, 4), (1, 3), (0, 5), (0, 6)

        def chunk_of(slot):
            return (slot // 4, slot % 4) if slot < 8 else ((slot - 8) // 2, 4 + slot % 2)

        FIRST_TURN = 9

        def chunk_use(slot):
            return slot // 2 if slot < 10 else 6

        def turn_use(n):
            return 5 if n < 2 else 6 + n // 2

        def layer_of(s):
            return s[0] if type(s) is tuple else s // B

        def rsqrt_guess(dve, dst, src, minus_half, done, count):
            tsc = nc.vector.tensor_scalar
            bits = lambda ap: ap.bitcast(mybir.dt.int32)
            tsc(bits(dst), bits(src), 1, None, ALU.logical_shift_right).then_inc(done, 1)
            tsc(minus_half, src, -0.5, None, ALU.mult).then_inc(done, 1)
            dve.wait_ge(done, count(0))
            tsc(bits(dst), bits(dst), -1.0, RSQRT_MAGIC, ALU.mult, ALU.add).then_inc(done, 1)

        def rsqrt(dve, dst, src, scratch, done, count):
            tt = nc.vector.tensor_tensor
            minus_half, tmp = scratch
            rsqrt_guess(dve, dst, src, minus_half, done, count)
            for n in range(3):
                dve.wait_ge(done, count(3 * n + 2))
                tt(tmp, dst, dst, ALU.mult).then_inc(done, 1)
                dve.wait_ge(done, count(3 * n + 3))
                tt(tmp, tmp, minus_half, ALU.mult).then_inc(done, 1)
                dve.wait_ge(done, count(3 * n + 4))
                nc.vector.scalar_tensor_tensor(out=dst, in0=tmp, scalar=1.5, in1=dst, op0=ALU.add,
                                               op1=ALU.mult).then_inc(done, 1)

        raw4 = raw[:, :, :].rearrange("p t (g n) -> p (t g) n", n=T)
        rope4 = rope[:, :, :].rearrange("p t (g n) -> p (t g) n", n=T)
        ropeb4 = rope_b[:, :, :].rearrange("p t (g n) -> p (t g) n", n=T)
        x_all = x_t[:, :, :].rearrange("p b n -> p (b n)")
        xs_all = xs_a[:, :, :]
        q_e, k_e, neg_q, neg_k = (raw4[:, i, :] for i in range(4))
        v_e, masked, att, y = (rope4[:, i, :] for i in range(4))
        yc, ysq, yvar, yrstd = (ropeb4[:, i, :] for i in range(4))
        qkf = qk_t2[:, 0].rearrange("p a c n -> p (a c n)")
        soft = qkf[:, 0:2 * T].rearrange("p (i k) -> p i k", k=N)
        soft_t = qkf[:, 2 * T:4 * T].rearrange("p (b n) -> p b n", n=2 * N)
        w_e = [o[:, 0, i * P:(i + 1) * P] for i in range(8)]
        WQ, WK, WV, WOT, XQ, XK, XV, SAME = range(8)
        vb1, vb2 = o[:, 1, 0:P], o[:, 1, P:2 * P]
        ctx_t = o_t[:, :, :].rearrange("p c n -> p (c n)")[:, 0:T]
        x_nb = o_t[:, :, :].rearrange("p c n -> p (c n)")[:, T:2 * T]
        ecols = sb("ecols", [P, 5])
        emax = sb("emax", [P, 8])
        esum = sb("esum", [P, 8])
        erec = sb("erec", [P, 8])
        half = lambda ap, g: ap[:, g * CH:(g + 1) * CH]
        E_PE = ["q0", "q1", "k0", "k1", "v0", "v1", "s0", "s1", "att0", "att1", "wo0", "wo1", "mean0", "mean1",
                "var0", "var1", "xk0", "xk1", "xv0", "xv1", "xq0", "xq1", "sc0", "sc1", "sc2", "sc3", "tr0", "tr1", "tr2",
                "tr3", "xo0", "xo1", "xo2", "xo3", "mean2", "mean3", "var2", "var3"]
        E_ACT = ["exp0", "exp1", "exp2", "exp3", "att0", "att1", "sq0", "sq1", "soft0", "soft1", "soft2", "soft3",
                 "tr0", "tr1", "tr2", "tr3", "sq2", "sq3"]
        E_DVE = ["neg0", "neg1", "neg2", "neg3", "pos0", "pos1", "pos2", "pos3", "v0", "v1", "q0", "q1", "k0", "k1",
                 "masked0", "masked1", "y0", "y1", "yc0", "yc1", "var0", "var1", "x0", "x1",
                 "xk0", "xk1", "xv0", "xv1", "xq0", "xq1", "max0", "max1", "max2", "max3", "rec", "soft", "y2", "y3",
                 "yc2", "yc3", "var2", "var3", "done"]
        F_PE = ["mean0", "mean1", "var0", "var1"]
        F_ACT = ["sq0", "sq1"]
        F_DVE = ["sum0", "sum1", "yc0", "yc1", "var0", "var1", "y0", "y1"]
        N_ENTRY_LOADS = 25

        def entry_loads(eng):
            for dst, src in ([(x_nb, a["x_nb"]), (ecols[:, :], a["ecols"])]
                             + [(w_e[i][0:h, :], a[n]) for i, (n, h) in enumerate(
                                 (("wq", P), ("wk", P), ("wv", P), ("wot", P), ("xwq", P), ("xwk", DC), ("xwv", DC), ("same", P)))]
                             + [(vb1, a["bv"].broadcast_to([P, P])), (vb2, a["xbv"].broadcast_to([P, P])),
                                (ctx_t[0:DC, :], a["ctx_t"]), (mean_w[:, :], a["mean_w"]), (ident[:, :], a["ident"])]):
                eng.dma_start(dst, src).then_inc(e_load, 16)
            for dst, src in ((identb[:, :], a["identb"]), (mask_q[:, :, :], a["mask_q"]), (shift_k[:, :], a["shift_k"]),
                             (pick[:, :, :], a["pick"]), (rot_base[:, :, :], a["rot_base"])):
                eng.dma_start(dst, src).then_inc(s_const, 16)
        E_LOADS, C_LOADS = 15 * 16, 5 * 16

        def entry_tensor(pe):
            mm = nc.tensor.matmul
            done = lambda ins: ins.then_inc(e_pe, 1)
            act_did = lambda name: pe.wait_ge(e_act, E_ACT.index(name) + 1)
            dve_did = lambda name: pe.wait_ge(e_dve, E_DVE.index(name) + 1)
            pe.wait_ge(e_load, E_LOADS)
            for i, w in enumerate((WQ, WK)):
                for g in range(2):
                    done(mm(ps[2 * i + g][:, :], w_e[w], half(x_nb, g), start=True, stop=True))
            for g in range(2):
                for k in range(4):
                    kk = 4 * g + k
                    last = mm(ps[4 + g][:, k * P:(k + 1) * P], x_nb[:, kk * P:(kk + 1) * P], w_e[WV], start=True, stop=True,
                              skip_group_check=True)
                done(last)
            dve_did("k1")
            for g in range(2):
                for k in range(4):
                    c = slice((4 * g + k) * P, (4 * g + k + 1) * P)
                    last = mm(ps[g][:, k * P:(k + 1) * P], k_e[:, c], q_e[:, c], start=True, stop=True, skip_group_check=True)
                done(last)
            for g in range(2):
                dve_did(f"masked{g}")
                for k in range(4):
                    c = slice((4 * g + k) * P, (4 * g + k + 1) * P)
                    last = mm(ps[2 + g][:, k * P:(k + 1) * P], v_e[:, c], masked[:, c], start=True, stop=True, skip_group_check=True)
                done(last)
            act_did("att1")
            for g in range(2):
                done(mm(ps[4 + g][:, :], w_e[WOT], half(att, g), start=True, stop=True))

            def norm_sums(src, ready, sq_ready, b0, b1):
                for g in range(2):
                    ready(g)
                    done(mm(ps[b0 + g][:, :], mean_w[:, :], half(src, g), start=True, stop=True))
                for g in range(2):
                    sq_ready(g)
                    done(mm(ps[b1 + g][:, :], mean_w[:, :], half(ysq, g), start=True, stop=True))

            norm_sums(y, lambda g: dve_did(f"y{g}"), lambda g: act_did(f"sq{g}"), 6, 0)
            for g in range(2):
                done(mm(ps[4 + g][:, :], w_e[XK][0:DC, :], half(ctx_t, g)[0:DC, :], start=True, stop=True))
            for g in range(2):
                for k in range(4):
                    kk = 4 * g + k
                    last = mm(ps[6 + g][:, k * P:(k + 1) * P], ctx_t[0:DC, kk * P:(kk + 1) * P], w_e[XV][0:DC, :],
                              start=True, stop=True, skip_group_check=True)
                done(last)
            for g in range(2):
                dve_did("x1")
                done(mm(ps[2 + g][:, :], w_e[XQ], half(x_all, g), start=True, stop=True))
            for b in range(B):
                dve_did("xq1")
                for j in range(2):
                    i = 2 * b + j
                    last = mm(ps[b][:, j * N:(j + 1) * N], q_e[:, i * P:(i + 1) * P], k_e[:, b * N:(b + 1) * N],
                              start=True, stop=True, skip_group_check=True)
                done(last)
            dve_did("soft")
            for b in range(B):
                for kt in range(2):
                    for j in range(2):
                        last = nc.tensor.transpose(ps[4 + b][:, kt * N + j * P:kt * N + (j + 1) * P],
                                                   soft[:, 2 * b + j, kt * P:(kt + 1) * P], ident[:, :])
                done(last)
            for b in range(B):
                act_did(f"tr{b}")
                for kt in range(2):
                    i = 2 * b + kt
                    last = mm(ps[b][:, 0:N], v_e[:, i * P:(i + 1) * P], soft_t[:, b, kt * N:(kt + 1) * N],
                              start=(kt == 0), stop=(kt == 1))
                done(last)
            norm_sums(y, lambda g: dve_did(f"y{2 + g}"), lambda g: act_did(f"sq{2 + g}"), 4, 6)

        def entry_scalar(act):
            fn = nc.scalar.activation
            done = lambda ins: ins.then_inc(e_act, 1)
            pe_did = lambda name: act.wait_ge(e_pe, E_PE.index(name) + 1)
            dve_did = lambda name: act.wait_ge(e_dve, E_DVE.index(name) + 1)
            for i in range(4):
                dve_did(f"neg{i}")
                src = half((neg_q, neg_k)[i // 2], i % 2)
                done(fn(src, src, ACT.Exp))
            for g in range(2):
                pe_did(f"att{g}")
                done(nc.scalar.copy(half(att, g), ps[2 + g][:, :]))
            for g in range(2):
                dve_did(f"yc{g}")
                done(fn(half(ysq, g), half(yc, g), ACT.Square))
            for b in range(B):
                dve_did(f"max{b}")
                for j in range(2):
                    i = 2 * b + j
                    last = fn(soft[:, i, :], ps[b][:, j * N:(j + 1) * N], ACT.Exp, bias=emax[:, i:i + 1],
                              accum_out=esum[:, i:i + 1])
                done(last)
            for b in range(B):
                pe_did(f"tr{b}")
                done(nc.scalar.copy(soft_t[:, b, :], ps[4 + b][:, :]))
            for g in range(2):
                dve_did(f"yc{2 + g}")
                done(fn(half(ysq, g), half(yc, g), ACT.Square))

        def entry_vector(dve):
            tt, tsc = nc.vector.tensor_tensor, nc.vector.tensor_scalar
            done = lambda ins: ins.then_inc(e_dve, 1)
            pe_did = lambda name: dve.wait_ge(e_pe, E_PE.index(name) + 1)
            act_did = lambda name: dve.wait_ge(e_act, E_ACT.index(name) + 1)
            dve_did = lambda name: dve.wait_ge(e_dve, E_DVE.index(name) + 1)
            nc.vector.memset(xs_a[64:P, :, 0:1], 0.0)
            nc.vector.memset(xs_f[64:P, 0:1], 0.0)
            dve.wait_ge(e_load, E_LOADS)
            pos = (yc, ysq)
            for i in range(4):
                pe_did(("q0", "q1", "k0", "k1")[i])
                done(tsc(half((neg_q, neg_k)[i // 2], i % 2), ps[i][:, :], ecols[:, i // 2:i // 2 + 1], 0.0, ALU.add, ALU.min))
            for i in range(4):
                done(tsc(half(pos[i // 2], i % 2), ps[i][:, :], ecols[:, i // 2:i // 2 + 1], 0.0, ALU.add, ALU.max))
            for g in range(2):
                pe_did(f"v{g}")
                done(tt(half(v_e, g).rearrange("p (k e) -> p k e", e=P), ps[4 + g][:, :].rearrange("p (k e) -> p k e", e=P),
                        vb1.unsqueeze(1).broadcast_to([P, 4, P]), ALU.add))
            for i in range(4):
                act_did(f"exp{i}")
                if i == 0:
                    dve_did("pos3")
                done(tt(half((q_e, k_e)[i // 2], i % 2), half(pos[i // 2], i % 2), half((neg_q, neg_k)[i // 2], i % 2), ALU.add))
            for g in range(2):
                pe_did(f"s{g}")
                done(tt(half(masked, g).rearrange("p (k e) -> p k e", e=P), ps[g][:, :].rearrange("p (k e) -> p k e", e=P),
                        w_e[SAME].unsqueeze(1).broadcast_to([P, 4, P]), ALU.mult))
            for g in range(2):
                pe_did(f"wo{g}")
                done(nc.vector.scalar_tensor_tensor(out=half(y, g), in0=ps[4 + g][:, :], scalar=ecols[:, 2:3],
                                                    in1=half(x_nb, g), op0=ALU.add, op1=ALU.add))

            def norm(k, b0, b1):
                for g in range(2):
                    pe_did(f"mean{k + g}")
                    if g == 0:
                        dve_did(f"y{k + 1}")
                    done(tt(half(yc, g), half(y, g), ps[b0 + g][:, :], ALU.subtract))
                for g in range(2):
                    pe_did(f"var{k + g}")
                    done(tsc(half(yvar, g), ps[b1 + g][:, :], EPS, None, ALU.add))

            def entry_rsqrt(k):
                dve_did(f"var{k + 1}")
                start = RSQRT_STEPS * (k // 2)
                rsqrt(dve, yrstd, yvar, (y, ysq), e_rstd, lambda i: start + i + 1)
                dve.wait_ge(e_rstd, start + RSQRT_STEPS)

            norm(0, 6, 0)
            entry_rsqrt(0)
            for g in range(2):
                done(tt(x_t[:, :, g * P:(g + 1) * P], half(yc, g).rearrange("p (n b) -> p b n", b=B),
                        half(yrstd, g).rearrange("p (n b) -> p b n", b=B), ALU.mult))
            for g in range(2):
                pe_did(f"xk{g}")
                done(tsc(half(k_e, g), ps[4 + g][:, :], ecols[:, 4:5], None, ALU.add))
            for g in range(2):
                pe_did(f"xv{g}")
                done(tt(half(v_e, g).rearrange("p (k e) -> p k e", e=P), ps[6 + g][:, :].rearrange("p (k e) -> p k e", e=P),
                        vb2.unsqueeze(1).broadcast_to([P, 4, P]), ALU.add))
            for g in range(2):
                pe_did(f"xq{g}")
                done(tsc(half(q_e, g), ps[2 + g][:, :], ecols[:, 3:4], None, ALU.add))
            for b in range(B):
                pe_did(f"sc{b}")
                done(nc.vector.tensor_reduce(emax[:, 2 * b:2 * b + 2], ps[b][:, :].rearrange("p (j k) -> p j k", j=2),
                                             AX.X, ALU.max, negate=True))
            act_did("soft3")
            done(nc.vector.reciprocal(erec[:, :], esum[:, :]))
            dve_did("rec")
            done(tt(soft, soft, erec[:, :].unsqueeze(2).broadcast_to([P, 8, N]), ALU.mult))
            for g in range(2):
                for j in range(2):
                    b = 2 * g + j
                    pe_did(f"xo{b}")
                    last = tt(y[:, b * N:(b + 1) * N], ps[b][:, 0:N], x_t[:, b, :], ALU.add)
                done(last)
            norm(2, 4, 6)
            entry_rsqrt(2)
            for g in range(2):
                bs = slice(2 * g, 2 * g + 2)
                c3 = half(yc, g).rearrange("p (b n) -> p b n", n=N)
                r3 = half(yrstd, g).rearrange("p (b n) -> p b n", n=N)
                tt(half(x_in, g), half(yc, g), half(yrstd, g), ALU.mult)
                last = tt(x_t[:, bs, :], c3, r3, ALU.mult)
                if g == 1:
                    last.then_inc(s_x2, 1)
                tt(xs_a[0:64, bs, :], c3[0:64], r3[0:64], ALU.mult)
                tt(xs_a[64:P, bs, 1:N], c3[64:P, :, 0:N - 1], r3[64:P, :, 0:N - 1], ALU.mult).then_inc(s_xsa, 2)

        def entry_gpsimd(pool):
            nc.gpsimd.memset(three_halves[:, :], 1.5).then_inc(s_zero, 1)
            nc.gpsimd.memset(v[:, :, :, :].rearrange("p a t (h e) -> p (a t h) e", e=VW)[:, :, DH:VW], 1.0).then_inc(s_zero, 1)

        def final_tensor(pe):
            dve_did = lambda name: pe.wait_ge(f_dve, F_DVE.index(name) + 1)
            for g in range(2):
                dve_did(f"sum{g}")
                nc.tensor.matmul(ps[g][:, :], mean_w[:, :], half(y, g), start=True, stop=True).then_inc(f_pe, 1)
            for g in range(2):
                pe.wait_ge(f_act, g + 1)
                nc.tensor.matmul(ps[2 + g][:, :], mean_w[:, :], half(ysq, g), start=True, stop=True).then_inc(f_pe, 1)

        def final_scalar(act):
            for g in range(2):
                act.wait_ge(f_dve, F_DVE.index(f"yc{g}") + 1)
                nc.scalar.activation(half(ysq, g), half(yc, g), ACT.Square).then_inc(f_act, 1)

        def final_vector(dve):
            dve_did = lambda name: dve.wait_ge(f_dve, F_DVE.index(name) + 1)
            dve.wait_ge(s_x2, 1 + DEPTH * B)
            for g in range(2):
                nc.vector.tensor_tensor(half(y, g), half(x_all, g), half(x_in, g), ALU.add).then_inc(f_dve, 1)
            for g in range(2):
                dve.wait_ge(f_pe, g + 1)
                dve_did(f"sum{g}")
                nc.vector.tensor_tensor(half(yc, g), half(y, g), ps[g][:, :], ALU.subtract).then_inc(f_dve, 1)
            for g in range(2):
                dve.wait_ge(f_pe, 3 + g)
                nc.vector.tensor_scalar(half(yvar, g), ps[2 + g][:, :], EPS, None, ALU.add).then_inc(f_dve, 1)
            dve_did("var1")
            rsqrt(dve, yrstd, yvar, (y, ysq), f_rstd, lambda i: i + 1)
            dve.wait_ge(f_rstd, RSQRT_STEPS)
            for g in range(2):
                nc.vector.tensor_tensor(half(y, g), half(yc, g), half(yrstd, g), ALU.mult).then_inc(f_dve, 1)

        def final_store(eng):
            for g in range(2):
                eng.wait_ge(f_dve, F_DVE.index(f"y{g}") + 1)
                eng.dma_start(out[:, g * CH:(g + 1) * CH], half(y, g)).then_inc(s_out, 16)
            eng.wait_ge(s_out, 32)

        block = ctx.enter_context(nc.Block())

        def iteration(s, turn, back_a, scores, back_b, shift, head, back_slot, proj_slot, tail,
                      do_back=True, do_attend=True, do_proj=True):
            if do_attend:
                turn(plus(s, 1), 7)
            if do_back:
                for n in range(4):
                    back_a(s, n)
            if do_attend:
                scores(plus(s, 1))
            if do_back:
                back_b(s)
            if do_attend:
                shift(plus(s, 1))
            for slot in range(HEADS):
                if do_proj:
                    proj_slot(plus(s, 2), slot)
                if do_attend:
                    head(plus(s, 1), slot)
                if do_proj and slot >= FIRST_TURN:
                    turn(plus(s, 2), slot - FIRST_TURN)
                if do_back:
                    back_slot(s, slot)
            if do_attend:
                tail(plus(s, 1))

        def run(fori, turn, back_a, scores, back_b, shift, head, back_slot, proj_slot, tail):
            stages = (turn, back_a, scores, back_b, shift, head, back_slot, proj_slot, tail)
            for slot in range(HEADS):
                proj_slot(0, slot)
                if slot >= FIRST_TURN:
                    turn(0, slot - FIRST_TURN)
            iteration(-1, *stages, do_back=False)
            with fori(0, DEPTH - 1) as layer:
                for b in range(B):
                    iteration((layer, b), *stages)
            for i in range((DEPTH - 1) * B, DEPTH * B):
                iteration(i, *stages, do_attend=i + 1 < DEPTH * B, do_proj=i + 2 < DEPTH * B)

        def normalise(eng, tt, s, n):
            t, c = divmod(n, 4)
            if c < 2:
                eng.wait_ge(s_rn, at(2 * POOL_STEPS, s, POOL_STEPS * (t + 1) - 1))
            eng.wait_ge(s_radd, at(8, s, n))
            ch3 = rope[:, t, c * CH:(c + 1) * CH].rearrange("p (h e) -> p h e", e=DH)
            tt(ch3, ch3, rnorm[:, t, c * HC:(c + 1) * HC].unsqueeze(2).broadcast_to([P, HC, DH]),
               ALU.mult).then_inc(s_rope[n % 2], 1)

        def take_turned(eng, copy, s, n):
            t, c = divmod(n, 4)
            par = n % 2
            qk_t, qk_b = qk_t2[:, batch(s) % 2], qk_b2[:, batch(s) % 2]
            eng.wait_ge(pf_full[par], at(F_USES, s, turn_use(n)))
            src = PF[par][:, :].rearrange("p (j t) -> p j t", j=4)
            j0 = (c % 2) * 4
            copy(qk_b[:, c // 2, j0:j0 + 4, t * P:(t + 1) * P], src)
            copy(qk_t[:, c // 2, j0:j0 + 4, t * P:(t + 1) * P], src).then_inc(s_qkt[par], 1)

        @block.sync
        def _(sp):
            def load(layer, what):
                if what == "wqkv":
                    sp.dma_start(wqkv[:, :], a["wqkv"][layer, :, :]).then_inc(s_wqkv, 16)
                elif what == "qks":
                    sp.dma_start(qk_scale[:, :], a["qk_scale"][layer, :, :].broadcast_to([P, 4 * DH])).then_inc(s_qks, 16)
                elif what == "wo":
                    sp.dma_start(wo[:, :, :], a["wo"][layer, :, :, :].rearrange("c p n -> p c n")).then_inc(s_wo, 16)
                elif what == "w1":
                    sp.dma_start(w1[:, :], a["w1"][layer, :, :]).then_inc(s_w1, 16)
                elif what == "w2":
                    sp.dma_start(w2[:, :, :], a["w2"][layer, :, :, :].rearrange("c p n -> p c n")).then_inc(s_w2, 16)
                elif what == "cols":
                    sp.dma_start(cols[:, :], a["cols"][layer, :, :]).then_inc(s_cols, 16)

            entry_loads(sp)
            for what in ("wqkv", "qks", "wo", "w1", "w2", "cols"):
                load(0, what)
            with sp.Fori(0, DEPTH - 1) as layer:
                last = (layer, B - 1)
                sp.wait_ge(pf_full[1], at(F_USES, last, 6))
                load(layer + 1, "wqkv")
                sp.wait_ge(s_rot, layer + 1)
                load(layer + 1, "qks")
                sp.wait_ge(pb_full[0], at(B_USES[0], last, WO_[1]))
                load(layer + 1, "wo")
                sp.wait_ge(pb_full[0], at(B_USES[0], last, A01[1]))
                load(layer + 1, "w1")
                sp.wait_ge(pb_full[0], at(B_USES[0], last, W2_[1]))
                load(layer + 1, "w2")
                sp.wait_ge(s_x2, at(1, last, 0) + 1)
                load(layer + 1, "cols")
            final_store(sp)

        @block.tensor
        def _(pe):
            mm = nc.tensor.matmul

            def front_bank_read(s, bank, use):
                if use == 0:
                    if not first(s):
                        pe.wait_ge(s_qkt[bank], at(4, s, 3) - 4)
                elif use in (6, 8, 9):
                    pe.wait_ge(s_qkt[bank], at(4, s, max(use - 7, 0)))
                else:
                    before = bank + (10 if use == 7 else 2 * (use - 1))
                    if before < 8:
                        pe.wait_ge(s_sq, at(8, s, before))
                    else:
                        pe.wait_ge(s_v, at(4, s, before - 8))

            def proj_slot(s, slot):
                if slot >= 12:
                    return
                b = batch(s)
                t, c = chunk_of(slot)
                if slot == 0:
                    pe.wait_ge(s_xsa, B if first(s) else at(1, s, 0))
                    if b == 0:
                        pe.wait_ge(s_wqkv, layer_of(s) * 16 + 16)
                bank, use = slot % 2, chunk_use(slot)
                front_bank_read(s, bank, use)
                mm(PF[bank][:, :], xs_a[:, b, t * P:(t + 1) * P], wqkv[:, c * CH:(c + 1) * CH],
                   start=True, stop=True).then_inc(pf_full[bank], 1)

            def turn(s, n):
                t, c = divmod(n, 4)
                bank, use = n % 2, turn_use(n)
                pe.wait_ge(s_rope[n % 2], at(4, s, n // 2))
                front_bank_read(s, bank, use)
                for j in range(4):
                    last = nc.tensor.transpose(PF[bank][:, j * P:(j + 1) * P],
                                               rope[:, t, c * CH + j * P:c * CH + (j + 1) * P], ident[:, :])
                last.then_inc(pf_full[bank], 1)

            def scores(s):
                qk_b = qk_b2[:, batch(s) % 2]
                for by in s_qkt:
                    pe.wait_ge(by, at(4, s, 3))
                for t in range(NT):
                    for par in range(2):
                        if t == 1:
                            pe.wait_ge(s_negm, at(4, s, par))
                        elif not first(s):
                            pe.wait_ge(s_probs, at(HEADS, s, 14 + par) - HEADS)
                        mm(PA[par][:, :], identb[:, :], mask_q[:, t, :], start=True, stop=False, skip_group_check=True)
                        r = 64 * par
                        for hh in range(8):
                            for u in range(4):
                                w = 4 * t + u
                                lo = max(w - 1, 0) * WIN
                                n = (w + 1) * WIN - lo
                                last = mm(PA[par][32 * u:32 * u + 32, hh * 64 + 64 - n:hh * 64 + 64],
                                          qk_b[r:r + 64, 0, hh, w * WIN:(w + 1) * WIN],
                                          qk_b[r:r + 64, 1, hh, lo:lo + n], start=False, stop=(hh == 7 and u == 3),
                                          skip_group_check=True)
                        last.then_inc(pa_full[par], 1)

            def shift(s):
                pe.wait_ge(s_negm, at(4, s, 3))
                for t in range(NT):
                    last = nc.tensor.transpose(negt_ps[0:HEADS, t * P:(t + 1) * P], negm[:, t, :], identb[:, :])
                last.then_inc(pa_full[0], 1)

            def head(s, h):
                par, hh = h % 2, h // 2
                r = 64 * par
                qk_t = qk_t2[:, batch(s) % 2]
                bank = PA[par]
                if h < 2:
                    pe.wait_ge(s_negt, at(1, s, 0))
                else:
                    pe.wait_ge(s_probs, at(HEADS, s, h - 2))
                mm(bank[:, 0:STW], pick[:, h, :], shift_k[:, :], start=True, stop=False, skip_group_check=True)
                mm(bank[:, 0:SPAN], qk_t[r:r + 64, 1, hh, 0:P], qk_t[r:r + 64, 0, hh, 0:SPAN],
                   start=False, stop=False, skip_group_check=True)
                mm(bank[:, SPAN:STW], qk_t[r:r + 64, 1, hh, P:N], qk_t[r:r + 64, 0, hh, P:N],
                   start=False, stop=True, skip_group_check=True).then_inc(pa_full[par], 1)
                if h > 0:
                    weigh(s, h - 1)

            def weigh(s, h):
                g = [i for i, (lo, hi) in enumerate(GROUPS) if lo <= h < hi][0]
                lo, hi = GROUPS[g]
                if h == lo and not (first(s) and g < 2):
                    pe.wait_ge(s_o, at(NG, s, g) - 2)
                if h == 0:
                    pe.wait_ge(s_v, at(4, s, 3))
                pe.wait_ge(s_probs, at(HEADS, s, h))
                vb = v[:, batch(s) % 2, :, h * VW:(h + 1) * VW]
                pr = probs[:, h % 4, :]
                bank = PO[g % 2]
                c0, c1 = (h - lo) * VW, (hi - lo + h - lo) * VW
                mm(bank[:, c0:c0 + VW], pr[:, 0:P], vb[:, 0, :], start=True, stop=True, skip_group_check=True)
                mm(bank[:, c1:c1 + VW], pr[:, SPAN:STW], vb[:, 1, :], start=True, stop=False, skip_group_check=True)
                mm(bank[0:WIN, c1:c1 + VW], pr[:, P:SPAN], vb[:, 0, :], start=False, stop=True,
                   skip_group_check=True).then_inc(s_av, 1)

            def tail(s):
                weigh(s, HEADS - 1)

            def loaded(s, which):
                if batch(s) == 0:
                    pe.wait_ge(which, layer_of(s) * 16 + 16)

            def back_a(s, n):
                if n == 0:
                    pe.wait_ge(s_o, at(NG, s, NG - 1))
                t, half = n // 2, n % 2
                bank = OT[n][0]
                if n >= 2:
                    pe.wait_ge(s_ot, at(4, s, n - 2))
                else:
                    pe.wait_ge(s_x2, at(1, s, 0))
                for j in range(4):
                    c = half * 4 + j
                    last = nc.tensor.transpose(PB[bank][:, j * P:(j + 1) * P], o[:, t, c * P:(c + 1) * P], ident[:, :])
                last.then_inc(pb_full[bank], 1)

            def back_b(s):
                pe.wait_ge(s_ot, at(4, s, 3))
                loaded(s, s_wo)
                for c in range(8):
                    last = mm(PB[0][:, 0:N], wo[:, c, :], o_t[:, c, :], start=(c == 0), stop=(c == 7))
                last.then_inc(pb_full[0], 1)

            def expand(bank, col, c, gate_part):
                m, w0 = FCH[c], gate_part * FF + c * P
                return mm(PB[bank][0:m, col:col + N], w1[:, w0:w0 + m], xg[:, :], start=True, stop=True, skip_group_check=True)

            def back_slot(s, slot):
                if slot == 1:
                    pe.wait_ge(s_x1, at(1, s, 0))
                    mm(PB[1][:, 0:N], mean_w[:, :], xs_f[:, :], start=True, stop=True).then_inc(pb_full[1], 1)
                elif slot == 3:
                    pe.wait_ge(s_xsq, at(1, s, 0))
                    pe.wait_ge(s_xt, at(1, s, 0))
                    mm(PB[0][:, 0:N], mean_w[:, :], xsq[:, :], start=True, stop=True).then_inc(pb_full[0], 1)
                elif slot == 7:
                    pe.wait_ge(s_xg, at(1, s, 0))
                    loaded(s, s_w1)
                    expand(0, 0, 0, 1)
                    expand(0, N, 1, 1).then_inc(pb_full[0], 1)
                elif slot == 8:
                    expand(1, 0, 2, 1)
                    expand(1, N, 2, 0).then_inc(pb_full[1], 1)
                elif slot == 10:
                    pe.wait_ge(s_gate, at(3, s, 1))
                    expand(0, 0, 0, 0)
                    expand(0, N, 1, 0).then_inc(pb_full[0], 1)
                elif slot == 13:
                    pe.wait_ge(s_hid, at(3, s, 2))
                    loaded(s, s_w2)
                    for c in range(3):
                        last = mm(PB[0][:, 0:N], w2[0:FCH[c], c, :], hid[0:FCH[c], c, :], start=(c == 0), stop=(c == 2))
                    last.then_inc(pb_full[0], 1)

            entry_tensor(pe)
            pe.wait_ge(s_const, C_LOADS)
            pe.wait_ge(s_zero, 2)
            run(pe.Fori, turn, back_a, scores, back_b, shift, head, back_slot, proj_slot, tail)
            final_tensor(pe)

        @block.scalar
        def _(act):
            fn = nc.scalar.activation

            def proj_slot(s, slot):
                if slot >= 12:
                    return
                t, c = chunk_of(slot)
                bank, use = slot % 2, chunk_use(slot)
                act.wait_ge(pf_full[bank], at(F_USES, s, use))
                if c < 4:
                    n = t * 4 + c
                    if not first(s):
                        act.wait_ge(s_rmul, at(8, s, n) - 8)
                    nc.scalar.copy(raw[:, t, c * CH:(c + 1) * CH], PF[bank][:, :]).then_inc(s_raw, 1)
                    if not (first(s) and n < 2):
                        act.wait_ge(s_ssq, at(8, s, n) - 2)
                    fn(sq[:, n % 2, :], PF[bank][:, :], ACT.Square).then_inc(s_sq, 1)
                else:
                    h0 = (c - 4) * HC
                    dst = v[:, batch(s) % 2, t, h0 * VW:(h0 + HC) * VW].rearrange("p (h e) -> p h e", e=VW)[:, :, 0:DH]
                    nc.scalar.copy(dst, PF[bank][:, :].rearrange("p (h e) -> p h e", e=DH)).then_inc(s_v, 1)

            def turn(s, n):
                if n % 2 == 0:
                    take_turned(act, nc.scalar.copy, s, n)

            def back_a(s, n):
                t, half = n // 2, n % 2
                bank, use = OT[n]
                act.wait_ge(pb_full[bank], at(B_USES[bank], s, use))
                nc.scalar.copy(o_t[:, half * 4:half * 4 + 4, t * P:(t + 1) * P],
                               PB[bank][:, :].rearrange("p (j t) -> p j t", j=4)).then_inc(s_ot, 1)

            def head(s, h):
                par, hh = h % 2, h // 2
                use = (3 if par == 0 else 2) + hh
                act.wait_ge(pa_full[par], at(A_USES[par], s, use))
                if not (first(s) and h < 4):
                    act.wait_ge(s_av, at(HEADS, s, h) - 4)
                fn(probs[:, h % 4, :], PA[par][:, 0:STW], ACT.Exp).then_inc(s_probs, 1)

            def back_slot(s, slot):
                if slot == 2:
                    act.wait_ge(s_xc, at(1, s, 0))
                    fn(xsq[:, :], xc[:, :], ACT.Square).then_inc(s_xsq, 1)
                elif slot == 4:
                    act.wait_ge(s_var, at(1, s, 0))
                    fn(rstd[:, :], var[:, :], ACT.Ln).then_inc(s_seed, 1)
                    act.wait_ge(s_seed, at(2, s, 0))
                    fn(rstd[:, :], rstd[:, :], ACT.Exp, scale=-0.5).then_inc(s_seed, 1)
                elif slot == 9:
                    if batch(s) == 0:
                        act.wait_ge(s_cols, layer_of(s) * 16 + 16)
                    for c, (where, col) in enumerate(((G01, 0), (G01, N), (C2, 0))):
                        bank, use = where
                        m = FCH[c]
                        if c != 1:
                            act.wait_ge(pb_full[bank], at(B_USES[bank], s, use))
                        fn(gate[0:m, c, :], PB[bank][0:m, col:col + N], ACT.Gelu, bias=cols[0:m, 6 + c:7 + c]).then_inc(s_gate, 1)

            nothing = lambda *_: None
            entry_scalar(act)
            run(act.Fori, turn, back_a, nothing, nothing, nothing, head, back_slot, proj_slot, nothing)
            final_scalar(act)

        @block.vector
        def _(dve):
            tt, tsc = nc.vector.tensor_tensor, nc.vector.tensor_scalar

            def combine(s, n):
                t, c = divmod(n, 4)
                ch = rope[:, t, c * CH:(c + 1) * CH]
                dve.wait_ge(s_rmul, at(8, s, n))
                tt(ch, ch, rope_b[:, t, c * CH:(c + 1) * CH], ALU.add).then_inc(s_radd, 1)

            def proj_slot(s, slot):
                if slot == 0 and batch(s) == 0:
                    dve.wait_ge(s_qks, layer_of(s) * 16 + 16)
                    if not first(s):
                        dve.wait_ge(s_rmul, at(8, s, 0) - 1)
                    tt(rot[:, :, :], rot_base[:, :, :], qk_scale[:, :].unsqueeze(1).broadcast_to([P, NT, 4 * DH]),
                       ALU.mult).then_inc(s_rot, 1)
                if slot < 8:
                    n = slot
                    t, c = divmod(n, 4)
                    dve.wait_ge(s_sq, at(8, s, n))
                    nc.vector.tensor_reduce(ssq[:, t, c * HC:(c + 1) * HC], sq[:, n % 2, :].rearrange("p (h e) -> p h e", e=DH),
                                            AX.X, ALU.add).then_inc(s_ssq, 1)
                    if c == 3:
                        dve.wait_ge(s_ssq, at(8, s, n))
                        if not first(s):
                            dve.wait_ge(s_rn, at(2 * POOL_STEPS, s, POOL_STEPS * t) - 2 * POOL_STEPS + POOL_STEPS - 1)
                        tsc(ssq_c[:, t, :], ssq[:, t, :], 1e-24, None, ALU.max).then_inc(s_clamp, 1)
                        dve.wait_ge(s_clamp, at(2, s, t))
                        rsqrt_guess(dve, rn_guess[:, t, :], ssq_c[:, t, :], minus_half_ssq[:, t, :], s_guess,
                                    lambda i: at(2 * 3, s, 3 * t + i))
                if 3 <= slot < 11:
                    combine(s, slot - 3)
                if slot in (7, 9, 11, 13):
                    normalise(dve, tt, s, slot - 6)

            def turn(s, n):
                if n % 2 == 1:
                    take_turned(dve, nc.vector.tensor_copy, s, n)

            def scores(s):
                for t in range(NT):
                    for par in range(2):
                        dve.wait_ge(pa_full[par], at(A_USES[par], s, t))
                        nc.vector.tensor_reduce(negm[:, t, :].rearrange("p (h two) -> p two h", two=2)[:, par, :],
                                                PA[par][:, :].rearrange("p (h k) -> p h k", h=8), AX.X, ALU.max,
                                                negate=True).then_inc(s_negm, 1)

            def shift(s):
                dve.wait_ge(pa_full[0], at(A_USES[0], s, 2))
                nc.vector.tensor_copy(shift_k[0:HEADS, 0:SPAN], negt_ps[0:HEADS, 0:SPAN])
                nc.vector.tensor_copy(shift_k[0:HEADS, SPAN:STW], negt_ps[0:HEADS, P:N]).then_inc(s_negt, 1)

            def evacuate(s, g):
                lo, hi = GROUPS[g]
                n = hi - lo
                dve.wait_ge(s_av, at(HEADS, s, hi - 1))
                src = PO[g % 2][:, 0:NT * n * VW].rearrange("p (t h e) -> p t h e", t=NT, e=VW)
                nc.vector.reciprocal(rsum[:, :, lo:hi], src[:, :, :, DH]).then_inc(s_rsum, 1)
                dve.wait_ge(s_rsum, at(NG, s, g))
                tt(o[:, :, lo * DH:hi * DH].rearrange("p t (h e) -> p t h e", e=DH), src[:, :, :, 0:DH],
                   rsum[:, :, lo:hi].unsqueeze(3).broadcast_to([P, NT, n, DH]), ALU.mult).then_inc(s_o, 1)

            def head(s, h):
                for g, (lo, hi) in enumerate(GROUPS[:-1]):
                    if h == hi + 1:
                        evacuate(s, g)

            def tail(s):
                evacuate(s, NG - 1)

            def shifted(dst, bank, b, op):
                op(dst[0:64, :], bank[0:64, 0:N], x_t[0:64, b, :])
                return op(dst[64:P, 1:N], bank[64:P, 0:N - 1], x_t[64:P, b, 0:N - 1])

            def back_b(s):
                b = batch(s)
                dve.wait_ge(pb_full[0], at(B_USES[0], s, WO_[1]))
                shifted(xs_f, PB[0], b, lambda d, p, x: tt(d, p, x, ALU.add)).then_inc(s_x1, 1)

            def back_slot(s, slot):
                b = batch(s)
                if slot == 0:
                    dve.wait_ge(s_x1, at(1, s, 0))
                    tt(x_t[:, b, :], PB[0][:, 0:N], x_t[:, b, :], ALU.add).then_inc(s_xt, 1)
                if slot == 1:
                    dve.wait_ge(pb_full[1], at(B_USES[1], s, MEAN[1]))
                    tt(xc[:, :], xs_f[:, :], PB[1][:, 0:N], ALU.subtract).then_inc(s_xc, 1)
                elif slot == 3:
                    dve.wait_ge(pb_full[0], at(B_USES[0], s, VAR[1]))
                    tsc(var[:, :], PB[0][:, 0:N], EPS, None, ALU.add).then_inc(s_var, 1)
                elif slot == 5:
                    newton = lambda k: at(3, s, k)
                    dve.wait_ge(s_seed, at(2, s, 1))
                    tt(rstd_tmp[:, :], rstd[:, :], rstd[:, :], ALU.mult).then_inc(s_rstd, 1)
                    dve.wait_ge(s_rstd, newton(0))
                    nc.vector.scalar_tensor_tensor(out=rstd_tmp[:, :], in0=var[:, :], scalar=-0.5, in1=rstd_tmp[:, :],
                                                   op0=ALU.mult, op1=ALU.mult).then_inc(s_rstd, 1)
                    dve.wait_ge(s_rstd, newton(1))
                    nc.vector.scalar_tensor_tensor(out=rstd[:, :], in0=rstd_tmp[:, :], scalar=1.5, in1=rstd[:, :],
                                                   op0=ALU.add, op1=ALU.mult).then_inc(s_rstd, 1)
                    dve.wait_ge(s_rstd, newton(2))
                    tt(xn[:, :], xc[:, :], rstd[:, :], ALU.mult).then_inc(s_xn, 1)
                    dve.wait_ge(s_xn, at(1, s, 0))
                    if b == 0:
                        dve.wait_ge(s_cols, layer_of(s) * 16 + 16)
                    tsc(xg[:, :], xn[:, :], cols[:, 0:1], cols[:, 1:2], ALU.mult, ALU.add).then_inc(s_xg, 1)
                elif slot in (10, 11):
                    for c, where, col, event in (((2, C2, N, 0),) if slot == 10 else ((0, A01, 0, 1), (1, A01, N, 2))):
                        bank, use = where
                        m = FCH[c]
                        dve.wait_ge(s_gate, at(3, s, c))
                        if col != N or c == 2:
                            dve.wait_ge(pb_full[bank], at(B_USES[bank], s, use))
                        nc.vector.scalar_tensor_tensor(out=hid[0:m, c, :], in0=PB[bank][0:m, col:col + N],
                                                       scalar=cols[0:m, 3 + c:4 + c], in1=gate[0:m, c, :],
                                                       op0=ALU.add, op1=ALU.mult).then_inc(s_hid, 1)
                elif slot == 13:
                    dve.wait_ge(pb_full[0], at(B_USES[0], s, W2_[1]))
                    add = lambda d, p, x, bias: nc.vector.scalar_tensor_tensor(out=d, in0=p, scalar=bias, in1=x,
                                                                              op0=ALU.add, op1=ALU.add)
                    add(xs_a[0:64, b, :], PB[0][0:64, 0:N], x_t[0:64, b, :], cols[0:64, 2:3])
                    add(xs_a[64:P, b, 1:N], PB[0][64:P, 0:N - 1], x_t[64:P, b, 0:N - 1], cols[64:P, 2:3]).then_inc(s_xsa, 1)
                    dve.wait_ge(s_xsa, at(1, plus(s, B), 0))
                    add(x_t[:, b, :], PB[0][:, 0:N], x_t[:, b, :], cols[:, 2:3]).then_inc(s_x2, 1)

            nothing = lambda *_: None
            entry_vector(dve)
            dve.wait_ge(s_const, C_LOADS)
            run(dve.Fori, turn, nothing, scores, back_b, shift, head, back_slot, proj_slot, tail)
            final_vector(dve)

        @block.gpsimd
        def _(pool):
            tt = nc.gpsimd.tensor_tensor

            def products(s, t, c):
                n = t * 4 + c
                kind = c // 2
                if n == 0 and batch(s) == 0:
                    pool.wait_ge(s_rot, layer_of(s) + 1)
                pool.wait_ge(s_raw, at(8, s, n))
                if not first(s):
                    pool.wait_ge(pf_full[n % 2], at(F_USES, s, turn_use(n)) - F_USES)
                ch = slice(c * CH, (c + 1) * CH)
                x3 = raw[:, t, ch].rearrange("p (h e) -> p h e", e=DH)
                a3 = rope[:, t, ch].rearrange("p (h e) -> p h e", e=DH)
                b3 = rope_b[:, t, ch].rearrange("p (h e) -> p h e", e=DH)
                ta = rot[:, t, kind * 2 * DH:kind * 2 * DH + DH].unsqueeze(1)
                tb = rot[:, t, kind * 2 * DH + DH:(kind + 1) * 2 * DH].unsqueeze(1)
                hf = DH // 2
                tt(a3, x3, ta.broadcast_to([P, HC, DH]), ALU.mult)
                tt(b3[:, :, 0:hf], x3[:, :, hf:DH], tb[:, :, 0:hf].broadcast_to([P, HC, hf]), ALU.mult)
                tt(b3[:, :, hf:DH], x3[:, :, 0:hf], tb[:, :, hf:DH].broadcast_to([P, HC, hf]), ALU.mult).then_inc(s_rmul, 1)

            def newton(s, t):
                count = lambda k: at(2 * POOL_STEPS, s, POOL_STEPS * t + k)
                y, mh, tmp = rnorm[:, t, :], minus_half_ssq[:, t, :], rn_tmp[:, :]
                pool.wait_ge(s_guess, at(6, s, 3 * t + 2))
                for n in range(3):
                    src = y
                    if n == 0:
                        src = rn_guess[:, t, :]
                    else:
                        pool.wait_ge(s_rn, count(4 * n - 1))
                    tt(tmp, src, src, ALU.mult).then_inc(s_rn, 1)
                    pool.wait_ge(s_rn, count(4 * n))
                    tt(tmp, tmp, mh, ALU.mult).then_inc(s_rn, 1)
                    pool.wait_ge(s_rn, count(4 * n + 1))
                    tt(tmp, tmp, three_halves[:, :], ALU.add).then_inc(s_rn, 1)
                    pool.wait_ge(s_rn, count(4 * n + 2))
                    tt(y, src, tmp, ALU.mult).then_inc(s_rn, 1)

            def proj_slot(s, slot):
                if slot in (5, 9):
                    newton(s, slot // 8)
                if 1 <= slot < 9:
                    products(s, *divmod(slot - 1, 4))
                if slot in (6, 8, 10, 12):
                    normalise(pool, tt, s, slot - 6)

            nothing = lambda *_: None
            entry_gpsimd(pool)
            pool.wait_ge(s_zero, 2)
            run(pool.Fori, nothing, nothing, nothing, nothing, nothing, nothing, nothing, proj_slot,
                nothing)


def tables():
    half = np.arange(0, DH, 2, dtype=np.float32)
    inv_freq = np.float32(1.0) / np.float32(10000.0) ** (half / np.float32(DH))
    t = np.arange(N, dtype=np.float32)
    freqs = (t[:, None] * inv_freq[None, :]).astype(np.float32)
    base = ((half + np.float32(0.4 * DH)) / np.float32(1.4 * DH)).astype(np.float32)
    power = ((t - N // 2) / (WIN // 2)).astype(np.float32)
    scale = (base[None, :].astype(np.float64) ** power[:, None].astype(np.float64))
    cos, sin = np.cos(freqs.astype(np.float64)), np.sin(freqs.astype(np.float64))
    two = lambda lo, hi: np.concatenate([lo, hi], -1)
    rows = np.stack([two(cos * scale, cos * scale) * 8.0, two(-sin * scale, sin * scale) * 8.0,
                     two(cos / scale, cos / scale), two(-sin / scale, sin / scale)], 1)
    rot_base = rows.reshape(NT, P, 4 * DH).transpose(1, 0, 2).astype(np.float32)
    bf = mybir.dt.np(BF16)
    i, rel = np.arange(WIN)[:, None], np.arange(2 * WIN)[None, :] - WIN
    win = np.where((i < rel) | (i > rel + WIN), BIG, 0.0)
    later = np.tile(win, (4, 1))
    start = later.copy()
    start[0:WIN, 0:WIN] = BIG
    mask_q = np.stack([np.tile(start, (1, 8)), np.tile(later, (1, 8))], 1).astype(bf)
    j, q = np.arange(P), np.arange(SPAN)
    left, right = np.zeros((P, P)), np.zeros((P, SPAN))
    for par in range(2):
        for r in range(WIN):
            own = j // WIN % 2 == par
            left[32 + par * WIN + r] = np.where(own, j % WIN > r, j % WIN < r)
            right[32 + par * WIN + r] = (q // WIN % 2 == par) & (q % WIN == r)
    for w in range(P // WIN):
        left[96 + w] = j // WIN == w
        right[96 + w] = (q // WIN != w) & (q // WIN != w + 1)
    shift_k = (np.concatenate([right, right[:, 0:P]], 1) * BIG).astype(bf)
    pick = np.repeat(left[:, None, :], HEADS, 1).astype(bf)
    for h in range(HEADS):
        pick[h, h, :] = 1
    pos = np.arange(P) // B
    return {
        "rot_base": rot_base, "mask_q": mask_q, "shift_k": shift_k, "pick": pick,
        "ident": np.eye(P, dtype=np.float32), "identb": np.eye(P).astype(bf),
        "mean_w": np.full((P, P), 1.0 / P, np.float32),
        "same": (pos[:, None] == pos[None, :]).astype(np.float32),
    }


def kernel(**inputs):
    import concourse.bacc as bacc
    from concourse.bass_utils import run_bass_kernel_spmd

    f = {n: np.asarray(x) for n, x in inputs.items()}
    row = lambda x: np.ascontiguousarray(x.reshape(1, -1))
    A, X, L = "L0_attn_", "L0_xattn_", "L0_ffn_"
    hf = DH // 2
    swap = lambda x: np.concatenate([x[:, hf:], x[:, :hf]], 1)
    qs, ks = f[L + "q_scale"], f[L + "k_scale"]
    wqkv = f[L + "Wqkv"]
    w2 = np.zeros((DEPTH, 3, P, D), np.float32)
    w2.reshape(DEPTH, 3 * P, D)[:, :FF] = f[L + "W2"]
    b1 = np.zeros((DEPTH, 2, 3 * P), np.float32)
    b1[:, :, :FF] = f[L + "b1"].reshape(DEPTH, 2, FF)
    cols = np.concatenate([f[L + "ln_g"][:, None], f[L + "ln_b"][:, None], f[L + "b2"][:, None], b1.reshape(DEPTH, 6, P)], 1)
    arrays = {
        "x_nb": f["x"].transpose(2, 1, 0).reshape(D, T), "ctx_t": f["ctx_768"].reshape(T, DC).T,
        "wq": f[A + "Wq"].T, "wk": f[A + "Wk"].T, "wv": f[A + "Wv"].T, "wot": f[A + "Wo"].T,
        "xwq": f[X + "Wq"], "xwk": f[X + "Wk"], "xwv": f[X + "Wv"],
        "bv": row(f[A + "bv"]), "xbv": row(f[X + "bv"]),
        "ecols": np.stack([f[A + "bq"], f[A + "bk"], f[A + "bo"], f[X + "bq"], f[X + "bk"]], 1),
        "wqkv": wqkv, "wo": f[L + "Wo"].reshape(DEPTH, 8, P, D), "w1": f[L + "W1"], "w2": w2,
        "cols": cols.transpose(0, 2, 1),
        "qk_scale": np.stack([qs, swap(qs), ks, swap(ks)], 1).reshape(DEPTH, 1, 4 * DH),
        **tables(),
    }
    nc = bacc.Bacc("TRN2", target_bir_lowering=False, num_devices=1)
    data, aps = {}, {}
    for name, x in arrays.items():
        x = np.ascontiguousarray(x)
        data[f"in_{name}"] = x
        aps[name] = nc.dram_tensor(f"in_{name}", x.shape, mybir.dt.from_np(x.dtype), kind="ExternalInput").ap()
    out = nc.dram_tensor("out_t", (D, T), F32, kind="ExternalOutput").ap()
    build(nc, aps, out)
    r = run_bass_kernel_spmd(nc, [data], core_ids=[0])
    return np.ascontiguousarray(r.results[0]["out_t"].T).reshape(B, N, D)
```

```python
import numpy as np
import concourse.bass as bass
from concourse import mybir
from contextlib import ExitStack

F32 = mybir.dt.float32
BF16 = mybir.dt.bfloat16
ALU = mybir.AluOpType
ACT = mybir.ActivationFunctionType
AX = mybir.AxisListType

P = 128
B, N, D = 4, 256, 128
T = B * N
DC = 96
DEPTH, HEADS, DH, WIN = 6, 16, 64, 32
INNER = HEADS * DH
QKV = 3 * INNER
FF = int(D * 4 * 2 / 3)
FCH = [128, 128, FF - 256]
NT = N // P
CH = 512
HC = CH // DH
SPAN = P + WIN
STW = SPAN + P
GROUPS = [(0, 3), (3, 6), (6, 9), (9, 12), (12, 14), (14, 16)]
NG = len(GROUPS)
VW = DH + 1
NCOL = 8
EPS = 1e-5
RSQRT_STEPS = 12
RSQRT_MAGIC = float(0x5F3759DF)
BIG = -1.0e30


def build(nc, a, out):
    ctx = ExitStack()
    with ctx:
        ctx.enter_context(nc.allow_low_precision(reason="operands split in two bf16 parts; shift of the softmax rounded alike in numerator and sum"))

        def sb(name, shape, dt=F32):
            return ctx.enter_context(nc.sbuf_tensor(name, shape, dt))

        def sem(name):
            return ctx.enter_context(nc.semaphore(name))

        wqkv = sb("wqkv", [P, QKV])
        wo = sb("wo", [P, 8, D])
        w1 = sb("w1", [P, 2 * FF])
        w2 = sb("w2", [P, 3, D])
        wqkv_s = sb("wqkv_s", [P, 2, QKV], BF16)
        wo_s = sb("wo_s", [P, 2, 8, D], BF16)
        w1_s = sb("w1_s", [P, 2, 2 * FF], BF16)
        w2_s = sb("w2_s", [P, 2, 3, D], BF16)
        cols = sb("cols", [P, NCOL])
        b2 = sb("b2", [P, 1])
        qk_scale = sb("qk_scale", [P, 4 * DH])
        ident = sb("ident", [P, P])
        identb = sb("identb", [P, P], BF16)
        mean_w = sb("mean_w", [P, P])
        rot_base = sb("rot_base", [P, NT, 4 * DH])
        rot = sb("rot", [P, NT, 4 * DH])
        mask_q = sb("mask_q", [P, 2, CH], BF16)
        pick = sb("pick", [P, HEADS, P], BF16)
        x_t = sb("x_t", [P, B, N])
        x_in = sb("x_in", [P, T])
        xs_a = sb("xs_a", [P, B, N])
        xs_s = sb("xs_s", [P, 2, B, N], BF16)
        xs_f = sb("xs_f", [P, N])
        raw = sb("raw", [P, 2 * INNER])
        sq = sb("sq", [P, 2, CH])
        rope = sb("rope", [P, NT, 2 * INNER])
        rope_b = sb("rope_b", [P, 2 * INNER])
        ssq = sb("ssq", [P, NT, 2 * HEADS])
        rn_tmp = sb("rn_tmp", [P, NT, 2 * HEADS])
        minus_half_ssq = sb("minus_half_ssq", [P, NT, 2 * HEADS])
        ssq_c = sb("ssq_c", [P, NT, 2 * HEADS])
        rnorm = sb("rnorm", [P, NT, 2 * HEADS])
        v = sb("v", [P, 2, NT, HEADS * VW])
        qk_t2 = sb("qk_t", [P, 2, 2, 8, N])
        qk_b2 = sb("qk_b", [P, 2, 2, 8, N], BF16)
        negm = sb("negm", [P, NT, HEADS], BF16)
        shift_k = sb("shift_k", [P, STW], BF16)
        probs = sb("probs", [P, 4, STW])
        rsum = sb("rsum", [P, NT, HEADS])
        o = sb("o", [P, NT, INNER])
        o_t = sb("o_t", [P, 2, 8, N], BF16)
        xc = sb("xc", [P, N])
        xsq = sb("xsq", [P, N])
        var = sb("var", [P, NT])
        rstd = sb("rstd", [P, NT])
        minus_half_var = sb("minus_half_var", [P, NT])
        rstd_tmp = sb("rstd_tmp", [P, NT])
        xg_s = sb("xg_s", [P, 2, N], BF16)
        gate = sb("gate", [P, 3, N])
        value = sb("value", [P, 3, N])
        warm = sb("warm", [P, 1])
        hid_s = sb("hid_s", [P, 2, 3, N], BF16)

        ps = [ctx.enter_context(nc.psum_tensor(f"ps{i}", [P, 512], F32)) for i in range(8)]
        PF = ps[0:2]
        PA = ps[2:4]
        PO = ps[4:6]
        PB = ps[6:8]
        negt_ps = PA[0][:, :].bitcast(BF16)

        s_const = sem("constants_loaded")
        s_wqkv, s_wo, s_w1, s_w2, s_cols, s_b2, s_qks = (sem(f"{n}_loaded") for n in
                                                         ("wqkv", "wo", "w1", "w2", "cols", "b2", "qk_scale"))
        s_zero = sem("zeros_set")
        s_xsa = sem("xs_a_ready")
        pf_full = [sem(f"front_bank{i}_full") for i in range(2)]
        pa_full = [sem(f"score_bank{i}_full") for i in range(2)]
        pb_full = [sem(f"back_bank{i}_full") for i in range(2)]
        s_rot = sem("rotation_tables_ready")
        s_raw = sem("raw_ready")
        s_sq = sem("squares_ready")
        s_ssq = sem("ssq_ready")
        s_clamp = sem("ssq_clamped")
        s_rn = sem("rnorm_steps")
        s_rmul = sem("rope_products_ready")
        s_radd = sem("rope_sum_ready")
        s_rope = sem("rope_ready")
        s_v = sem("v_ready")
        s_qkb = [sem("qk_b_ready_by_scalar"), sem("qk_b_ready_by_vector")]
        s_qkt = sem("qk_t_ready")
        s_negm = sem("negm_ready")
        s_negt = sem("negm_t_ready")
        s_probs = sem("probs_ready")
        s_av = sem("values_weighted")
        s_rsum = sem("rsum_ready")
        s_o = sem("o_ready")
        s_oth = sem("o_t_high_ready")
        s_ot = sem("o_t_ready")
        s_wh = {n: sem(f"{n}_high_ready") for n in ("wqkv", "wo", "w1", "w2")}
        s_ws = {n: sem(f"{n}_split") for n in ("wqkv", "wo", "w1", "w2")}
        s_xsh = sem("xs_high_ready")
        s_xss = sem("xs_split")
        s_xgs = sem("xg_split_steps")
        s_hidh = sem("hid_high_ready")
        s_hids = sem("hid_split")
        s_x1 = sem("x_after_attention_ready")
        s_xc = sem("xc_ready")
        s_xsq = sem("xsq_ready")
        s_var = sem("var_ready")
        s_rstd = sem("rstd_steps")
        s_xn = sem("xn_ready")
        s_xg = sem("xg_ready")
        s_gate = sem("gate_ready")
        s_value = sem("value_ready")
        s_gelu = sem("gelu_ready")
        s_ffo = sem("feed_forward_output_ready")
        s_hid = sem("hid_ready")
        s_xt = sem("x_after_attention_kept")
        s_x2 = sem("x_kept")
        s_out = sem("out_written")
        e_first = sem("first_entry_inputs_loaded")
        e_load = sem("entry_inputs_loaded")
        e_pe, e_act, e_dve, e_rstd = (sem(f"entry_{n}") for n in ("products", "activations", "vectors", "rstd_steps"))
        f_pe, f_act, f_dve, f_rstd = (sem(f"final_{n}") for n in ("products", "activations", "vectors", "rstd_steps"))

        def at(per_step, s, k):
            if type(s) is tuple:
                layer, b = s
                return layer * (B * per_step) + (b * per_step + k + 1)
            return s * per_step + k + 1

        def plus(s, n):
            if type(s) is tuple:
                layer, b = s
                return (layer + (b + n) // B, (b + n) % B) if (b + n) // B else (layer, b + n)
            return s + n

        def batch(s):
            return s[1] if type(s) is tuple else s % B

        def first(s):
            return type(s) is not tuple and s == 0

        def last_step(s):
            return type(s) is not tuple and s == DEPTH * B - 1

        F_USES, A_USES, B_USES = 10, (11, 10), (5, 6)
        OT = [(0, 0), (1, 0), (0, 1), (1, 1)]
        WO_, MEAN, VAR, RSTD, G01, C2, A01 = (0, 2), (1, 2), (0, 3), (1, 3), (1, 4), (0, 4), (1, 5)

        def chunk_of(slot):
            return (slot // 4, slot % 4) if slot < 8 else ((slot - 8) // 2, 4 + slot % 2)

        ROPE_SLOTS = (4, 5, 7, 8, 10, 11, 13, 14)
        FIRST_TURN = 9

        def chunk_use(slot):
            return slot // 2 if slot < 10 else 6

        def turn_use(n):
            return 5 if n < 2 else 6 + n // 2

        def last_layer(s):
            return type(s) is not tuple and s >= (DEPTH - 1) * B

        def has_next(s):
            return type(s) is tuple or layer_of(s) + 1 < DEPTH

        def layer_of(s):
            return s[0] if type(s) is tuple else s // B

        def rsqrt(dve, *jobs):
            tt, tsc, stt = nc.vector.tensor_tensor, nc.vector.tensor_scalar, nc.vector.scalar_tensor_tensor
            bits = lambda ap: ap.bitcast(mybir.dt.int32)
            for dst, src, (minus_half, tmp), done, count in jobs:
                tsc(bits(dst), bits(src), 1, None, ALU.logical_shift_right).then_inc(done, 1)
                tsc(minus_half, src, -0.5, None, ALU.mult).then_inc(done, 1)
            for dst, src, (minus_half, tmp), done, count in jobs:
                dve.wait_ge(done, count(0))
                tsc(bits(dst), bits(dst), -1.0, RSQRT_MAGIC, ALU.mult, ALU.add).then_inc(done, 1)
            for n in range(3):
                for dst, src, (minus_half, tmp), done, count in jobs:
                    dve.wait_ge(done, count(3 * n + 2))
                    tt(tmp, dst, dst, ALU.mult).then_inc(done, 1)
                for dst, src, (minus_half, tmp), done, count in jobs:
                    dve.wait_ge(done, count(3 * n + 3))
                    tt(tmp, tmp, minus_half, ALU.mult).then_inc(done, 1)
                for dst, src, (minus_half, tmp), done, count in jobs:
                    dve.wait_ge(done, count(3 * n + 4))
                    stt(out=dst, in0=tmp, scalar=1.5, in1=dst, op0=ALU.add, op1=ALU.mult).then_inc(done, 1)

        qk4 = qk_t2[:, 1].rearrange("p a c n -> p (a c n)").rearrange("p (g n) -> p g n", n=T)
        rope4 = rope[:, :, :].rearrange("p t (g n) -> p (t g) n", n=T)
        x_all = x_t[:, :, :].rearrange("p b n -> p (b n)")
        q_e, k_e, neg_q, neg_k = (qk4[:, i, :] for i in range(4))
        v_e, masked, att, y = (rope4[:, i, :] for i in range(4))
        pos_q, pos_k, ysq, yc = raw[:, 0:T], raw[:, T:2 * T], rope_b[:, 0:T], rope_b[:, T:2 * T]
        qkf = qk_t2[:, 0].rearrange("p a c n -> p (a c n)")
        soft = qkf[:, 0:2 * T].rearrange("p (i k) -> p i k", k=N)
        soft_t = qkf[:, 2 * T:4 * T].rearrange("p (b n) -> p b n", n=2 * N)
        w_e = [o[:, 0, i * P:(i + 1) * P] for i in range(8)]
        WQ, WK, WV, WOT, XQ, XK, XV, SAME = range(8)
        vb1, vb2 = o[:, 1, 0:P], o[:, 1, P:2 * P]
        ctx_t = o_t[:, :, :, :].rearrange("p s c n -> p (s c n)").bitcast(F32)[:, 0:T]
        x_nb = o_t[:, :, :, :].rearrange("p s c n -> p (s c n)").bitcast(F32)[:, T:2 * T]
        ecols = sb("ecols", [P, 5])
        emax = sb("emax", [P, 8])
        esum = sb("esum", [P, 8])
        erec = sb("erec", [P, 8])
        evar, erstd, minus_half_evar, erstd_tmp = (sb(n, [P, 8]) for n in ("evar", "erstd", "minus_half_evar", "erstd_tmp"))
        half = lambda ap, g: ap[:, g * CH:(g + 1) * CH]
        E_PE = ["q0", "q1", "k0", "k1", "v0", "v1", "s0", "s1", "att0", "att1", "wo0", "wo1", "mean0", "mean1",
                "var0", "xk0", "xk1", "xv0", "xv1", "rstd0", "rstd1", "xq0", "xq1", "sc0", "sc1", "sc2", "sc3", "tr0", "tr1", "tr2",
                "tr3", "xo0", "xo1", "xo2", "xo3", "mean2", "mean3", "var2", "rstd2", "rstd3"]
        E_ACT = ["exp0", "exp1", "exp2", "exp3", "att0", "att1", "sq0", "sq1", "soft0", "soft1", "soft2", "soft3",
                 "tr0", "tr1", "tr2", "tr3", "sq2", "sq3"]
        E_DVE = ["neg0", "neg1", "neg2", "neg3", "pos0", "pos1", "pos2", "pos3", "v0", "v1", "q0", "q1", "k0", "k1",
                 "masked0", "masked1", "y0", "y1", "yc0", "yc1", "var0", "x0", "x1",
                 "xk0", "xk1", "xv0", "xv1", "xq0", "xq1", "max0", "max1", "max2", "max3", "rec", "soft", "y2", "y3",
                 "yc2", "yc3", "var2"]
        F_PE, F_DVE = ["mean", "var", "rstd"], ["sum", "yc", "var", "y"]

        def entry_loads(eng):
            weights = [(w_e[i][0:h, :], a[n]) for i, (n, h) in enumerate(
                (("wq", P), ("wk", P), ("wv", P), ("wot", P), ("xwq", P), ("xwk", DC), ("xwv", DC), ("same", P)))]
            for dst, src in [(x_nb, a["x_nb"]), *weights[:2], (ecols[:, :], a["ecols"])]:
                eng.dma_start(dst, src).then_inc(e_first, 16)
            for dst, src in [*weights[2:], (vb1, a["bv"].broadcast_to([P, P])), (vb2, a["xbv"].broadcast_to([P, P])),
                             (ctx_t[0:DC, :], a["ctx_t"]), (mean_w[:, :], a["mean_w"]), (ident[:, :], a["ident"])]:
                eng.dma_start(dst, src).then_inc(e_load, 16)
            for dst, src in ((identb[:, :], a["identb"]), (mask_q[:, :, :], a["mask_q"]), (shift_k[:, :], a["shift_k"]),
                             (pick[:, :, :], a["pick"]), (rot_base[:, :, :], a["rot_base"])):
                eng.dma_start(dst, src).then_inc(s_const, 16)
        E_FIRST, E_LOADS, C_LOADS = 4 * 16, 11 * 16, 5 * 16

        def entry_tensor(pe):
            mm = nc.tensor.matmul
            done = lambda ins: ins.then_inc(e_pe, 1)
            act_did = lambda name: pe.wait_ge(e_act, E_ACT.index(name) + 1)
            dve_did = lambda name: pe.wait_ge(e_dve, E_DVE.index(name) + 1)
            pe.wait_ge(e_first, E_FIRST)
            for i, w in enumerate((WQ, WK)):
                for g in range(2):
                    done(mm(ps[2 * i + g][:, :], w_e[w], half(x_nb, g), start=True, stop=True))
            pe.wait_ge(e_load, E_LOADS)
            for g in range(2):
                for k in range(4):
                    kk = 4 * g + k
                    last = mm(ps[4 + g][:, k * P:(k + 1) * P], x_nb[:, kk * P:(kk + 1) * P], w_e[WV], start=True, stop=True,
                              skip_group_check=True)
                done(last)
            dve_did("k1")
            for g in range(2):
                for k in range(4):
                    c = slice((4 * g + k) * P, (4 * g + k + 1) * P)
                    last = mm(ps[g][:, k * P:(k + 1) * P], k_e[:, c], q_e[:, c], start=True, stop=True, skip_group_check=True)
                done(last)
            for g in range(2):
                dve_did(f"masked{g}")
                for k in range(4):
                    c = slice((4 * g + k) * P, (4 * g + k + 1) * P)
                    last = mm(ps[2 + g][:, k * P:(k + 1) * P], v_e[:, c], masked[:, c], start=True, stop=True, skip_group_check=True)
                done(last)
            act_did("att1")
            for g in range(2):
                done(mm(ps[4 + g][:, :], w_e[WOT], half(att, g), start=True, stop=True))

            def norm_sums(src, ready, sq_ready, b0, b1):
                for g in range(2):
                    ready(g)
                    done(mm(ps[b0 + g][:, :], mean_w[:, :], half(src, g), start=True, stop=True))
                for i in range(8):
                    if i % 4 == 0:
                        sq_ready(i // 4)
                    last = mm(ps[b1][:, i:i + 1], ysq[:, i * P:(i + 1) * P], mean_w[:, 0:1], start=True, stop=True,
                              skip_group_check=True)
                done(last)

            def spread_rstd(k, b0):
                pe.wait_ge(e_rstd, RSQRT_STEPS * (k + 1))
                for g in range(2):
                    for i in range(4):
                        last = mm(ps[b0 + g][:, i * P:(i + 1) * P], erstd[:, 4 * g + i:4 * g + i + 1].broadcast_to([P, P]),
                                  ident[:, :], start=True, stop=True, skip_group_check=True)
                    done(last)

            norm_sums(y, lambda g: dve_did(f"y{g}"), lambda g: act_did(f"sq{g}"), 6, 0)
            for g in range(2):
                done(mm(ps[4 + g][:, :], w_e[XK][0:DC, :], half(ctx_t, g)[0:DC, :], start=True, stop=True))
            for g in range(2):
                for k in range(4):
                    kk = 4 * g + k
                    last = mm(ps[6 + g][:, k * P:(k + 1) * P], ctx_t[0:DC, kk * P:(kk + 1) * P], w_e[XV][0:DC, :],
                              start=True, stop=True, skip_group_check=True)
                done(last)
            spread_rstd(0, 0)
            for g in range(2):
                dve_did("x1")
                done(mm(ps[2 + g][:, :], w_e[XQ], half(x_all, g), start=True, stop=True))
            for b in range(B):
                dve_did("xq1")
                for j in range(2):
                    i = 2 * b + j
                    last = mm(ps[b][:, j * N:(j + 1) * N], q_e[:, i * P:(i + 1) * P], k_e[:, b * N:(b + 1) * N],
                              start=True, stop=True, skip_group_check=True)
                done(last)
            dve_did("soft")
            for b in range(B):
                for kt in range(2):
                    for j in range(2):
                        last = nc.tensor.transpose(ps[4 + b][:, kt * N + j * P:kt * N + (j + 1) * P],
                                                   soft[:, 2 * b + j, kt * P:(kt + 1) * P], ident[:, :])
                done(last)
            for b in range(B):
                act_did(f"tr{b}")
                for kt in range(2):
                    i = 2 * b + kt
                    last = mm(ps[b][:, 0:N], v_e[:, i * P:(i + 1) * P], soft_t[:, b, kt * N:(kt + 1) * N],
                              start=(kt == 0), stop=(kt == 1))
                done(last)
            norm_sums(y, lambda g: dve_did(f"y{2 + g}"), lambda g: act_did(f"sq{2 + g}"), 4, 6)
            spread_rstd(1, 6)

        def entry_scalar(act):
            fn = nc.scalar.activation
            done = lambda ins: ins.then_inc(e_act, 1)
            pe_did = lambda name: act.wait_ge(e_pe, E_PE.index(name) + 1)
            dve_did = lambda name: act.wait_ge(e_dve, E_DVE.index(name) + 1)
            for i in range(4):
                dve_did(f"neg{i}")
                src = half((neg_q, neg_k)[i // 2], i % 2)
                done(fn(src, src, ACT.Exp))
            for g in range(2):
                pe_did(f"att{g}")
                done(nc.scalar.copy(half(att, g), ps[2 + g][:, :]))
            for g in range(2):
                dve_did(f"yc{g}")
                done(fn(half(ysq, g), half(yc, g), ACT.Square))
            for name in ("wqkv", "wo", "w1", "w2"):
                split_high(act, name, 0, lambda: None)
            for b in range(B):
                dve_did(f"max{b}")
                for j in range(2):
                    i = 2 * b + j
                    last = fn(soft[:, i, :], ps[b][:, j * N:(j + 1) * N], ACT.Exp, bias=emax[:, i:i + 1],
                              accum_out=esum[:, i:i + 1])
                done(last)
            for b in range(B):
                pe_did(f"tr{b}")
                done(nc.scalar.copy(soft_t[:, b, :], ps[4 + b][:, :]))
            for g in range(2):
                dve_did(f"yc{2 + g}")
                done(fn(half(ysq, g), half(yc, g), ACT.Square))

        def entry_vector(dve):
            tt, tsc = nc.vector.tensor_tensor, nc.vector.tensor_scalar
            done = lambda ins: ins.then_inc(e_dve, 1)
            pe_did = lambda name: dve.wait_ge(e_pe, E_PE.index(name) + 1)
            act_did = lambda name: dve.wait_ge(e_act, E_ACT.index(name) + 1)
            dve_did = lambda name: dve.wait_ge(e_dve, E_DVE.index(name) + 1)
            nc.vector.memset(xs_a[64:P, :, 0:1], 0.0)
            nc.vector.memset(xs_f[64:P, 0:1], 0.0)
            dve.wait_ge(e_first, E_FIRST)
            pos = (pos_q, pos_k)
            for i in range(4):
                pe_did(("q0", "q1", "k0", "k1")[i])
                done(tsc(half((neg_q, neg_k)[i // 2], i % 2), ps[i][:, :], ecols[:, i // 2:i // 2 + 1], 0.0, ALU.add, ALU.min))
            for i in range(4):
                done(tsc(half(pos[i // 2], i % 2), ps[i][:, :], ecols[:, i // 2:i // 2 + 1], 0.0, ALU.add, ALU.max))
            dve.wait_ge(e_load, E_LOADS)
            for g in range(2):
                pe_did(f"v{g}")
                done(tt(half(v_e, g).rearrange("p (k e) -> p k e", e=P), ps[4 + g][:, :].rearrange("p (k e) -> p k e", e=P),
                        vb1.unsqueeze(1).broadcast_to([P, 4, P]), ALU.add))
            for i in range(4):
                act_did(f"exp{i}")
                if i == 0:
                    dve_did("pos3")
                done(tt(half((q_e, k_e)[i // 2], i % 2), half(pos[i // 2], i % 2), half((neg_q, neg_k)[i // 2], i % 2), ALU.add))
            for g in range(2):
                pe_did(f"s{g}")
                done(tt(half(masked, g).rearrange("p (k e) -> p k e", e=P), ps[g][:, :].rearrange("p (k e) -> p k e", e=P),
                        w_e[SAME].unsqueeze(1).broadcast_to([P, 4, P]), ALU.mult))
            for g in range(2):
                pe_did(f"wo{g}")
                done(nc.vector.scalar_tensor_tensor(out=half(y, g), in0=ps[4 + g][:, :], scalar=ecols[:, 2:3],
                                                    in1=half(x_nb, g), op0=ALU.add, op1=ALU.add))

            def norm(k, b0, b1):
                for g in range(2):
                    pe_did(f"mean{k + g}")
                    if g == 0:
                        dve_did(f"y{k + 1}")
                    done(tt(half(yc, g), half(y, g), ps[b0 + g][:, :], ALU.subtract))
                pe_did(f"var{k}")
                done(tsc(evar[:, :], ps[b1][:, 0:8], EPS, None, ALU.add))
                dve_did(f"var{k}")
                start = RSQRT_STEPS * (k // 2)
                rsqrt(dve, (erstd[:, :], evar[:, :], (minus_half_evar[:, :], erstd_tmp[:, :]), e_rstd, lambda i: start + i + 1))

            norm(0, 6, 0)
            for g in range(2):
                pe_did(f"rstd{g}")
                done(tt(x_t[:, :, g * P:(g + 1) * P], half(yc, g).rearrange("p (n b) -> p b n", b=B),
                        ps[g][:, :].rearrange("p (n b) -> p b n", b=B), ALU.mult))
            for g in range(2):
                pe_did(f"xk{g}")
                done(tsc(half(k_e, g), ps[4 + g][:, :], ecols[:, 4:5], None, ALU.add))
            for g in range(2):
                pe_did(f"xv{g}")
                done(tt(half(v_e, g).rearrange("p (k e) -> p k e", e=P), ps[6 + g][:, :].rearrange("p (k e) -> p k e", e=P),
                        vb2.unsqueeze(1).broadcast_to([P, 4, P]), ALU.add))
            for g in range(2):
                pe_did(f"xq{g}")
                done(tsc(half(q_e, g), ps[2 + g][:, :], ecols[:, 3:4], None, ALU.add))
            for b in range(B):
                pe_did(f"sc{b}")
                done(nc.vector.tensor_reduce(emax[:, 2 * b:2 * b + 2], ps[b][:, :].rearrange("p (j k) -> p j k", j=2),
                                             AX.X, ALU.max, negate=True))
            act_did("soft3")
            done(nc.vector.reciprocal(erec[:, :], esum[:, :]))
            dve_did("rec")
            done(tt(soft, soft, erec[:, :].unsqueeze(2).broadcast_to([P, 8, N]), ALU.mult))
            for g in range(2):
                for j in range(2):
                    b = 2 * g + j
                    pe_did(f"xo{b}")
                    last = tt(y[:, b * N:(b + 1) * N], ps[b][:, 0:N], x_t[:, b, :], ALU.add)
                done(last)
            norm(2, 4, 6)
            views = []
            for g in range(2):
                bs = slice(2 * g, 2 * g + 2)
                c3 = half(yc, g).rearrange("p (b n) -> p b n", n=N)
                r3 = ps[6 + g][:, :].rearrange("p (b n) -> p b n", n=N)
                views.append((bs, c3, r3))
                pe_did(f"rstd{2 + g}")
                tt(xs_a[0:64, bs, :], c3[0:64], r3[0:64], ALU.mult)
                tt(xs_a[64:P, bs, 1:N], c3[64:P, :, 0:N - 1], r3[64:P, :, 0:N - 1], ALU.mult).then_inc(s_xsa, 2)
            for g, (bs, c3, r3) in enumerate(views):
                last = tt(x_t[:, bs, :], c3, r3, ALU.mult)
                if g == 1:
                    last.then_inc(s_x2, 1)
            for g in range(2):
                tt(half(x_in, g), half(yc, g), ps[6 + g][:, :], ALU.mult)

        def entry_gpsimd(pool):
            nc.gpsimd.memset(warm[:, :], 0.0).then_inc(s_zero, 1)
            nc.gpsimd.memset(gate[:, 2, :], 0.0).then_inc(s_zero, 1)
            nc.gpsimd.memset(value[:, 2, :], 0.0).then_inc(s_zero, 1)
            nc.gpsimd.memset(v[:, :, :, :].rearrange("p a t (h e) -> p (a t h) e", e=VW)[:, :, DH:VW], 1.0).then_inc(s_zero, 1)

        f_at = lambda names, g, name: len(names) * g + names.index(name) + 1

        def final_tensor(pe, g):
            mm = nc.tensor.matmul
            dve_did = lambda name: pe.wait_ge(f_dve, f_at(F_DVE, g, name))
            a, b = ps[2 * g], ps[2 * g + 1]
            dve_did("sum")
            mm(a[:, :], mean_w[:, :], half(y, g), start=True, stop=True).then_inc(f_pe, 1)
            pe.wait_ge(f_act, g + 1)
            for i in range(4):
                last = mm(b[:, i:i + 1], half(ysq, g)[:, i * P:(i + 1) * P], mean_w[:, 0:1], start=True, stop=True,
                          skip_group_check=True)
            last.then_inc(f_pe, 1)
            pe.wait_ge(f_rstd, RSQRT_STEPS * (g + 1))
            for i in range(4):
                last = mm(a[:, i * P:(i + 1) * P], erstd[:, 4 * g + i:4 * g + i + 1].broadcast_to([P, P]), ident[:, :],
                          start=True, stop=True, skip_group_check=True)
            last.then_inc(f_pe, 1)

        def final_scalar(act, g):
            act.wait_ge(f_dve, f_at(F_DVE, g, "yc"))
            nc.scalar.activation(half(ysq, g), half(yc, g), ACT.Square).then_inc(f_act, 1)

        def final_vector(dve, g):
            tt = nc.vector.tensor_tensor
            dve_did = lambda name: dve.wait_ge(f_dve, f_at(F_DVE, g, name))
            pe_did = lambda name: dve.wait_ge(f_pe, f_at(F_PE, g, name))
            dve.wait_ge(s_x2, 1 + DEPTH * B - 2 * (1 - g))
            a, b, cols4 = ps[2 * g], ps[2 * g + 1], slice(4 * g, 4 * g + 4)
            tt(half(y, g), half(x_all, g), half(x_in, g), ALU.add).then_inc(f_dve, 1)
            pe_did("mean")
            dve_did("sum")
            tt(half(yc, g), half(y, g), a[:, :], ALU.subtract).then_inc(f_dve, 1)
            pe_did("var")
            nc.vector.tensor_scalar(evar[:, cols4], b[:, 0:4], EPS, None, ALU.add).then_inc(f_dve, 1)
            dve_did("var")
            rsqrt(dve, (erstd[:, cols4], evar[:, cols4], (minus_half_evar[:, cols4], erstd_tmp[:, cols4]), f_rstd,
                        lambda i: RSQRT_STEPS * g + i + 1))
            pe_did("rstd")
            tt(half(y, g), half(yc, g), a[:, :], ALU.mult).then_inc(f_dve, 1)

        def final_store(eng):
            for g in range(2):
                eng.wait_ge(f_dve, f_at(F_DVE, g, "y"))
                eng.dma_start(out[:, g * CH:(g + 1) * CH], half(y, g)).then_inc(s_out, 16)
            eng.wait_ge(s_out, 32)

        block = ctx.enter_context(nc.Block())

        def iteration(s, turn, back_a, scores, back_b, shift, finish_a, head, back_slot, proj_slot, finish_slot, back_tail, tail,
                      do_back=True, do_finish=True, do_attend=True, do_proj=True):
            if do_attend:
                turn(plus(s, 1), 7)
            for part in range(2):
                for n in (2 * part, 2 * part + 1):
                    if do_back:
                        back_a(s, n)
                for n in (2 * part, 2 * part + 1):
                    if do_attend:
                        scores(plus(s, 1), n)
            for part in range(2):
                if do_back:
                    back_b(s, part)
                if do_attend and part == 0:
                    shift(plus(s, 1))
            if do_finish:
                finish_a(plus(s, -1))
            for slot in range(HEADS):
                if do_proj and slot < FIRST_TURN:
                    proj_slot(plus(s, 2), slot)
                if do_attend:
                    head(plus(s, 1), slot)
                if do_proj and slot >= FIRST_TURN:
                    proj_slot(plus(s, 2), slot)
                if do_finish:
                    finish_slot(plus(s, -1), slot)
                if do_back:
                    back_slot(s, slot)
                if do_proj and slot >= FIRST_TURN:
                    turn(plus(s, 2), slot - FIRST_TURN)
            if do_back:
                back_tail(s)
            if do_attend:
                tail(plus(s, 1))

        def run(fori, final, turn, back_a, scores, back_b, shift, finish_a, head, back_slot, proj_slot, finish_slot, back_tail, tail):
            stages = (turn, back_a, scores, back_b, shift, finish_a, head, back_slot, proj_slot, finish_slot, back_tail, tail)
            for slot in range(HEADS):
                proj_slot(0, slot)
                if slot >= FIRST_TURN:
                    turn(0, slot - FIRST_TURN)
            iteration(-1, *stages, do_back=False, do_finish=False)
            iteration(0, *stages, do_finish=False)
            with fori(0, DEPTH - 1) as layer:
                for b in range(1, B + 1):
                    iteration(plus((layer, 0), b), *stages)
            for i in range((DEPTH - 1) * B + 1, DEPTH * B):
                iteration(i, *stages, do_attend=i + 1 < DEPTH * B, do_proj=i + 2 < DEPTH * B)
            final(0)
            iteration(DEPTH * B, *stages, do_back=False, do_attend=False, do_proj=False)
            final(1)

        whole = {"wqkv": (wqkv[:, :], wqkv_s[:, 0, :], wqkv_s[:, 1, :], s_wqkv),
                 "wo": (wo[:, :, :].rearrange("p c n -> p (c n)"), wo_s[:, 0].rearrange("p c n -> p (c n)"),
                        wo_s[:, 1].rearrange("p c n -> p (c n)"), s_wo),
                 "w1": (w1[:, :], w1_s[:, 0, :], w1_s[:, 1, :], s_w1),
                 "w2": (w2[:, :, :].rearrange("p c n -> p (c n)"), w2_s[:, 0].rearrange("p c n -> p (c n)"),
                        w2_s[:, 1].rearrange("p c n -> p (c n)"), s_w2)}
        PIECE = 1024

        def pieces(name):
            return range(0, whole[name][0].shape[1], PIECE)

        def split_high(eng, name, layer, last_use):
            w, hi, _, loaded = whole[name]
            eng.wait_ge(loaded, layer * 16 + 16)
            last_use()
            for c in pieces(name):
                end = min(c + PIECE, w.shape[1])
                nc.scalar.copy(hi[:, c:end], w[:, c:end]).then_inc(s_wh[name], 1)

        def split_rest(eng, name, layer):
            w, hi, lo, _ = whole[name]
            n = len(pieces(name))
            for k, c in enumerate(pieces(name)):
                end = min(c + PIECE, w.shape[1])
                eng.wait_ge(s_wh[name], layer * n + (k + 1))
                nc.gpsimd.tensor_tensor(lo[:, c:end], w[:, c:end], hi[:, c:end], ALU.subtract).then_inc(s_ws[name], 1)

        def weight_ready(eng, name, layer):
            n = len(pieces(name))
            eng.wait_ge(s_ws[name], layer * n + n)

        def mm3(out_ap, w, x, start, stop):
            for k, (i, j) in enumerate(((0, 0), (0, 1), (1, 0))):
                last = nc.tensor.matmul(out_ap, w[i], x[j], start=start and k == 0, stop=stop and k == 2,
                                        skip_group_check=True)
            return last

        @block.sync
        def _(sp):
            def load(layer, what):
                if what == "wqkv":
                    sp.dma_start(wqkv[:, :], a["wqkv"][layer, :, :]).then_inc(s_wqkv, 16)
                elif what == "qks":
                    sp.dma_start(qk_scale[:, :], a["qk_scale"][layer, :, :].broadcast_to([P, 4 * DH])).then_inc(s_qks, 16)
                elif what == "wo":
                    sp.dma_start(wo[:, :, :], a["wo"][layer, :, :, :].rearrange("c p n -> p c n")).then_inc(s_wo, 16)
                elif what == "w1":
                    sp.dma_start(w1[:, :], a["w1"][layer, :, :]).then_inc(s_w1, 16)
                elif what == "w2":
                    sp.dma_start(w2[:, :, :], a["w2"][layer, :, :, :].rearrange("c p n -> p c n")).then_inc(s_w2, 16)
                elif what == "cols":
                    sp.dma_start(cols[:, :], a["cols"][layer, :, :]).then_inc(s_cols, 16)
                elif what == "b2":
                    sp.dma_start(b2[:, :], a["b2"][layer, :, :]).then_inc(s_b2, 16)

            entry_loads(sp)
            for what in ("wqkv", "qks", "wo", "w1", "w2", "cols", "b2"):
                load(0, what)
            with sp.Fori(0, DEPTH - 1) as layer:
                weight_ready(sp, "wqkv", layer)
                load(layer + 1, "wqkv")
                sp.wait_ge(s_rot, layer + 1)
                load(layer + 1, "qks")
                for what in ("wo", "w1", "w2"):
                    weight_ready(sp, what, layer)
                    load(layer + 1, what)
                sp.wait_ge(s_value, at(3, (layer, B - 1), 2))
                sp.wait_ge(s_gate, at(3, (layer, B - 1), 2))
                load(layer + 1, "cols")
                sp.wait_ge(s_x2, at(1, (layer, B - 1), 0) + 1)
                load(layer + 1, "b2")
            final_store(sp)

        @block.tensor
        def _(pe):
            mm = nc.tensor.matmul

            def front_bank_read(s, bank, use):
                if use == 0:
                    if not first(s):
                        pe.wait_ge(s_qkt, at(8, s, 6 + bank) - 8)
                elif use in (6, 8, 9):
                    pe.wait_ge(s_qkt, at(8, s, 2 * max(use - 7, 0) + bank))
                else:
                    before = bank + (10 if use == 7 else 2 * (use - 1))
                    if before < 8:
                        pe.wait_ge(s_sq, at(8, s, before))
                    else:
                        pe.wait_ge(s_v, at(4, s, before - 8))

            def proj_slot(s, slot):
                if slot >= 12:
                    return
                b = batch(s)
                t, c = chunk_of(slot)
                if slot == 0:
                    pe.wait_ge(s_xss, B if first(s) else at(1, s, 0))
                    if b == 0:
                        weight_ready(pe, "wqkv", layer_of(s))
                bank, use = slot % 2, chunk_use(slot)
                front_bank_read(s, bank, use)
                mm3(PF[bank][:, :], [xs_s[:, i, b, t * P:(t + 1) * P] for i in range(2)],
                    [wqkv_s[:, i, c * CH:(c + 1) * CH] for i in range(2)], True, True).then_inc(pf_full[bank], 1)

            def turn(s, n):
                t, c = divmod(n, 4)
                bank, use = n % 2, turn_use(n)
                pe.wait_ge(s_rope, at(8, s, n))
                front_bank_read(s, bank, use)
                for j in range(4):
                    last = nc.tensor.transpose(PF[bank][:, j * P:(j + 1) * P],
                                               rope[:, t, c * CH + j * P:c * CH + (j + 1) * P], ident[:, :])
                last.then_inc(pf_full[bank], 1)

            def scores(s, n):
                t, par = divmod(n, 2)
                qk_b = qk_b2[:, batch(s) % 2]
                if n == 0:
                    pe.wait_ge(s_qkb[0], at(3, s, 2))
                    pe.wait_ge(s_qkb[1], at(5, s, 4))
                if t == 1:
                    pe.wait_ge(s_negm, at(4, s, par))
                elif not first(s):
                    pe.wait_ge(s_probs, at(HEADS, s, 14 + par) - HEADS)
                mm(PA[par][:, :], identb[:, :], mask_q[:, t, :], start=True, stop=False, skip_group_check=True)
                r = 64 * par
                for hh in range(8):
                    for u in range(4):
                        w = 4 * t + u
                        lo = max(w - 1, 0) * WIN
                        n = (w + 1) * WIN - lo
                        last = mm(PA[par][32 * u:32 * u + 32, hh * 64 + 64 - n:hh * 64 + 64],
                                  qk_b[r:r + 64, 0, hh, w * WIN:(w + 1) * WIN],
                                  qk_b[r:r + 64, 1, hh, lo:lo + n], start=False, stop=(hh == 7 and u == 3),
                                  skip_group_check=True)
                last.then_inc(pa_full[par], 1)

            def shift(s):
                pe.wait_ge(s_negm, at(4, s, 3))
                for t in range(NT):
                    last = nc.tensor.transpose(negt_ps[0:HEADS, t * P:(t + 1) * P], negm[:, t, :], identb[:, :])
                last.then_inc(pa_full[0], 1)

            def head(s, h):
                par, hh = h % 2, h // 2
                r = 64 * par
                qk_t = qk_t2[:, batch(s) % 2]
                bank = PA[par]
                if h == 0:
                    pe.wait_ge(s_qkt, at(8, s, 7))
                if h < 2:
                    pe.wait_ge(s_negt, at(1, s, 0))
                else:
                    pe.wait_ge(s_probs, at(HEADS, s, h - 2))
                mm(bank[:, 0:STW], pick[:, h, :], shift_k[:, :], start=True, stop=False, skip_group_check=True)
                mm(bank[:, 0:SPAN], qk_t[r:r + 64, 1, hh, 0:P], qk_t[r:r + 64, 0, hh, 0:SPAN],
                   start=False, stop=False, skip_group_check=True)
                mm(bank[:, SPAN:STW], qk_t[r:r + 64, 1, hh, P:N], qk_t[r:r + 64, 0, hh, P:N],
                   start=False, stop=True, skip_group_check=True).then_inc(pa_full[par], 1)
                if h > 0:
                    weigh(s, h - 1)

            def weigh(s, h):
                g = [i for i, (lo, hi) in enumerate(GROUPS) if lo <= h < hi][0]
                lo, hi = GROUPS[g]
                if h == lo and not (first(s) and g < 2):
                    pe.wait_ge(s_o, at(NG, s, g) - 2)
                if h == 0:
                    pe.wait_ge(s_v, at(4, s, 3))
                pe.wait_ge(s_probs, at(HEADS, s, h))
                vb = v[:, batch(s) % 2, :, h * VW:(h + 1) * VW]
                pr = probs[:, h % 4, :]
                bank = PO[g % 2]
                c0, c1 = (h - lo) * VW, (hi - lo + h - lo) * VW
                mm(bank[:, c0:c0 + VW], pr[:, 0:P], vb[:, 0, :], start=True, stop=True, skip_group_check=True)
                mm(bank[:, c1:c1 + VW], pr[:, SPAN:STW], vb[:, 1, :], start=True, stop=False, skip_group_check=True)
                mm(bank[0:WIN, c1:c1 + VW], pr[:, P:SPAN], vb[:, 0, :], start=False, stop=True,
                   skip_group_check=True).then_inc(s_av, 1)

            def tail(s):
                weigh(s, HEADS - 1)

            def back_a(s, n):
                if n == 0:
                    pe.wait_ge(s_o, at(NG, s, 2))
                elif n == 2:
                    pe.wait_ge(s_o, at(NG, s, NG - 1))
                half, t = divmod(n, 2)
                bank = OT[n][0]
                if n >= 2:
                    pe.wait_ge(s_ot, at(4, s, n - 2))
                elif first(s):
                    pe.wait_ge(s_x2, 1)
                else:
                    pe.wait_ge(s_value, at(3, plus(s, -1), (0, 2)[n]))
                    if n == 0:
                        pe.wait_ge(s_gate, at(3, plus(s, -1), 2))
                for j in range(4):
                    c = half * 4 + j
                    last = nc.tensor.transpose(PB[bank][:, j * P:(j + 1) * P], o[:, t, c * P:(c + 1) * P], ident[:, :])
                last.then_inc(pb_full[bank], 1)

            def back_b(s, part):
                if part == 0:
                    pe.wait_ge(s_ot, at(4, s, 3))
                    if batch(s) == 0:
                        weight_ready(pe, "wo", layer_of(s))
                for c in range(4 * part, 4 * part + 4):
                    last = mm3(PB[0][:, 0:N], [wo_s[:, i, c, :] for i in range(2)], [o_t[:, i, c, :] for i in range(2)],
                               c == 0, c == 7)
                if part == 1:
                    last.then_inc(pb_full[0], 1)

            def expand(bank, col, c, gate_part):
                m, w0 = FCH[c], gate_part * FF + c * P
                return mm3(PB[bank][0:m, col:col + N], [w1_s[:, i, w0:w0 + m] for i in range(2)],
                           [xg_s[:, i, :] for i in range(2)], True, True)

            def back_slot(s, slot):
                if slot == 1:
                    pe.wait_ge(s_x1, at(1, s, 0))
                    mm(PB[1][:, 0:N], mean_w[:, :], xs_f[:, :], start=True, stop=True).then_inc(pb_full[1], 1)
                elif slot == 4:
                    pe.wait_ge(s_xsq, at(1, s, 0))
                    pe.wait_ge(s_xt, at(1, s, 0))
                    for t in range(NT):
                        last = mm(PB[0][:, t:t + 1], xsq[:, t * P:(t + 1) * P], mean_w[:, 0:1], start=True, stop=True,
                                  skip_group_check=True)
                    last.then_inc(pb_full[0], 1)
                elif slot == 9:
                    pe.wait_ge(s_rstd, at(RSQRT_STEPS, s, RSQRT_STEPS - 1))
                    for t in range(NT):
                        last = mm(PB[1][:, t * P:(t + 1) * P], rstd[:, t:t + 1].broadcast_to([P, P]), ident[:, :],
                                  start=True, stop=True, skip_group_check=True)
                    last.then_inc(pb_full[1], 1)
                elif slot == 13:
                    pe.wait_ge(s_xgs, at(2, s, 1))
                    if batch(s) == 0:
                        weight_ready(pe, "w1", layer_of(s))
                    expand(1, 0, 0, 1)
                    expand(1, N, 1, 1).then_inc(pb_full[1], 1)
                elif slot == 14:
                    if not first(s):
                        pe.wait_ge(s_x2, at(1, s, 0))
                    expand(0, 0, 2, 1)
                    expand(0, N, 2, 0).then_inc(pb_full[0], 1)
                elif slot == 15:
                    pe.wait_ge(s_gate, at(3, s, 1))
                    expand(1, 0, 0, 0)
                    expand(1, N, 1, 0).then_inc(pb_full[1], 1)

            def finish_slot(s, slot):
                if slot == 8:
                    pe.wait_ge(s_hids, at(1, s, 0))
                    if batch(s) == 0:
                        weight_ready(pe, "w2", layer_of(s))
                    if last_step(s):
                        pe.wait_ge(s_value, at(3, s, 0))
                        pe.wait_ge(s_gate, at(3, s, 2))
                    else:
                        pe.wait_ge(s_var, at(1, plus(s, 1), 0))
                    for c in range(3):
                        m = FCH[c]
                        last = mm3(PB[0][:, 0:N], [w2_s[0:m, i, c, :] for i in range(2)],
                                   [hid_s[0:m, i, c, :] for i in range(2)], c == 0, c == 2)
                    last.then_inc(s_ffo, 1)

            nothing = lambda *_: None
            entry_tensor(pe)
            pe.wait_ge(s_const, C_LOADS)
            pe.wait_ge(s_zero, 4)
            run(pe.Fori, lambda g: final_tensor(pe, g), turn, back_a, scores, back_b, shift, nothing, head, back_slot, proj_slot, finish_slot, nothing, tail)

        @block.scalar
        def _(act):
            fn = nc.scalar.activation

            def proj_slot(s, slot):
                if slot == 12 and batch(s) == B - 1 and has_next(s):
                    split_high(act, "wqkv", layer_of(s) + 1, lambda: act.wait_ge(pf_full[1], at(F_USES, s, 6)))
                if slot >= 12:
                    return
                t, c = chunk_of(slot)
                bank, use = slot % 2, chunk_use(slot)
                act.wait_ge(pf_full[bank], at(F_USES, s, use))
                if c < 4:
                    n = t * 4 + c
                    if not (first(s) and n < 4):
                        act.wait_ge(s_rmul, at(8, s, n) - 4)
                    nc.scalar.copy(raw[:, c * CH:(c + 1) * CH], PF[bank][:, :]).then_inc(s_raw, 1)
                    if not (first(s) and n < 2):
                        act.wait_ge(s_ssq, at(8, s, n) - 2)
                    fn(sq[:, n % 2, :], PF[bank][:, :], ACT.Square).then_inc(s_sq, 1)
                else:
                    h0 = (c - 4) * HC
                    dst = v[:, batch(s) % 2, t, h0 * VW:(h0 + HC) * VW].rearrange("p (h e) -> p h e", e=VW)[:, :, 0:DH]
                    nc.scalar.copy(dst, PF[bank][:, :].rearrange("p (h e) -> p h e", e=DH)).then_inc(s_v, 1)

            def turn(s, n):
                t, c = divmod(n, 4)
                par = n % 2
                qk_t, qk_b = qk_t2[:, batch(s) % 2], qk_b2[:, batch(s) % 2]
                act.wait_ge(pf_full[par], at(F_USES, s, turn_use(n)))
                src = PF[par][:, :].rearrange("p (j t) -> p j t", j=4)
                j0 = (c % 2) * 4
                if n >= 5:
                    nc.scalar.copy(qk_b[:, c // 2, j0:j0 + 4, t * P:(t + 1) * P], src).then_inc(s_qkb[0], 1)
                nc.scalar.copy(qk_t[:, c // 2, j0:j0 + 4, t * P:(t + 1) * P], src).then_inc(s_qkt, 1)

            def back_a(s, n):
                half, t = divmod(n, 2)
                bank, use = OT[n]
                act.wait_ge(pb_full[bank], at(B_USES[bank], s, use))
                nc.scalar.copy(o_t[:, 0, half * 4:half * 4 + 4, t * P:(t + 1) * P],
                               PB[bank][:, :].rearrange("p (j t) -> p j t", j=4)).then_inc(s_oth, 1)

            def head(s, h):
                par, hh = h % 2, h // 2
                use = (3 if par == 0 else 2) + hh
                act.wait_ge(pa_full[par], at(A_USES[par], s, use))
                if not (first(s) and h < 4):
                    act.wait_ge(s_av, at(HEADS, s, h) - 4)
                fn(probs[:, h % 4, :], PA[par][:, 0:STW], ACT.Exp).then_inc(s_probs, 1)

            def back_slot(s, slot):
                if slot == 3:
                    act.wait_ge(s_xc, at(1, s, 0))
                    fn(xsq[:, :], xc[:, :], ACT.Square).then_inc(s_xsq, 1)
                elif slot in (14, 15):
                    if batch(s) == 0 and slot == 14:
                        act.wait_ge(s_cols, layer_of(s) * 16 + 16)
                    if slot == 14 and not first(s):
                        act.wait_ge(s_hids, at(1, plus(s, -1), 0))
                    (bank, use), chunks = (G01, (0, 1)) if slot == 14 else (C2, (2,))
                    act.wait_ge(pb_full[bank], at(B_USES[bank], s, use))
                    for c in chunks:
                        m, col = FCH[c], c % 2 * N
                        fn(gate[0:m, c, :], PB[bank][0:m, col:col + N], ACT.Identity, bias=cols[0:m, 5 + c:6 + c]).then_inc(s_gate, 1)
                if slot == 15 and batch(s) == B - 1 and has_next(s):
                    for name, (bank, use) in (("wo", WO_), ("w1", A01)):
                        split_high(act, name, layer_of(s) + 1,
                                   lambda: act.wait_ge(pb_full[bank], at(B_USES[bank], s, use)))

            def finish_a(s):
                act.wait_ge(s_gate, at(3, s, 2))
                flat = gate[:, :, :].rearrange("p c n -> p (c n)")
                fn(flat, flat, ACT.Gelu).then_inc(s_gelu, 1)
                if not last_step(s):
                    fn(warm[:, :], warm[:, :], ACT.Exp, scale=0.0)
                act.wait_ge(s_hid, at(1, s, 0))
                if not first(s):
                    act.wait_ge(s_ffo, at(1, s, 0) - 1)
                nc.scalar.copy(hid_s[:, 0].rearrange("p c n -> p (c n)"),
                               gate[:, :, :].rearrange("p c n -> p (c n)")).then_inc(s_hidh, 1)

            def finish_slot(s, slot):
                if slot == 13:
                    b = batch(s)
                    if not last_layer(s):
                        act.wait_ge(s_xsa, at(1, plus(s, B), 0))
                        nc.scalar.copy(xs_s[:, 0, b, :], xs_a[:, b, :]).then_inc(s_xsh, 1)
                    if b == B - 1 and has_next(s):
                        split_high(act, "w2", layer_of(s) + 1, lambda: act.wait_ge(s_ffo, at(1, s, 0)))

            nothing = lambda *_: None
            entry_scalar(act)
            for b in range(B):
                act.wait_ge(s_xsa, 2 * (b // 2) + 2)
                nc.scalar.copy(xs_s[:, 0, b, :], xs_a[:, b, :]).then_inc(s_xsh, 1)
            run(act.Fori, lambda g: final_scalar(act, g), turn, back_a, nothing, nothing, nothing, finish_a, head, back_slot, proj_slot, finish_slot, nothing, nothing)

        @block.vector
        def _(dve):
            tt, tsc = nc.vector.tensor_tensor, nc.vector.tensor_scalar

            def combine(s, n):
                t, c = divmod(n, 4)
                ch = rope[:, t, c * CH:(c + 1) * CH]
                dve.wait_ge(s_rmul, at(8, s, n))
                tt(ch, ch, rope_b[:, c * CH:(c + 1) * CH], ALU.add).then_inc(s_radd, 1)

            def normalise(s, n):
                t, c = divmod(n, 4)
                if n == 0:
                    dve.wait_ge(s_rn, at(RSQRT_STEPS, s, RSQRT_STEPS - 1))
                dve.wait_ge(s_radd, at(8, s, n))
                ch3 = rope[:, t, c * CH:(c + 1) * CH].rearrange("p (h e) -> p h e", e=DH)
                tt(ch3, ch3, rnorm[:, t, c * HC:(c + 1) * HC].unsqueeze(2).broadcast_to([P, HC, DH]),
                   ALU.mult).then_inc(s_rope, 1)

            def proj_slot(s, slot):
                if slot == 0 and batch(s) == 0:
                    dve.wait_ge(s_qks, layer_of(s) * 16 + 16)
                    if not first(s):
                        dve.wait_ge(s_rmul, at(8, s, 0) - 1)
                    tt(rot[:, :, :], rot_base[:, :, :], qk_scale[:, :].unsqueeze(1).broadcast_to([P, NT, 4 * DH]),
                       ALU.mult).then_inc(s_rot, 1)
                if slot < 8:
                    n = slot
                    t, c = divmod(n, 4)
                    dve.wait_ge(s_sq, at(8, s, n))
                    nc.vector.tensor_reduce(ssq[:, t, c * HC:(c + 1) * HC], sq[:, n % 2, :].rearrange("p (h e) -> p h e", e=DH),
                                            AX.X, ALU.add).then_inc(s_ssq, 1)
                if slot >= 8:
                    normalise(s, slot - 8)
                if slot in ROPE_SLOTS:
                    combine(s, ROPE_SLOTS.index(slot))
                if slot == 7 and type(s) is not tuple and s < 2:
                    rsqrt(dve, norms(s))

            def norms(s):
                dve.wait_ge(s_ssq, at(8, s, 7))
                tsc(ssq_c[:, :, :], ssq[:, :, :], 1e-24, None, ALU.max).then_inc(s_clamp, 1)
                dve.wait_ge(s_clamp, at(1, s, 0))
                if not first(s):
                    dve.wait_ge(s_rope, at(8, s, 7) - 8)
                return (rnorm[:, :, :], ssq_c[:, :, :], (minus_half_ssq[:, :, :], rn_tmp[:, :, :]), s_rn,
                        lambda i: at(RSQRT_STEPS, s, i))

            def turn(s, n):
                if n in (0, 6, 7):
                    return
                t, c = divmod(n - 1, 4)
                place = (slice(None), c // 2, slice((c % 2) * 4, (c % 2) * 4 + 4), slice(t * P, (t + 1) * P))
                dve.wait_ge(s_qkt, at(8, s, n - 1))
                nc.vector.tensor_copy(qk_b2[:, batch(s) % 2][place], qk_t2[:, batch(s) % 2][place]).then_inc(s_qkb[1], 1)

            def back_a(s, n):
                half, t = divmod(n, 2)
                bank = OT[n][0]
                out_cols = slice(half * 4, half * 4 + 4), slice(t * P, (t + 1) * P)
                dve.wait_ge(s_oth, at(4, s, n))
                tt(o_t[:, 1, out_cols[0], out_cols[1]], PB[bank][:, :].rearrange("p (j t) -> p j t", j=4),
                   o_t[:, 0, out_cols[0], out_cols[1]], ALU.subtract).then_inc(s_ot, 1)

            def scores(s, n):
                t, par = divmod(n, 2)
                dve.wait_ge(pa_full[par], at(A_USES[par], s, t))
                nc.vector.tensor_reduce(negm[:, t, :].rearrange("p (h two) -> p two h", two=2)[:, par, :],
                                        PA[par][:, :].rearrange("p (h k) -> p h k", h=8), AX.X, ALU.max,
                                        negate=True).then_inc(s_negm, 1)

            def shift(s):
                dve.wait_ge(pa_full[0], at(A_USES[0], s, 2))
                nc.vector.tensor_copy(shift_k[0:HEADS, 0:SPAN], negt_ps[0:HEADS, 0:SPAN])
                nc.vector.tensor_copy(shift_k[0:HEADS, SPAN:STW], negt_ps[0:HEADS, P:N]).then_inc(s_negt, 1)

            def evacuate(s, g):
                lo, hi = GROUPS[g]
                n = hi - lo
                dve.wait_ge(s_av, at(HEADS, s, hi - 1))
                src = PO[g % 2][:, 0:NT * n * VW].rearrange("p (t h e) -> p t h e", t=NT, e=VW)
                nc.vector.reciprocal(rsum[:, :, lo:hi], src[:, :, :, DH]).then_inc(s_rsum, 1)
                dve.wait_ge(s_rsum, at(NG, s, g))
                tt(o[:, :, lo * DH:hi * DH].rearrange("p t (h e) -> p t h e", e=DH), src[:, :, :, 0:DH],
                   rsum[:, :, lo:hi].unsqueeze(3).broadcast_to([P, NT, n, DH]), ALU.mult).then_inc(s_o, 1)

            def head(s, h):
                for g, (lo, hi) in enumerate(GROUPS[:-1]):
                    if h == (hi if g < 2 else hi + 1):
                        evacuate(s, g)

            def tail(s):
                evacuate(s, NG - 1)

            def shifted(dst, bank, b, op):
                op(dst[0:64, :], bank[0:64, 0:N], x_t[0:64, b, :])
                return op(dst[64:P, 1:N], bank[64:P, 0:N - 1], x_t[64:P, b, 0:N - 1])

            def back_b(s, part):
                if part == 0:
                    return
                b = batch(s)
                dve.wait_ge(pb_full[0], at(B_USES[0], s, WO_[1]))
                shifted(xs_f, PB[0], b, lambda d, p, x: tt(d, p, x, ALU.add)).then_inc(s_x1, 1)

            def back_slot(s, slot):
                b = batch(s)
                if slot == 0:
                    dve.wait_ge(s_x1, at(1, s, 0))
                    tt(x_t[:, b, :], PB[0][:, 0:N], x_t[:, b, :], ALU.add).then_inc(s_xt, 1)
                if slot == 2:
                    dve.wait_ge(pb_full[1], at(B_USES[1], s, MEAN[1]))
                    tt(xc[:, :], xs_f[:, :], PB[1][:, 0:N], ALU.subtract).then_inc(s_xc, 1)
                elif slot == 5:
                    dve.wait_ge(pb_full[0], at(B_USES[0], s, VAR[1]))
                    tsc(var[:, :], PB[0][:, 0:NT], EPS, None, ALU.add).then_inc(s_var, 1)
                elif slot == 7:
                    dve.wait_ge(s_var, at(1, s, 0))
                    if not first(s):
                        dve.wait_ge(pb_full[1], at(B_USES[1], s, RSTD[1]) - B_USES[1])
                    jobs = [(rstd[:, :], var[:, :], (minus_half_var[:, :], rstd_tmp[:, :]), s_rstd,
                             lambda i: at(RSQRT_STEPS, s, i))]
                    if type(s) is tuple or s + 2 < DEPTH * B:
                        jobs.append(norms(plus(s, 2)))
                    rsqrt(dve, *jobs)
                elif slot == 10:
                    dve.wait_ge(pb_full[1], at(B_USES[1], s, RSTD[1]))
                    tt(xc[:, :], xc[:, :], PB[1][:, 0:N], ALU.mult).then_inc(s_xn, 1)
                    dve.wait_ge(s_xn, at(1, s, 0))
                    if b == 0:
                        dve.wait_ge(s_cols, layer_of(s) * 16 + 16)
                    tsc(xc[:, :], xc[:, :], cols[:, 0:1], cols[:, 1:2], ALU.mult, ALU.add).then_inc(s_xg, 1)
                    dve.wait_ge(s_xg, at(1, s, 0))
                    nc.vector.tensor_copy(xg_s[:, 0, :], xc[:, :]).then_inc(s_xgs, 1)
                    dve.wait_ge(s_xgs, at(2, s, 0))
                    tt(xg_s[:, 1, :], xc[:, :], xg_s[:, 0, :], ALU.subtract).then_inc(s_xgs, 1)
                elif slot == 15:
                    values(s, C2, (2,))

            def back_tail(s):
                values(s, A01, (0, 1))

            def values(s, where, chunks):
                bank, use = where
                dve.wait_ge(pb_full[bank], at(B_USES[bank], s, use))
                if where == C2:
                    dve.wait_ge(s_gate, at(3, s, 2))
                    if not first(s):
                        dve.wait_ge(s_hid, at(1, plus(s, -1), 0))
                for c in chunks:
                    m, col = FCH[c], N if c else 0
                    tsc(value[0:m, c, :], PB[bank][0:m, col:col + N], cols[0:m, 2 + c:3 + c], None, ALU.add).then_inc(s_value, 1)

            def finish_slot(s, slot):
                if slot == 12:
                    b = batch(s)
                    dve.wait_ge(s_ffo, at(1, s, 0))
                    if b == 0:
                        dve.wait_ge(s_b2, layer_of(s) * 16 + 16)
                    add = lambda d, p, x, bias: nc.vector.scalar_tensor_tensor(out=d, in0=p, scalar=bias, in1=x,
                                                                              op0=ALU.add, op1=ALU.add)
                    if not last_layer(s):
                        add(xs_a[0:64, b, :], PB[0][0:64, 0:N], x_t[0:64, b, :], b2[0:64, :])
                        add(xs_a[64:P, b, 1:N], PB[0][64:P, 0:N - 1], x_t[64:P, b, 0:N - 1], b2[64:P, :]).then_inc(s_xsa, 1)
                        dve.wait_ge(s_xsa, at(1, plus(s, B), 0))
                    add(x_t[:, b, :], PB[0][:, 0:N], x_t[:, b, :], b2[:, :]).then_inc(s_x2, 1)

            nothing = lambda *_: None
            entry_vector(dve)
            dve.wait_ge(s_const, C_LOADS)
            run(dve.Fori, lambda g: final_vector(dve, g), turn, back_a, scores, back_b, shift, nothing, head, back_slot, proj_slot, finish_slot, back_tail, tail)

        @block.gpsimd
        def _(pool):
            tt = nc.gpsimd.tensor_tensor

            def products(s, t, c):
                n = t * 4 + c
                kind = c // 2
                if n == 0 and batch(s) == 0:
                    pool.wait_ge(s_rot, layer_of(s) + 1)
                pool.wait_ge(s_raw, at(8, s, n))
                if not first(s):
                    pool.wait_ge(pf_full[n % 2], at(F_USES, s, turn_use(n)) - F_USES)
                ch = slice(c * CH, (c + 1) * CH)
                if not (first(s) and n < 4):
                    pool.wait_ge(s_radd, at(8, s, n) - 4)
                x3 = raw[:, ch].rearrange("p (h e) -> p h e", e=DH)
                a3 = rope[:, t, ch].rearrange("p (h e) -> p h e", e=DH)
                b3 = rope_b[:, ch].rearrange("p (h e) -> p h e", e=DH)
                ta = rot[:, t, kind * 2 * DH:kind * 2 * DH + DH].unsqueeze(1)
                tb = rot[:, t, kind * 2 * DH + DH:(kind + 1) * 2 * DH].unsqueeze(1)
                hf = DH // 2
                tt(a3, x3, ta.broadcast_to([P, HC, DH]), ALU.mult)
                tt(b3[:, :, 0:hf], x3[:, :, hf:DH], tb[:, :, 0:hf].broadcast_to([P, HC, hf]), ALU.mult)
                tt(b3[:, :, hf:DH], x3[:, :, 0:hf], tb[:, :, hf:DH].broadcast_to([P, HC, hf]), ALU.mult).then_inc(s_rmul, 1)

            def proj_slot(s, slot):
                if 1 <= slot < 9:
                    products(s, *divmod(slot - 1, 4))
                if slot == 13 and batch(s) == B - 1 and has_next(s):
                    split_rest(pool, "wqkv", layer_of(s) + 1)

            def back_slot(s, slot):
                if slot == 15 and batch(s) == B - 1 and has_next(s):
                    for name in ("wo", "w1"):
                        split_rest(pool, name, layer_of(s) + 1)

            def finish_a(s):
                pool.wait_ge(s_gelu, at(1, s, 0))
                pool.wait_ge(s_value, at(3, s, 2))
                tt(gate[:, :, :], gate[:, :, :], value[:, :, :], ALU.mult).then_inc(s_hid, 1)
                pool.wait_ge(s_hidh, at(1, s, 0))
                tt(hid_s[:, 1], gate[:, :, :], hid_s[:, 0], ALU.subtract).then_inc(s_hids, 1)

            def finish_slot(s, slot):
                if slot == 13:
                    b = batch(s)
                    if not last_layer(s):
                        pool.wait_ge(s_xsh, at(1, plus(s, B), 0))
                        tt(xs_s[:, 1, b, :], xs_a[:, b, :], xs_s[:, 0, b, :], ALU.subtract).then_inc(s_xss, 1)
                    if b == B - 1 and has_next(s):
                        split_rest(pool, "w2", layer_of(s) + 1)

            nothing = lambda *_: None
            entry_gpsimd(pool)
            for name in ("wqkv", "wo", "w1", "w2"):
                split_rest(pool, name, 0)
            for b in range(B):
                pool.wait_ge(s_xsh, b + 1)
                tt(xs_s[:, 1, b, :], xs_a[:, b, :], xs_s[:, 0, b, :], ALU.subtract).then_inc(s_xss, 1)
            run(pool.Fori, nothing, nothing, nothing, nothing, nothing, nothing, finish_a, nothing, back_slot, proj_slot,
                finish_slot, nothing, nothing)


def tables():
    half = np.arange(0, DH, 2, dtype=np.float32)
    inv_freq = np.float32(1.0) / np.float32(10000.0) ** (half / np.float32(DH))
    t = np.arange(N, dtype=np.float32)
    freqs = (t[:, None] * inv_freq[None, :]).astype(np.float32)
    base = ((half + np.float32(0.4 * DH)) / np.float32(1.4 * DH)).astype(np.float32)
    power = ((t - N // 2) / (WIN // 2)).astype(np.float32)
    scale = (base[None, :].astype(np.float64) ** power[:, None].astype(np.float64))
    cos, sin = np.cos(freqs.astype(np.float64)), np.sin(freqs.astype(np.float64))
    two = lambda lo, hi: np.concatenate([lo, hi], -1)
    rows = np.stack([two(cos * scale, cos * scale) * 8.0, two(-sin * scale, sin * scale) * 8.0,
                     two(cos / scale, cos / scale), two(-sin / scale, sin / scale)], 1)
    rot_base = rows.reshape(NT, P, 4 * DH).transpose(1, 0, 2).astype(np.float32)
    bf = mybir.dt.np(BF16)
    i, rel = np.arange(WIN)[:, None], np.arange(2 * WIN)[None, :] - WIN
    win = np.where((i < rel) | (i > rel + WIN), BIG, 0.0)
    later = np.tile(win, (4, 1))
    start = later.copy()
    start[0:WIN, 0:WIN] = BIG
    mask_q = np.stack([np.tile(start, (1, 8)), np.tile(later, (1, 8))], 1).astype(bf)
    j, q = np.arange(P), np.arange(SPAN)
    left, right = np.zeros((P, P)), np.zeros((P, SPAN))
    for par in range(2):
        for r in range(WIN):
            own = j // WIN % 2 == par
            left[32 + par * WIN + r] = np.where(own, j % WIN > r, j % WIN < r)
            right[32 + par * WIN + r] = (q // WIN % 2 == par) & (q % WIN == r)
    for w in range(P // WIN):
        left[96 + w] = j // WIN == w
        right[96 + w] = (q // WIN != w) & (q // WIN != w + 1)
    shift_k = (np.concatenate([right, right[:, 0:P]], 1) * BIG).astype(bf)
    pick = np.repeat(left[:, None, :], HEADS, 1).astype(bf)
    for h in range(HEADS):
        pick[h, h, :] = 1
    pos = np.arange(P) // B
    return {
        "rot_base": rot_base, "mask_q": mask_q, "shift_k": shift_k, "pick": pick,
        "ident": np.eye(P, dtype=np.float32), "identb": np.eye(P).astype(bf),
        "mean_w": np.full((P, P), 1.0 / P, np.float32),
        "same": (pos[:, None] == pos[None, :]).astype(np.float32),
    }


def kernel(**inputs):
    import concourse.bacc as bacc
    from concourse.bass_utils import run_bass_kernel_spmd

    f = {n: np.asarray(x) for n, x in inputs.items()}
    row = lambda x: np.ascontiguousarray(x.reshape(1, -1))
    A, X, L = "L0_attn_", "L0_xattn_", "L0_ffn_"
    hf = DH // 2
    swap = lambda x: np.concatenate([x[:, hf:], x[:, :hf]], 1)
    qs, ks = f[L + "q_scale"], f[L + "k_scale"]
    wqkv = f[L + "Wqkv"]
    w2 = np.zeros((DEPTH, 3, P, D), np.float32)
    w2.reshape(DEPTH, 3 * P, D)[:, :FF] = f[L + "W2"]
    b1 = np.zeros((DEPTH, 2, 3 * P), np.float32)
    b1[:, :, :FF] = f[L + "b1"].reshape(DEPTH, 2, FF)
    cols = np.concatenate([f[L + "ln_g"][:, None], f[L + "ln_b"][:, None], b1.reshape(DEPTH, 6, P)], 1)
    arrays = {
        "x_nb": f["x"].transpose(2, 1, 0).reshape(D, T), "ctx_t": f["ctx_768"].reshape(T, DC).T,
        "wq": f[A + "Wq"].T, "wk": f[A + "Wk"].T, "wv": f[A + "Wv"].T, "wot": f[A + "Wo"].T,
        "xwq": f[X + "Wq"], "xwk": f[X + "Wk"], "xwv": f[X + "Wv"],
        "bv": row(f[A + "bv"]), "xbv": row(f[X + "bv"]),
        "ecols": np.stack([f[A + "bq"], f[A + "bk"], f[A + "bo"], f[X + "bq"], f[X + "bk"]], 1),
        "wqkv": wqkv, "wo": f[L + "Wo"].reshape(DEPTH, 8, P, D), "w1": f[L + "W1"], "w2": w2,
        "cols": cols.transpose(0, 2, 1), "b2": f[L + "b2"][:, :, None],
        "qk_scale": np.stack([qs, swap(qs), ks, swap(ks)], 1).reshape(DEPTH, 1, 4 * DH),
        **tables(),
    }
    nc = bacc.Bacc("TRN2", target_bir_lowering=False, num_devices=1)
    data, aps = {}, {}
    for name, x in arrays.items():
        x = np.ascontiguousarray(x)
        data[f"in_{name}"] = x
        aps[name] = nc.dram_tensor(f"in_{name}", x.shape, mybir.dt.from_np(x.dtype), kind="ExternalInput").ap()
    out = nc.dram_tensor("out_t", (D, T), F32, kind="ExternalOutput").ap()
    build(nc, aps, out)
    r = run_bass_kernel_spmd(nc, [data], core_ids=[0])
    return np.ascontiguousarray(r.results[0]["out_t"].T).reshape(B, N, D)
```
